# Optimizing a Trainium2 kernel written in Bass

```python
import numpy as np
import jax
import jax.numpy as jnp

def _softmax(x, axis=-1):
    return jax.nn.softmax(x, axis=axis)

def _gelu(x):
    return jax.nn.gelu(x, approximate=True)

def _silu(x):
    return jax.nn.silu(x)

def _sigmoid(x):
    return jax.nn.sigmoid(x)

def _layernorm(x, axis=-1, eps=1e-05):
    m = jnp.mean(x, axis=axis, keepdims=True)
    v = jnp.var(x, axis=axis, keepdims=True)
    return (x - m) / jnp.sqrt(v + eps)

def _scatter_add(tgt, idx, src, axis=0):
    return tgt.at[idx].add(src)

def _segment_sum(src, seg, n):
    return jax.ops.segment_sum(src, seg, n)
kernel_name = 'mk_recurrent_d2_jaxref_r8_b59422'

def setup_inputs(seed: int=0):
    np.random.seed(seed)
    _w = jnp.asarray

    def _L0_attn_setup():
        import jax, jax.numpy as jnp
        import numpy as np
        EPS = 1e-05
        NUM_HEADS = 16
        FEATURE_DIM = 16
        CHUNK = 64

        def _phi(x):
            f = x.shape[-1]
            return (x[..., :, None] * x[..., None, :]).reshape(*x.shape[:-1], f * f)
        key = jax.random.key(seed)
        ks = jax.random.split(key, 5)
        b, l, d = (4, 256, 128)
        h, f = (NUM_HEADS, FEATURE_DIM)
        hd = d // h
        scale = 0.02
        return {'hidden_states': jax.random.normal(ks[0], (b, l, d), jnp.float32), 'Wq': jax.random.normal(ks[1], (d, h * f), jnp.float32) * scale, 'Wk': jax.random.normal(ks[2], (d, h * f), jnp.float32) * scale, 'Wv': jax.random.normal(ks[3], (d, h * hd), jnp.float32) * scale, 'Wo': jax.random.normal(ks[4], (h * hd, d), jnp.float32) * scale}
    _L0_attn_in = _L0_attn_setup()

    def _L0_ffn_setup():
        import jax, jax.numpy as jnp
        import numpy as np
        B, T, D = (2, 256, 128)
        DCD = 512
        RET = 128
        NEXP = 512
        NKEYS = 64
        H = 4
        KPH = 8
        key = jax.random.key(seed)
        ks = jax.random.split(key, 10)
        s = lambda k, shape, scale: jax.random.normal(k, shape, jnp.float32) * scale
        return {'hidden_states': jax.random.normal(ks[0], (B, T, D), jnp.float32), 'Wg': s(ks[1], (D, DCD), 0.02), 'bg': jnp.zeros((DCD,), jnp.float32), 'Wu': s(ks[2], (D, DCD), 0.02), 'bu': jnp.zeros((DCD,), jnp.float32), 'Wd': s(ks[3], (DCD, D), 0.02), 'bd': jnp.zeros((D,), jnp.float32), 'Wq': s(ks[4], (D, RET * H), 0.02), 'keys': s(ks[5], (H, NKEYS, 2, RET // 2), 0.02), 'down_embed': s(ks[6], (NEXP, D), 0.02), 'up_embed': s(ks[7], (NEXP, D), 0.02)}
    _L0_ffn_in = _L0_ffn_setup()

    def _L1_attn_setup():
        import jax, jax.numpy as jnp
        import numpy as np
        from jax import lax
        B, T, D = (2, 256, 128)
        D_STATE, EXPAND, K = (64, 2, 3)
        INNER = D * EXPAND
        FF_MULT, E, TOP_K = (4, 4, 2)
        HID = D * FF_MULT

        def _rmsnorm(x, w, eps=1e-06):
            nr = lax.rsqrt(jnp.mean(x * x, axis=-1, keepdims=True) + eps)
            return x * nr * w

        def _layernorm(x, eps=1e-05):
            mu = jnp.mean(x, axis=-1, keepdims=True)
            var = jnp.mean((x - mu) ** 2, axis=-1, keepdims=True)
            return (x - mu) * lax.rsqrt(var + eps)

        def _mixer(h, in_proj_w, in_proj_b, conv_w, conv_b, dt_w, dt_b, bp_w, bp_b, cp_w, cp_b, s2i_w, s2i_b, D_param, out_w, out_b):
            seq_len = h.shape[1]
            xz = h @ in_proj_w + in_proj_b
            x_main, gate = jnp.split(xz, 2, axis=-1)
            xc = jnp.swapaxes(x_main, 1, 2)
            xc = lax.conv_general_dilated(xc, conv_w, window_strides=(1,), padding=[(K - 1, K - 1)], dimension_numbers=('NCH', 'OIH', 'NCH'), feature_group_count=INNER)
            xc = xc[..., :seq_len] + conv_b[None, :, None]
            x_main = jax.nn.silu(jnp.swapaxes(xc, 1, 2))
            dt = jax.nn.sigmoid(x_main @ dt_w + dt_b)
            Bm = x_main @ bp_w + bp_b
            Cm = x_main @ cp_w + cp_b

            def step(state, inp):
                dt_t, b_t, c_t = inp
                state = (1.0 - dt_t) * state + dt_t * b_t
                return (state, c_t * state)
            init = jnp.zeros((h.shape[0], D_STATE), h.dtype)
            _, y = lax.scan(step, init, (jnp.swapaxes(dt, 0, 1), jnp.swapaxes(Bm, 0, 1), jnp.swapaxes(Cm, 0, 1)))
            y = jnp.swapaxes(y, 0, 1)
            y = _layernorm(y)
            y = y @ s2i_w + s2i_b
            y = y + D_param * x_main
            y = y * jax.nn.sigmoid(gate)
            return y @ out_w + out_b

        def _moe(h, gate_w, gate_b, e_w1, e_b1, e_w2, e_b2):
            logits = h @ gate_w + gate_b
            top_vals, top_idx = lax.top_k(logits, TOP_K)
            top_probs = jax.nn.softmax(top_vals, axis=-1)
            w_full = jnp.sum(jax.nn.one_hot(top_idx, E, dtype=h.dtype) * top_probs[..., None], axis=-2)
            hid = jax.nn.gelu(jnp.einsum('btd,edh->ebth', h, e_w1) + e_b1[:, None, None, :], approximate=False)
            eo = jnp.einsum('ebth,ehd->ebtd', hid, e_w2) + e_b2[:, None, None, :]
            return jnp.einsum('ebtd,bte->btd', eo, w_full)
        key = jax.random.key(seed)
        ks = jax.random.split(key, 20)
        s = 0.02
        inp = {'x': jax.random.normal(ks[0], (B, T, D), jnp.float32), 'norm1_w': jnp.ones((D,), jnp.float32), 'norm2_w': jnp.ones((D,), jnp.float32), 'in_proj_w': jax.random.normal(ks[1], (D, 2 * INNER), jnp.float32) * s, 'in_proj_b': jnp.zeros((2 * INNER,), jnp.float32), 'conv_w': jax.random.normal(ks[2], (INNER, 1, K), jnp.float32) * s, 'conv_b': jnp.zeros((INNER,), jnp.float32), 'dt_w': jax.random.normal(ks[3], (INNER, D_STATE), jnp.float32) * s, 'dt_b': jnp.zeros((D_STATE,), jnp.float32), 'bp_w': jax.random.normal(ks[4], (INNER, D_STATE), jnp.float32) * s, 'bp_b': jnp.zeros((D_STATE,), jnp.float32), 'cp_w': jax.random.normal(ks[5], (INNER, D_STATE), jnp.float32) * s, 'cp_b': jnp.zeros((D_STATE,), jnp.float32), 's2i_w': jax.random.normal(ks[6], (D_STATE, INNER), jnp.float32) * s, 's2i_b': jnp.zeros((INNER,), jnp.float32), 'D_param': jnp.ones((INNER,), jnp.float32), 'out_w': jax.random.normal(ks[7], (INNER, D), jnp.float32) * s, 'out_b': jnp.zeros((D,), jnp.float32), 'gate_w': jax.random.normal(ks[8], (D, E), jnp.float32) * s, 'gate_b': jnp.zeros((E,), jnp.float32), 'e_w1': jax.random.normal(ks[9], (E, D, HID), jnp.float32) * s, 'e_b1': jnp.zeros((E, HID), jnp.float32), 'e_w2': jax.random.normal(ks[10], (E, HID, D), jnp.float32) * s, 'e_b2': jnp.zeros((E, D), jnp.float32)}
        return inp
    _L1_attn_in = _L1_attn_setup()

    def _L1_ffn_setup():
        import jax, jax.numpy as jnp
        import numpy as np
        DIM = 128
        DEPTH = 6
        HEADS = 16
        DIM_HEAD = 64
        WINDOW = 32
        INNER = HEADS * DIM_HEAD
        DIM_INNER = int(DIM * 4 * 2 / 3)
        QK_SCALE = 8.0

        def shift_tokens(t):
            a, s = jnp.split(t, 2, -1)
            s = jnp.pad(s, ((0, 0), (1, 0), (0, 0)))[:, :-1]
            return jnp.concatenate([a, s], -1)

        def l2norm(t):
            return t / jnp.maximum(jnp.linalg.norm(t, axis=-1, keepdims=True), 1e-12)

        def rotate_half(x):
            x1, x2 = jnp.split(x, 2, -1)
            return jnp.concatenate([-x2, x1], -1)

        def rotary_tables(n):
            half = jnp.arange(0, DIM_HEAD, 2, dtype=jnp.float32)
            inv_freq = 1.0 / 10000.0 ** (half / DIM_HEAD)
            t = jnp.arange(n, dtype=jnp.float32)
            freqs = t[:, None] * inv_freq[None, :]
            freqs = jnp.concatenate([freqs, freqs], -1)
            base_scale = (half + 0.4 * DIM_HEAD) / (1.4 * DIM_HEAD)
            power = (t - n // 2) / (WINDOW // 2)
            scale = base_scale[None, :] ** power[:, None]
            scale = jnp.concatenate([scale, scale], -1)
            return (freqs, scale)

        def local_attention(q, k, v):
            b, h, n, d = q.shape
            w = WINDOW
            nw = n // w
            bq = q.reshape(b, h, nw, w, d)
            bk = k.reshape(b, h, nw, w, d)
            bv = v.reshape(b, h, nw, w, d)

            def look(t):
                p = jnp.pad(t, ((0, 0), (0, 0), (1, 0), (0, 0), (0, 0)))
                return jnp.concatenate([p[:, :, :nw], p[:, :, 1:]], axis=3)
            bk2, bv2 = (look(bk), look(bv))
            seq = jnp.arange(n).reshape(nw, w)
            seq_p = jnp.pad(seq, ((1, 0), (0, 0)), constant_values=-1)
            jt = jnp.concatenate([seq_p[:nw], seq_p[1:]], axis=1)
            it = seq[:, :, None]
            jb = jt[:, None, :]
            mask = (it < jb) | (it > jb + w) | (jb == -1)
            sim = jnp.einsum('bhwie,bhwje->bhwij', bq, bk2) * QK_SCALE
            sim = jnp.where(mask, -jnp.finfo(sim.dtype).max, sim)
            attn = jax.nn.softmax(sim, -1)
            out = jnp.einsum('bhwij,bhwje->bhwie', attn, bv2)
            return out.reshape(b, h, n, d)

        def attn_layer(x, Wqkv, qs, ksc, Wo):
            b, n, _ = x.shape
            qkv = x @ Wqkv
            q, k, v = jnp.split(qkv, 3, -1)
            sh = lambda t: t.reshape(b, n, HEADS, DIM_HEAD).transpose(0, 2, 1, 3)
            q, k, v = (sh(q), sh(k), sh(v))
            q = l2norm(q) * qs
            k = l2norm(k) * ksc
            freqs, scale = rotary_tables(n)
            cos, sin = (jnp.cos(freqs), jnp.sin(freqs))
            q = q * cos * scale + rotate_half(q) * sin * scale
            inv = 1.0 / scale
            k = k * cos * inv + rotate_half(k) * sin * inv
            out = local_attention(q, k, v)
            out = out.transpose(0, 2, 1, 3).reshape(b, n, INNER)
            return out @ Wo

        def ffn_layer(x, g, bln, W1, b1, W2, b2):
            mu = x.mean(-1, keepdims=True)
            var = ((x - mu) ** 2).mean(-1, keepdims=True)
            xn = (x - mu) / jnp.sqrt(var + 1e-05) * g + bln
            hg = xn @ W1 + b1
            a, gate = jnp.split(hg, 2, -1)
            return a * jax.nn.gelu(gate, approximate=False) @ W2 + b2
        key = jax.random.key(seed)
        ks = jax.random.split(key, 8)
        B, N = (2, 256)
        init = lambda k, shape: jax.random.normal(k, shape, jnp.float32) * 0.02
        return {'x': jax.random.normal(ks[0], (B, N, DIM), jnp.float32), 'Wqkv': init(ks[1], (DEPTH, DIM, 3 * INNER)), 'q_scale': jnp.ones((DEPTH, DIM_HEAD), jnp.float32), 'k_scale': jnp.ones((DEPTH, DIM_HEAD), jnp.float32), 'Wo': init(ks[2], (DEPTH, INNER, DIM)), 'ln_g': jnp.ones((DEPTH, DIM), jnp.float32), 'ln_b': jnp.zeros((DEPTH, DIM), jnp.float32), 'W1': init(ks[3], (DEPTH, DIM, 2 * DIM_INNER)), 'b1': jnp.zeros((DEPTH, 2 * DIM_INNER), jnp.float32), 'W2': init(ks[4], (DEPTH, DIM_INNER, DIM)), 'b2': jnp.zeros((DEPTH, DIM), jnp.float32)}
    _L1_ffn_in = _L1_ffn_setup()
    _d = {'L0_attn_hidden_states': _L0_attn_in['hidden_states'], 'L0_attn_Wq': _L0_attn_in['Wq'], 'L0_attn_Wk': _L0_attn_in['Wk'], 'L0_attn_Wv': _L0_attn_in['Wv'], 'L0_attn_Wo': _L0_attn_in['Wo'], 'L0_ffn_Wg': _L0_ffn_in['Wg'], 'L0_ffn_bg': _L0_ffn_in['bg'], 'L0_ffn_Wu': _L0_ffn_in['Wu'], 'L0_ffn_bu': _L0_ffn_in['bu'], 'L0_ffn_Wd': _L0_ffn_in['Wd'], 'L0_ffn_bd': _L0_ffn_in['bd'], 'L0_ffn_Wq': _L0_ffn_in['Wq'], 'L0_ffn_keys': _L0_ffn_in['keys'], 'L0_ffn_down_embed': _L0_ffn_in['down_embed'], 'L0_ffn_up_embed': _L0_ffn_in['up_embed'], 'L1_attn_norm1_w': _L1_attn_in['norm1_w'], 'L1_attn_norm2_w': _L1_attn_in['norm2_w'], 'L1_attn_in_proj_w': _L1_attn_in['in_proj_w'], 'L1_attn_in_proj_b': _L1_attn_in['in_proj_b'], 'L1_attn_conv_w': _L1_attn_in['conv_w'], 'L1_attn_conv_b': _L1_attn_in['conv_b'], 'L1_attn_dt_w': _L1_attn_in['dt_w'], 'L1_attn_dt_b': _L1_attn_in['dt_b'], 'L1_attn_bp_w': _L1_attn_in['bp_w'], 'L1_attn_bp_b': _L1_attn_in['bp_b'], 'L1_attn_cp_w': _L1_attn_in['cp_w'], 'L1_attn_cp_b': _L1_attn_in['cp_b'], 'L1_attn_s2i_w': _L1_attn_in['s2i_w'], 'L1_attn_s2i_b': _L1_attn_in['s2i_b'], 'L1_attn_D_param': _L1_attn_in['D_param'], 'L1_attn_out_w': _L1_attn_in['out_w'], 'L1_attn_out_b': _L1_attn_in['out_b'], 'L1_attn_gate_w': _L1_attn_in['gate_w'], 'L1_attn_gate_b': _L1_attn_in['gate_b'], 'L1_attn_e_w1': _L1_attn_in['e_w1'], 'L1_attn_e_b1': _L1_attn_in['e_b1'], 'L1_attn_e_w2': _L1_attn_in['e_w2'], 'L1_attn_e_b2': _L1_attn_in['e_b2'], 'L1_ffn_Wqkv': _L1_ffn_in['Wqkv'], 'L1_ffn_q_scale': _L1_ffn_in['q_scale'], 'L1_ffn_k_scale': _L1_ffn_in['k_scale'], 'L1_ffn_Wo': _L1_ffn_in['Wo'], 'L1_ffn_ln_g': _L1_ffn_in['ln_g'], 'L1_ffn_ln_b': _L1_ffn_in['ln_b'], 'L1_ffn_W1': _L1_ffn_in['W1'], 'L1_ffn_b1': _L1_ffn_in['b1'], 'L1_ffn_W2': _L1_ffn_in['W2'], 'L1_ffn_b2': _L1_ffn_in['b2']}
    _x0 = _d['L0_attn_hidden_states']
    _d['L0_attn_hidden_states'] = jax.random.normal(jax.random.fold_in(jax.random.key(seed), 1), (8, 512, 128), dtype=_x0.dtype)
    del _x0
    return _d

def reference(L0_attn_hidden_states, L0_attn_Wq, L0_attn_Wk, L0_attn_Wv, L0_attn_Wo, L0_ffn_Wg, L0_ffn_bg, L0_ffn_Wu, L0_ffn_bu, L0_ffn_Wd, L0_ffn_bd, L0_ffn_Wq, L0_ffn_keys, L0_ffn_down_embed, L0_ffn_up_embed, L1_attn_norm1_w, L1_attn_norm2_w, L1_attn_in_proj_w, L1_attn_in_proj_b, L1_attn_conv_w, L1_attn_conv_b, L1_attn_dt_w, L1_attn_dt_b, L1_attn_bp_w, L1_attn_bp_b, L1_attn_cp_w, L1_attn_cp_b, L1_attn_s2i_w, L1_attn_s2i_b, L1_attn_D_param, L1_attn_out_w, L1_attn_out_b, L1_attn_gate_w, L1_attn_gate_b, L1_attn_e_w1, L1_attn_e_b1, L1_attn_e_w2, L1_attn_e_b2, L1_ffn_Wqkv, L1_ffn_q_scale, L1_ffn_k_scale, L1_ffn_Wo, L1_ffn_ln_g, L1_ffn_ln_b, L1_ffn_W1, L1_ffn_b1, L1_ffn_W2, L1_ffn_b2):

    def _L0_attn_ref(hidden_states, Wq, Wk, Wv, Wo):
        import jax, jax.numpy as jnp
        import numpy as np
        EPS = 1e-05
        NUM_HEADS = 16
        FEATURE_DIM = 16
        CHUNK = 64

        def _phi(x):
            f = x.shape[-1]
            return (x[..., :, None] * x[..., None, :]).reshape(*x.shape[:-1], f * f)
        b, l, d = hidden_states.shape
        h, f = (NUM_HEADS, FEATURE_DIM)
        hd = d // h
        q = (hidden_states @ Wq).reshape(b, l, h, f).transpose(0, 2, 1, 3)
        k = (hidden_states @ Wk).reshape(b, l, h, f).transpose(0, 2, 1, 3)
        v = (hidden_states @ Wv).reshape(b, l, h, hd).transpose(0, 2, 1, 3)
        q = q * f ** (-0.5)
        n = l // CHUNK
        qc = q.reshape(b, h, n, CHUNK, f)
        kc = k.reshape(b, h, n, CHUNK, f)
        vc = v.reshape(b, h, n, CHUNK, hd)
        phi_q = _phi(qc)
        phi_k = _phi(kc)
        mask = jnp.tril(jnp.ones((CHUNK, CHUNK), dtype=q.dtype))

        def step(carry, inp):
            S, z = carry
            pq, pk, qi, ki, vi = inp
            inter_o = jnp.einsum('bhcf,bhfd->bhcd', pq, S)
            inter_z = jnp.einsum('bhcf,bhf->bhc', pq, z)
            A = jnp.einsum('bhcf,bhsf->bhcs', qi, ki) ** 2 * mask
            intra_o = jnp.einsum('bhcs,bhsd->bhcd', A, vi)
            intra_z = A.sum(-1)
            o = (inter_o + intra_o) / (inter_z + intra_z + EPS)[..., None]
            S = S + jnp.einsum('bhcf,bhcd->bhfd', pk, vi)
            z = z + pk.sum(2)
            return ((S, z), o)
        f2 = f * f
        S0 = jnp.zeros((b, h, f2, hd), q.dtype)
        z0 = jnp.zeros((b, h, f2), q.dtype)
        xs = (jnp.moveaxis(phi_q, 2, 0), jnp.moveaxis(phi_k, 2, 0), jnp.moveaxis(qc, 2, 0), jnp.moveaxis(kc, 2, 0), jnp.moveaxis(vc, 2, 0))
        _, o = jax.lax.scan(step, (S0, z0), xs)
        o = jnp.moveaxis(o, 0, 2).reshape(b, h, l, hd)
        o = o.transpose(0, 2, 1, 3).reshape(b, l, h * hd)
        return o @ Wo

    def _L0_ffn_ref(hidden_states, Wg, bg, Wu, bu, Wd, bd, Wq, keys, down_embed, up_embed):
        import jax, jax.numpy as jnp
        import numpy as np
        B, T, D = (2, 256, 128)
        DCD = 512
        RET = 128
        NEXP = 512
        NKEYS = 64
        H = 4
        KPH = 8
        b, t, d = hidden_states.shape
        q = (hidden_states @ Wq).reshape(b, t, 2, H, RET // 2)
        sim = jnp.einsum('btphn,hkpn->pbthk', q, keys)
        sc, ix = jax.lax.top_k(sim, KPH)
        sx, sy = (sc[0], sc[1])
        ixx, ixy = (ix[0], ix[1])
        all_sc = (sx[..., :, None] + sy[..., None, :]).reshape(b, t, H, KPH * KPH)
        all_ix = (ixx[..., :, None] * NKEYS + ixy[..., None, :]).reshape(b, t, H, KPH * KPH)
        scores, pk = jax.lax.top_k(all_sc, KPH)
        idx = jnp.take_along_axis(all_ix, pk, axis=-1)
        de = down_embed[idx]
        ue = up_embed[idx]
        w = jnp.einsum('btd,bthkd->bthk', hidden_states, de)
        w = jax.nn.silu(w) * jax.nn.softmax(scores, axis=-1)
        experts_states = jnp.einsum('bthk,bthkd->btd', w, ue)
        mlp = jax.nn.silu(hidden_states @ Wg + bg) * (hidden_states @ Wu + bu) @ Wd + bd
        return mlp + experts_states

    def _L1_attn_ref(x, norm1_w, norm2_w, in_proj_w, in_proj_b, conv_w, conv_b, dt_w, dt_b, bp_w, bp_b, cp_w, cp_b, s2i_w, s2i_b, D_param, out_w, out_b, gate_w, gate_b, e_w1, e_b1, e_w2, e_b2):
        import jax, jax.numpy as jnp
        import numpy as np
        from jax import lax
        B, T, D = (2, 256, 128)
        D_STATE, EXPAND, K = (64, 2, 3)
        INNER = D * EXPAND
        FF_MULT, E, TOP_K = (4, 4, 2)
        HID = D * FF_MULT

        def _rmsnorm(x, w, eps=1e-06):
            nr = lax.rsqrt(jnp.mean(x * x, axis=-1, keepdims=True) + eps)
            return x * nr * w

        def _layernorm(x, eps=1e-05):
            mu = jnp.mean(x, axis=-1, keepdims=True)
            var = jnp.mean((x - mu) ** 2, axis=-1, keepdims=True)
            return (x - mu) * lax.rsqrt(var + eps)

        def _mixer(h, in_proj_w, in_proj_b, conv_w, conv_b, dt_w, dt_b, bp_w, bp_b, cp_w, cp_b, s2i_w, s2i_b, D_param, out_w, out_b):
            seq_len = h.shape[1]
            xz = h @ in_proj_w + in_proj_b
            x_main, gate = jnp.split(xz, 2, axis=-1)
            xc = jnp.swapaxes(x_main, 1, 2)
            xc = lax.conv_general_dilated(xc, conv_w, window_strides=(1,), padding=[(K - 1, K - 1)], dimension_numbers=('NCH', 'OIH', 'NCH'), feature_group_count=INNER)
            xc = xc[..., :seq_len] + conv_b[None, :, None]
            x_main = jax.nn.silu(jnp.swapaxes(xc, 1, 2))
            dt = jax.nn.sigmoid(x_main @ dt_w + dt_b)
            Bm = x_main @ bp_w + bp_b
            Cm = x_main @ cp_w + cp_b

            def step(state, inp):
                dt_t, b_t, c_t = inp
                state = (1.0 - dt_t) * state + dt_t * b_t
                return (state, c_t * state)
            init = jnp.zeros((h.shape[0], D_STATE), h.dtype)
            _, y = lax.scan(step, init, (jnp.swapaxes(dt, 0, 1), jnp.swapaxes(Bm, 0, 1), jnp.swapaxes(Cm, 0, 1)))
            y = jnp.swapaxes(y, 0, 1)
            y = _layernorm(y)
            y = y @ s2i_w + s2i_b
            y = y + D_param * x_main
            y = y * jax.nn.sigmoid(gate)
            return y @ out_w + out_b

        def _moe(h, gate_w, gate_b, e_w1, e_b1, e_w2, e_b2):
            logits = h @ gate_w + gate_b
            top_vals, top_idx = lax.top_k(logits, TOP_K)
            top_probs = jax.nn.softmax(top_vals, axis=-1)
            w_full = jnp.sum(jax.nn.one_hot(top_idx, E, dtype=h.dtype) * top_probs[..., None], axis=-2)
            hid = jax.nn.gelu(jnp.einsum('btd,edh->ebth', h, e_w1) + e_b1[:, None, None, :], approximate=False)
            eo = jnp.einsum('ebth,ehd->ebtd', hid, e_w2) + e_b2[:, None, None, :]
            return jnp.einsum('ebtd,bte->btd', eo, w_full)
        x = x + _mixer(_rmsnorm(x, norm1_w), in_proj_w, in_proj_b, conv_w, conv_b, dt_w, dt_b, bp_w, bp_b, cp_w, cp_b, s2i_w, s2i_b, D_param, out_w, out_b)
        x = x + _moe(_rmsnorm(x, norm2_w), gate_w, gate_b, e_w1, e_b1, e_w2, e_b2)
        return x

    def _L1_ffn_ref(x, Wqkv, q_scale, k_scale, Wo, ln_g, ln_b, W1, b1, W2, b2):
        import jax, jax.numpy as jnp
        import numpy as np
        DIM = 128
        DEPTH = 6
        HEADS = 16
        DIM_HEAD = 64
        WINDOW = 32
        INNER = HEADS * DIM_HEAD
        DIM_INNER = int(DIM * 4 * 2 / 3)
        QK_SCALE = 8.0

        def shift_tokens(t):
            a, s = jnp.split(t, 2, -1)
            s = jnp.pad(s, ((0, 0), (1, 0), (0, 0)))[:, :-1]
            return jnp.concatenate([a, s], -1)

        def l2norm(t):
            return t / jnp.maximum(jnp.linalg.norm(t, axis=-1, keepdims=True), 1e-12)

        def rotate_half(x):
            x1, x2 = jnp.split(x, 2, -1)
            return jnp.concatenate([-x2, x1], -1)

        def rotary_tables(n):
            half = jnp.arange(0, DIM_HEAD, 2, dtype=jnp.float32)
            inv_freq = 1.0 / 10000.0 ** (half / DIM_HEAD)
            t = jnp.arange(n, dtype=jnp.float32)
            freqs = t[:, None] * inv_freq[None, :]
            freqs = jnp.concatenate([freqs, freqs], -1)
            base_scale = (half + 0.4 * DIM_HEAD) / (1.4 * DIM_HEAD)
            power = (t - n // 2) / (WINDOW // 2)
            scale = base_scale[None, :] ** power[:, None]
            scale = jnp.concatenate([scale, scale], -1)
            return (freqs, scale)

        def local_attention(q, k, v):
            b, h, n, d = q.shape
            w = WINDOW
            nw = n // w
            bq = q.reshape(b, h, nw, w, d)
            bk = k.reshape(b, h, nw, w, d)
            bv = v.reshape(b, h, nw, w, d)

            def look(t):
                p = jnp.pad(t, ((0, 0), (0, 0), (1, 0), (0, 0), (0, 0)))
                return jnp.concatenate([p[:, :, :nw], p[:, :, 1:]], axis=3)
            bk2, bv2 = (look(bk), look(bv))
            seq = jnp.arange(n).reshape(nw, w)
            seq_p = jnp.pad(seq, ((1, 0), (0, 0)), constant_values=-1)
            jt = jnp.concatenate([seq_p[:nw], seq_p[1:]], axis=1)
            it = seq[:, :, None]
            jb = jt[:, None, :]
            mask = (it < jb) | (it > jb + w) | (jb == -1)
            sim = jnp.einsum('bhwie,bhwje->bhwij', bq, bk2) * QK_SCALE
            sim = jnp.where(mask, -jnp.finfo(sim.dtype).max, sim)
            attn = jax.nn.softmax(sim, -1)
            out = jnp.einsum('bhwij,bhwje->bhwie', attn, bv2)
            return out.reshape(b, h, n, d)

        def attn_layer(x, Wqkv, qs, ksc, Wo):
            b, n, _ = x.shape
            qkv = x @ Wqkv
            q, k, v = jnp.split(qkv, 3, -1)
            sh = lambda t: t.reshape(b, n, HEADS, DIM_HEAD).transpose(0, 2, 1, 3)
            q, k, v = (sh(q), sh(k), sh(v))
            q = l2norm(q) * qs
            k = l2norm(k) * ksc
            freqs, scale = rotary_tables(n)
            cos, sin = (jnp.cos(freqs), jnp.sin(freqs))
            q = q * cos * scale + rotate_half(q) * sin * scale
            inv = 1.0 / scale
            k = k * cos * inv + rotate_half(k) * sin * inv
            out = local_attention(q, k, v)
            out = out.transpose(0, 2, 1, 3).reshape(b, n, INNER)
            return out @ Wo

        def ffn_layer(x, g, bln, W1, b1, W2, b2):
            mu = x.mean(-1, keepdims=True)
            var = ((x - mu) ** 2).mean(-1, keepdims=True)
            xn = (x - mu) / jnp.sqrt(var + 1e-05) * g + bln
            hg = xn @ W1 + b1
            a, gate = jnp.split(hg, 2, -1)
            return a * jax.nn.gelu(gate, approximate=False) @ W2 + b2
        for i in range(DEPTH):
            x = attn_layer(shift_tokens(x), Wqkv[i], q_scale[i], k_scale[i], Wo[i]) + x
            x = ffn_layer(shift_tokens(x), ln_g[i], ln_b[i], W1[i], b1[i], W2[i], b2[i]) + x
        return x
    x = L0_attn_hidden_states
    xn = _layernorm(x, axis=-1)
    s = _L0_attn_ref(xn, L0_attn_Wq, L0_attn_Wk, L0_attn_Wv, L0_attn_Wo)
    g = _silu(_L0_ffn_ref(xn, L0_ffn_Wg, L0_ffn_bg, L0_ffn_Wu, L0_ffn_bu, L0_ffn_Wd, L0_ffn_bd, L0_ffn_Wq, L0_ffn_keys, L0_ffn_down_embed, L0_ffn_up_embed))
    x = x + s * g
    xn = _layernorm(x, axis=-1)
    s = _L1_attn_ref(xn, L1_attn_norm1_w, L1_attn_norm2_w, L1_attn_in_proj_w, L1_attn_in_proj_b, L1_attn_conv_w, L1_attn_conv_b, L1_attn_dt_w, L1_attn_dt_b, L1_attn_bp_w, L1_attn_bp_b, L1_attn_cp_w, L1_attn_cp_b, L1_attn_s2i_w, L1_attn_s2i_b, L1_attn_D_param, L1_attn_out_w, L1_attn_out_b, L1_attn_gate_w, L1_attn_gate_b, L1_attn_e_w1, L1_attn_e_b1, L1_attn_e_w2, L1_attn_e_b2)
    g = _silu(_L1_ffn_ref(xn, L1_ffn_Wqkv, L1_ffn_q_scale, L1_ffn_k_scale, L1_ffn_Wo, L1_ffn_ln_g, L1_ffn_ln_b, L1_ffn_W1, L1_ffn_b1, L1_ffn_W2, L1_ffn_b2))
    x = x + s * g
    return x

_drawn_inputs = setup_inputs


def setup_inputs(seed=0):
    import zlib

    import numpy as np

    out = dict(_drawn_inputs(seed))
    spreads = {'L0_ffn_bg': (0.0, 0.8),
     'L0_ffn_bu': (0.0, 0.8),
     'L0_ffn_bd': (0.0, 0.8),
     'L1_attn_norm1_w': (1.0, 0.6),
     'L1_attn_norm2_w': (1.0, 0.6),
     'L1_attn_in_proj_b': (0.0, 0.8),
     'L1_attn_conv_b': (0.0, 0.8),
     'L1_attn_dt_b': (0.0, 0.8),
     'L1_attn_bp_b': (0.0, 0.774),
     'L1_attn_cp_b': (0.0, 0.735),
     'L1_attn_s2i_b': (0.0, 0.8),
     'L1_attn_D_param': (1.0, 0.6),
     'L1_attn_out_b': (0.0, 0.1),
     'L1_attn_gate_b': (0.0, 0.509),
     'L1_attn_e_b1': (0.0, 0.8),
     'L1_attn_e_b2': (0.0, 0.333),
     'L1_ffn_q_scale': (1.0, 0.6),
     'L1_ffn_k_scale': (1.0, 0.6),
     'L1_ffn_ln_g': (1.0, 0.6),
     'L1_ffn_ln_b': (0.0, 0.8),
     'L1_ffn_b1': (0.0, 0.8),
     'L1_ffn_b2': (0.0, 0.1)}
    factors = {'L0_attn_Wq': 8.0,
     'L0_attn_Wk': 8.0,
     'L0_attn_Wv': 8.0,
     'L0_attn_Wo': 8.0,
     'L0_ffn_Wg': 8.0,
     'L0_ffn_Wu': 8.0,
     'L0_ffn_Wd': 8.0,
     'L0_ffn_Wq': 8.0,
     'L0_ffn_keys': 8.0,
     'L0_ffn_down_embed': 8.0,
     'L0_ffn_up_embed': 8.0,
     'L1_attn_in_proj_w': 8.0,
     'L1_attn_conv_w': 8.0,
     'L1_attn_dt_w': 8.0,
     'L1_attn_bp_w': 8.0,
     'L1_attn_cp_w': 8.0,
     'L1_attn_s2i_w': 6.128,
     'L1_attn_out_w': 5.524,
     'L1_attn_gate_w': 3.05,
     'L1_attn_e_w1': 4.22,
     'L1_attn_e_w2': 3.78,
     'L1_ffn_W1': 4.558,
     'L1_ffn_W2': 4.45}
    for name, (base, spread) in spreads.items():
        noise = np.random.default_rng([zlib.crc32(name.encode()), seed]).standard_normal(out[name].shape)
        drawn = base * np.exp(spread * noise) if base else spread * noise
        out[name] = jnp.asarray(drawn.astype(out[name].dtype))
    for name, factor in factors.items():
        out[name] = (out[name] * factor).astype(out[name].dtype)
    return out
```

```python
from contextlib import ExitStack

import numpy as np

import concourse.bass as bass
from concourse import mybir
from concourse.alu_op_type import AluOpType as ALU

ACT = mybir.ActivationFunctionType
F32 = mybir.dt.float32
BF16 = mybir.dt.bfloat16
AX = mybir.AxisListType

P = 128
SEQS, SEQ = 8, 512
TILE = 128
TILES = SEQ // TILE
DEPTH = 6
HEADS, DH = 16, 64
HALF = DH // 2
LOOK = 32
BAND = LOOK + TILE
FF = 341
FCH = [(0, 128), (128, 128), (256, FF - 256)]
QK_SCALE = 8.0
NORM_MIN = 1e-12
LN_SHIFT = 20

W_QK = 0
W_V = W_QK + 2 * HEADS * DH
W_O = W_V + HEADS * DH
W_1 = W_O + HEADS * DH
W_2 = W_1 + 2 * FF
W_P = W_2 + 3 * P
PAR = {"qA": 0, "qB": 1, "kA": 2, "kB": 3, "g": 4, "b": 5, "b1": 6, "b2": 12}
W_END = W_P + 13


class Signal:

    def __init__(self, sem, per=0, primed=0):
        self.sem, self.per, self.primed, self.n = sem, per, primed, 0

    def prime(self):
        assert self.primed
        return self.sem, 1

    def up(self):
        self.n += 1
        return self.sem, 1

    def nth(self, n, turn=0):
        assert n + self.primed > 0
        return self.sem, turn * self.per + (n + self.primed) if self.per else n

    def last(self, turn=0):
        return self.nth(self.n, turn)

    def full(self):
        assert self.n == self.per, (self.n, self.per)


def network(nc, xf, w_dram, tab_dram, const, depth, seqs):
    with ExitStack() as ctx:
        def sb(name, shape, dt=F32):
            return ctx.enter_context(nc.sbuf_tensor("c_" + name, shape, dt))

        def ps(name, shape, dt=F32):
            return ctx.enter_context(nc.psum_tensor("c_" + name, shape, dt))

        def sig(name, per=0, primed=0):
            return Signal(ctx.enter_context(nc.semaphore("c_" + name)), per, primed)

        ident, ones_mean, ones_head, col = const.ident, const.mean, const.head, const.col
        W = sb("W", [P, W_END])
        base = sb("base", [P, 4, SEQ])
        TC = sb("TC", [P, 2, 2, SEQ])
        TS = sb("TS", [P, 2, 2, SEQ])
        xs = sb("xs", [P, SEQ])
        ab = sb("ab", [P, 2, 2, SEQ])
        sq = sb("sq", [P, 2, SEQ])
        lnr = sb("lnr", [P, SEQ])
        rinv = sb("rinv", [P, 2, SEQ])
        tc_ = sb("tc", [P, 2, SEQ])
        ts_ = sb("ts", [P, 2, SEQ])
        rot = sb("rot", [P, 2, 2, SEQ])
        QK = sb("QK", [P, 2, 4, 2, SEQ])
        V = sb("V", [P, TILES, HEADS * DH])
        OT = sb("OT", [P, HEADS // 2, SEQ])
        mx = sb("mx", [P, 2, 4])
        nb = sb("nb", [P, 2, 4])
        sums = sb("sums", [P, 2, 4])
        rs = sb("rs", [P, 2, 4])
        Pb = sb("Pb", [P, 2, 4, 96 + BAND])
        PTs = sb("PTs", [P, 2, 4, TILE])
        PT2s = sb("PT2s", [P, 2, 4, LOOK])
        x1 = sb("x1", [P, 1 + SEQ])
        xs2 = sb("xs2", [P, SEQ])
        cen = sb("cen", [P, SEQ])
        csq = sb("csq", [P, SEQ])
        rstd = sb("rstd", [P, SEQ])
        xn = sb("xn", [P, SEQ])
        gl = sb("gl", [P, 3, SEQ])
        hh = sb("hh", [P, 3, SEQ])
        S = ps("S", [P, 4, 512])
        PAB = ps("PAB", [P, 2, 512])
        PT = ps("PT", [P, 512])
        PX = ps("PX", [P, 512])

        def wqk(kind, g, half):
            c = W_QK + ((kind * 4 + g) * 2 + half) * P
            return W[:, c:c + P]

        def par(name, k=0):
            return W[:, W_P + PAR[name] + k:W_P + PAR[name] + k + 1]

        NS = 16
        weights_in = sig("weights_in")
        base_in = sig("base_in")
        layer_done = sig("layer_done", 1, 1)
        tables = sig("tables", 8)
        zeroed = sig("zeroed")
        shifted = sig("shifted", 2)
        projected = sig("projected", 8)
        copied = sig("copied", 8)
        summed = sig("summed", 8)
        logs = sig("logs", 8)
        rinvs = sig("rinvs", 8)
        prods = sig("prods", 16)
        rotated = sig("rotated", 16)
        qk_ready = sig("qk_ready", 8)
        v_done = sig("v_done", 8)
        v_copied = sig("v_copied", 8)
        s_done = sig("s_done", NS)
        maxed = sig("maxed", NS)
        nb_ready = sig("nb_ready", NS)
        exps = sig("exps", NS)
        rs_ready = sig("rs_ready", NS)
        p_ready = sig("p_ready", NS)
        pt_done = sig("pt_done", NS)
        pt_copied = sig("pt_copied", NS)
        px_copied = sig("px_copied", 12)
        pv_done = sig("pv_done", NS)
        po_copied = sig("po_copied", NS)
        wo_done = sig("wo_done", 1)
        x1_ready = sig("x1_ready", 1)
        xs2_ready = sig("xs2_ready", 2)
        mean_done = sig("mean_done", 1)
        centred = sig("centred", 1)
        squared = sig("squared", 1)
        var_done = sig("var_done", 1)
        lnv = sig("lnv", 1)
        rstd_ready = sig("rstd_ready", 1)
        xnorm = sig("xnorm", 1)
        xn_ready = sig("xn_ready", 1)
        hg_done = sig("hg_done", 3)
        gelus = sig("gelus", 3)
        h_ready = sig("h_ready", 3)
        w2_done = sig("w2_done", 1)

        unit = [(u % 2, u // 2) for u in range(8)]
        prevs = lambda n: (n // 4) * 3 + n % 4
        gate_bank = [S[:, 0, :], S[:, 1, :], S[:, 2, :]]
        val_bank = [S[:, 3, :], PAB[:, 0, :], PX[:, :]]

        with nc.Block() as block:
            @block.sync
            def _(sp):
                sp.dma_start(base[:, :, :], tab_dram).then_inc(base_in.sem, 16)
                with sp.Fori(0, depth) as l:
                    sp.wait_ge(*layer_done.nth(0, l * seqs))
                    sp.dma_start(W[:, :], w_dram[bass.ds(l, 1), :, :].rearrange("a p c -> (a p) c")).then_inc(weights_in.sem, 16)

            @block.gpsimd
            def _(pool):
                nc.gpsimd.memset(Pb[:, :, :, 0:128], 0.0).then_inc(*zeroed.up())
                nc.gpsimd.memset(x1[:, 0:1], 0.0).then_inc(*zeroed.up())

                def rotate(u, turn):
                    pool.wait_ge(*prods.nth(2 * u + 2, turn))
                    if u >= 2:
                        pool.wait_ge(*qk_ready.nth(u - 1, turn))
                    r = rot[:, u % 2]
                    nc.gpsimd.tensor_tensor(r[:, 0, :], tc_[:, 0, :], ts_[:, 1, :], ALU.subtract).then_inc(*rotated.up())
                    nc.gpsimd.tensor_tensor(r[:, 1, :], tc_[:, 1, :], ts_[:, 0, :], ALU.add).then_inc(*rotated.up())

                def normalise(n, turn):
                    pool.wait_ge(*rs_ready.nth(n + 1, turn))
                    lo = 96 if n % 4 else 128
                    p = Pb[:, n % 2, :, lo:]
                    r = rs[:, n % 2, :].unsqueeze(2).broadcast_to([P, 4, 96 + BAND - lo])
                    nc.gpsimd.tensor_tensor(p, p, r, ALU.mult).then_inc(*p_ready.up())

                with pool.Fori(0, depth) as l:
                    with pool.Fori(0, seqs) as s:
                        turn = l * seqs + s
                        for q in (rotated, p_ready):
                            q.n = 0
                        rotate(0, turn)
                        rotate(1, turn)
                        for n in range(NS):
                            normalise(n, turn)
                            if n // 4 < 3 and n % 4 == 1:
                                rotate(2 * (n // 4) + 2, turn)
                            if n // 4 < 3 and n % 4 == 3:
                                rotate(2 * (n // 4) + 3, turn)
                        rotated.full()
                        p_ready.full()

            @block.scalar
            def _(act):
                nc.scalar.preload_act_table_set("natural_log_exp_and_others")

                def halves(u, turn):
                    act.wait_ge(*projected.nth(u + 1, turn))
                    if u >= 2:
                        act.wait_ge(*prods.nth(2 * u - 2, turn))
                    if u >= 1:
                        act.wait_ge(*summed.nth(u, turn))
                    nc.scalar.activation(ab[:, u % 2], PAB[:, :, :], ACT.Copy)
                    nc.scalar.activation(sq[:, :, :], PAB[:, :, :], ACT.Square).then_inc(*copied.up())

                def inverse_norm(u, turn):
                    act.wait_ge(*summed.nth(u + 1, turn))
                    if u >= 2:
                        act.wait_ge(*qk_ready.nth(u - 1, turn))
                    if u >= 1:
                        act.wait_ge(*rinvs.nth(u, turn))
                    nc.scalar.activation(lnr[:, :], PAB[:, 0, :], ACT.Ln, bias=col["tiny"], scale=float(2 ** LN_SHIFT)).then_inc(*logs.up())
                    act.wait_ge(*logs.nth(u + 1, turn))
                    nc.scalar.activation(rinv[:, u % 2], lnr[:, :], ACT.Exp, bias=col["shift"], scale=-0.5).then_inc(*rinvs.up())

                def v_copy(i, turn):
                    act.wait_ge(*v_done.nth(i + 1, turn))
                    src = (PT, PX)[i % 2]
                    nc.scalar.activation(V[:, i // 2, (i % 2) * 512:(i % 2) * 512 + 512], src[:, :], ACT.Copy).then_inc(*v_copied.up())

                def exp(n, turn):
                    act.wait_ge(*nb_ready.nth(n + 1, turn))
                    if n >= 2:
                        act.wait_ge(*pt_done.nth(n - 1, turn))
                        act.wait_ge(*rs_ready.nth(n - 1, turn))
                    lo = 0 if n % 4 else LOOK
                    for j in range(4):
                        e = nc.scalar.activation(Pb[:, n % 2, j, 96 + lo:], S[:, j, lo:BAND], ACT.Exp,
                                                 bias=nb[:, n % 2, j:j + 1], scale=QK_SCALE, accum_out=sums[:, n % 2, j:j + 1])
                    e.then_inc(*exps.up())

                def prev_copy(n, turn):
                    if n % 4:
                        act.wait_ge(*pt_done.nth(n + 1, turn))
                        if n >= 2:
                            act.wait_ge(*pv_done.nth(n - 1, turn))
                        nc.scalar.activation(PT2s[:, n % 2], PX[:, 256:384].rearrange("p (j q) -> p j q", j=4), ACT.Copy).then_inc(*px_copied.up())

                def out_copy(n, turn):
                    g, t = n // 4, n % 4
                    act.wait_ge(*pv_done.nth(n + 1, turn))
                    nc.scalar.activation(OT[:, 2 * g:2 * g + 2, t * TILE:(t + 1) * TILE],
                                                      PX[:, 0:256].rearrange("p (j q) -> p j q", j=2), ACT.Copy).then_inc(*po_copied.up())

                act.wait_ge(*zeroed.nth(2))
                with act.Fori(0, depth) as l:
                    with act.Fori(0, seqs) as s:
                        turn = l * seqs + s
                        act.wait_ge(weights_in.sem, l * 16 + 16)
                        mine = (copied, logs, rinvs, v_copied, exps, px_copied, po_copied, squared, lnv, rstd_ready, gelus)
                        for q in mine:
                            q.n = 0
                        halves(0, turn)
                        for i in range(4):
                            v_copy(i, turn)
                        inverse_norm(0, turn)
                        halves(1, turn)
                        for i in range(4, 8):
                            v_copy(i, turn)
                        inverse_norm(1, turn)
                        for n in range(NS + 1):
                            g = n // 4
                            if n < NS:
                                exp(n, turn)
                            if n >= 1:
                                prev_copy(n - 1, turn)
                            if n < 12 and n % 4 == 0:
                                halves(2 * g + 2, turn)
                            if n < 12 and n % 4 == 1:
                                inverse_norm(2 * g + 2, turn)
                            if n < 12 and n % 4 == 2:
                                halves(2 * g + 3, turn)
                            if n < 12 and n % 4 == 3:
                                inverse_norm(2 * g + 3, turn)
                            if n >= 1:
                                out_copy(n - 1, turn)
                        act.wait_ge(*centred.nth(1, turn))
                        nc.scalar.activation(csq[:, :], cen[:, :], ACT.Square).then_inc(*squared.up())
                        act.wait_ge(*var_done.nth(1, turn))
                        nc.scalar.activation(lnr[:, :], PAB[:, 1, :], ACT.Ln, bias=col["eps5"]).then_inc(*lnv.up())
                        act.wait_ge(*lnv.nth(1, turn))
                        nc.scalar.activation(rstd[:, :], lnr[:, :], ACT.Exp, scale=-0.5).then_inc(*rstd_ready.up())
                        for c, (_, m) in enumerate(FCH):
                            act.wait_ge(*hg_done.nth(c + 1, turn))
                            nc.scalar.activation(gl[0:m, c], gate_bank[c][0:m, :], ACT.Gelu, bias=par("b1", 3 + c)[0:m, :]).then_inc(*gelus.up())
                        for q in mine:
                            q.full()

            @block.tensor
            def _(pe):
                def proj(u, turn):
                    kind, g = unit[u]
                    if u == 0:
                        pe.wait_ge(*shifted.nth(2, turn))
                    else:
                        pe.wait_ge(*copied.nth(u, turn))
                        pe.wait_ge(*logs.nth(u, turn))
                    nc.tensor.matmul(PAB[:, 0, :], wqk(kind, g, 0), xs[:, :], start=True, stop=True)
                    nc.tensor.matmul(PAB[:, 1, :], wqk(kind, g, 1), xs[:, :], start=True, stop=True).then_inc(*projected.up())

                def sumsq(u, turn):
                    pe.wait_ge(*copied.nth(u + 1, turn))
                    nc.tensor.matmul(PAB[:, 0, :], ones_head, sq[:, 0, :], start=True, stop=False)
                    nc.tensor.matmul(PAB[:, 0, :], ones_head, sq[:, 1, :], start=False, stop=True).then_inc(*summed.up())

                def v_proj(i, turn):
                    if i >= 2:
                        pe.wait_ge(*v_copied.nth(i - 1, turn))
                    t, h = i // 2, i % 2
                    nc.tensor.matmul((PT, PX)[h][:, :], xs[:, t * TILE:(t + 1) * TILE],
                                               W[:, W_V + h * 512:W_V + h * 512 + 512], start=True, stop=True).then_inc(*v_done.up())

                def scores(n, turn):
                    g, t = n // 4, n % 4
                    if t == 0:
                        pe.wait_ge(*qk_ready.nth(2 * g + 2, turn))
                    if n >= 1:
                        pe.wait_ge(*exps.nth(n, turn))
                    lo = 0 if t else LOOK
                    k0 = t * TILE - LOOK + lo
                    for j in range(4):
                        nc.tensor.matmul(S[:, j, lo:BAND], const.identb, const.mask[:, lo:BAND], start=True, stop=False)
                    for half in range(2):
                        for j in range(4):
                            r = slice(32 * j, 32 * j + 32)
                            mm = nc.tensor.matmul(S[:, j, lo:BAND], QK[r, 0, g, half, t * TILE:(t + 1) * TILE],
                                                  QK[r, 1, g, half, k0:(t + 1) * TILE], start=False, stop=half == 1)
                    mm.then_inc(*s_done.up())

                def turn_probs(n, turn):
                    pe.wait_ge(*p_ready.nth(n + 1, turn))
                    if n >= 1:
                        pe.wait_ge(*pt_copied.nth(n, turn))
                        pe.wait_ge(*po_copied.nth(n, turn))
                    else:
                        pe.wait_ge(*v_copied.nth(8, turn))
                    for j in range(4):
                        mm = nc.tensor.transpose(PT[:, j * TILE:(j + 1) * TILE], Pb[:, n % 2, j, 128:], ident)
                    if n % 4:
                        for j in range(4):
                            mm = nc.tensor.transpose(PX[:, 256 + j * LOOK:256 + (j + 1) * LOOK], Pb[0:LOOK, n % 2, j, 0:128],
                                                     ident[0:LOOK, 0:LOOK])
                    mm.then_inc(*pt_done.up())

                def values(n, turn):
                    g, t = n // 4, n % 4
                    pe.wait_ge(*pt_copied.nth(n + 1, turn))
                    if t:
                        pe.wait_ge(*px_copied.nth(prevs(n), turn))
                    for j in range(4):
                        h = 4 * g + j
                        r = slice(64 * (j % 2), 64 * (j % 2) + 64)
                        c = (j // 2) * TILE
                        mm = nc.tensor.matmul(PX[r, c:c + TILE], V[:, t, h * DH:(h + 1) * DH], PTs[:, n % 2, j, :],
                                              start=True, stop=t == 0)
                        if t:
                            mm = nc.tensor.matmul(PX[r, c:c + LOOK], V[:, t - 1, h * DH:(h + 1) * DH], PT2s[:, n % 2, j, :],
                                                  start=False, stop=True)
                    mm.then_inc(*pv_done.up())

                with pe.Fori(0, depth) as l:
                    with pe.Fori(0, seqs) as s:
                        turn = l * seqs + s
                        pe.wait_ge(weights_in.sem, l * 16 + 16)
                        mine = (projected, summed, v_done, s_done, pt_done, pv_done, wo_done, mean_done, var_done, hg_done, w2_done)
                        for q in mine:
                            q.n = 0
                        proj(0, turn)
                        for i in range(4):
                            v_proj(i, turn)
                        sumsq(0, turn)
                        proj(1, turn)
                        for i in range(4, 8):
                            v_proj(i, turn)
                        sumsq(1, turn)
                        for n in range(NS + 1):
                            g = n // 4
                            if n < NS:
                                scores(n, turn)
                            if n >= 1:
                                turn_probs(n - 1, turn)
                            if n < 12 and n % 4 == 0:
                                proj(2 * g + 2, turn)
                            if n < 12 and n % 4 == 1:
                                sumsq(2 * g + 2, turn)
                            if n < 12 and n % 4 == 2:
                                proj(2 * g + 3, turn)
                            if n < 12 and n % 4 == 3:
                                sumsq(2 * g + 3, turn)
                            if n >= 1:
                                values(n - 1, turn)
                        pe.wait_ge(*po_copied.nth(NS, turn))
                        for p in range(HEADS // 2):
                            mm = nc.tensor.matmul(PT[:, :], W[:, W_O + p * P:W_O + (p + 1) * P], OT[:, p, :],
                                                  start=p == 0, stop=p == HEADS // 2 - 1)
                        mm.then_inc(*wo_done.up())
                        pe.wait_ge(*xs2_ready.nth(2, turn))
                        nc.tensor.matmul(PAB[:, 0, :], ones_mean, xs2[:, :], start=True, stop=True).then_inc(*mean_done.up())
                        pe.wait_ge(*squared.nth(1, turn))
                        nc.tensor.matmul(PAB[:, 1, :], ones_mean, csq[:, :], start=True, stop=True).then_inc(*var_done.up())
                        pe.wait_ge(*xn_ready.nth(1, turn))
                        for c, (f, m) in enumerate(FCH):
                            nc.tensor.matmul(gate_bank[c][0:m, :], W[:, W_1 + FF + f:W_1 + FF + f + m], xn[:, :], start=True, stop=True)
                            nc.tensor.matmul(val_bank[c][0:m, :], W[:, W_1 + f:W_1 + f + m], xn[:, :], start=True, stop=True).then_inc(*hg_done.up())
                        for c, (f, m) in enumerate(FCH):
                            pe.wait_ge(*h_ready.nth(c + 1, turn))
                            mm = nc.tensor.matmul(PT[:, :], W[0:m, W_2 + c * P:W_2 + (c + 1) * P], hh[0:m, c],
                                                  start=c == 0, stop=c == 2)
                        mm.then_inc(*w2_done.up())
                        for q in mine:
                            q.full()

            @block.vector
            def _(dve):
                def products(u, turn):
                    kind = unit[u][0]
                    dve.wait_ge(*copied.nth(u + 1, turn))
                    if u >= 1:
                        dve.wait_ge(*rotated.nth(2 * u, turn))
                    nc.vector.tensor_tensor(tc_[:, :, :], ab[:, u % 2], TC[:, kind], ALU.mult).then_inc(*prods.up())
                    nc.vector.tensor_tensor(ts_[:, :, :], ab[:, u % 2], TS[:, kind], ALU.mult).then_inc(*prods.up())

                def finish(u, turn):
                    kind, g = unit[u]
                    dve.wait_ge(*rotated.nth(2 * u + 2, turn))
                    dve.wait_ge(*rinvs.nth(u + 1, turn))
                    r = rinv[:, u % 2].unsqueeze(1).broadcast_to([P, 2, SEQ])
                    nc.vector.scalar_tensor_tensor(out=QK[:, kind, g], in0=r, scalar=1.0 / NORM_MIN,
                                                               in1=rot[:, u % 2], op0=ALU.min, op1=ALU.mult).then_inc(*qk_ready.up())

                def row_max(n, turn):
                    dve.wait_ge(*s_done.nth(n + 1, turn))
                    lo = 0 if n % 4 else LOOK
                    nc.vector.tensor_reduce(mx[:, n % 2], S[:, :, lo:BAND], AX.X, ALU.max).then_inc(*maxed.up())
                    dve.wait_ge(*maxed.nth(n + 1, turn))
                    if n >= 2:
                        dve.wait_ge(*exps.nth(n - 1, turn))
                    nc.vector.tensor_scalar(nb[:, n % 2], mx[:, n % 2], -QK_SCALE, None, ALU.mult).then_inc(*nb_ready.up())

                def inv_sum(n, turn):
                    dve.wait_ge(*exps.nth(n + 1, turn))
                    if n >= 2:
                        dve.wait_ge(*p_ready.nth(n - 1, turn))
                    nc.vector.reciprocal(rs[:, n % 2], sums[:, n % 2]).then_inc(*rs_ready.up())

                def pt_copy(n, turn):
                    dve.wait_ge(*pt_done.nth(n + 1, turn))
                    if n >= 2:
                        dve.wait_ge(*pv_done.nth(n - 1, turn))
                    nc.vector.tensor_copy(PTs[:, n % 2], PT[:, :].rearrange("p (j q) -> p j q", j=4)).then_inc(*pt_copied.up())

                nc.vector.memset(mx[:, :, :], 0.0).then_inc(*layer_done.prime())
                dve.wait_ge(base_in.sem, 16)
                dve.wait_ge(*zeroed.nth(2))
                with dve.Fori(0, depth) as l:
                    dve.wait_ge(weights_in.sem, l * 16 + 16)
                    for kind in range(2):
                        for half in range(2):
                            c = par("kA" if kind else "qA", half)
                            nc.vector.tensor_scalar(TC[:, kind, half], base[:, 2 * kind], c, None, ALU.mult).then_inc(*tables.up())
                            nc.vector.tensor_scalar(TS[:, kind, half], base[:, 2 * kind + 1], c, None, ALU.mult).then_inc(*tables.up())
                    with dve.Fori(0, seqs) as s:
                        turn = l * seqs + s
                        dve.wait_ge(*tables.nth(8, l))
                        mine = (layer_done, shifted, prods, qk_ready, maxed, nb_ready, rs_ready, pt_copied, x1_ready,
                                xs2_ready, centred, xnorm, xn_ready, h_ready)
                        for q in mine:
                            q.n = 0
                        src = xf[:, bass.ds(s * (SEQ + 1), SEQ + 1)]
                        nc.vector.tensor_copy(xs[0:64, :], src[0:64, 1:SEQ + 1]).then_inc(*shifted.up())
                        nc.vector.tensor_copy(xs[64:P, :], src[64:P, 0:SEQ]).then_inc(*shifted.up())
                        products(0, turn)
                        finish(0, turn)
                        products(1, turn)
                        finish(1, turn)
                        for n in range(NS + 1):
                            g = n // 4
                            if n < NS:
                                row_max(n, turn)
                            if n >= 1:
                                pt_copy(n - 1, turn)
                            if n < 12 and n % 4 == 0:
                                products(2 * g + 2, turn)
                            if n < NS:
                                inv_sum(n, turn)
                            if n < 12 and n % 4 == 1:
                                finish(2 * g + 2, turn)
                            if n < 12 and n % 4 == 2:
                                products(2 * g + 3, turn)
                            if n < 12 and n % 4 == 3:
                                finish(2 * g + 3, turn)
                        dve.wait_ge(*wo_done.nth(1, turn))
                        nc.vector.tensor_tensor(x1[:, 1:SEQ + 1], PT[:, :], src[:, 1:SEQ + 1], ALU.add).then_inc(*x1_ready.up())
                        dve.wait_ge(*x1_ready.nth(1, turn))
                        nc.vector.tensor_copy(xs2[0:64, :], x1[0:64, 1:SEQ + 1]).then_inc(*xs2_ready.up())
                        nc.vector.tensor_copy(xs2[64:P, :], x1[64:P, 0:SEQ]).then_inc(*xs2_ready.up())
                        dve.wait_ge(*mean_done.nth(1, turn))
                        nc.vector.tensor_tensor(cen[:, :], xs2[:, :], PAB[:, 0, :], ALU.subtract).then_inc(*centred.up())
                        dve.wait_ge(*rstd_ready.nth(1, turn))
                        nc.vector.tensor_tensor(xn[:, :], cen[:, :], rstd[:, :], ALU.mult).then_inc(*xnorm.up())
                        dve.wait_ge(*xnorm.nth(1, turn))
                        nc.vector.tensor_scalar(xn[:, :], xn[:, :], par("g"), par("b"), ALU.mult, ALU.add).then_inc(*xn_ready.up())
                        for c, (_, m) in enumerate(FCH):
                            dve.wait_ge(*gelus.nth(c + 1, turn))
                            nc.vector.scalar_tensor_tensor(out=hh[0:m, c], in0=val_bank[c][0:m, :], scalar=par("b1", c)[0:m, :],
                                                                      in1=gl[0:m, c], op0=ALU.add, op1=ALU.mult).then_inc(*h_ready.up())
                        dve.wait_ge(*w2_done.nth(1, turn))
                        nc.vector.scalar_tensor_tensor(out=src[:, 1:SEQ + 1], in0=PT[:, :], scalar=par("b2"),
                                                                     in1=x1[:, 1:SEQ + 1], op0=ALU.add, op1=ALU.add).then_inc(*layer_done.up())
                        dve.wait_ge(*layer_done.nth(1, turn))
                        for q in mine:
                            q.full()


A_Q = 0
A_K = A_Q + HEADS * 32
A_V = A_K + HEADS * 32
A_O = A_V + P
A_G = A_O + P
A_U = A_G + 512
A_D = A_U + 512
A_DOWN = A_D + 512
A_UP = A_DOWN + 512
A_WQT = A_UP + 512
A_KEYS = A_WQT + 512
A_BG = A_KEYS + 256
A_BU = A_BG + 4
A_BD = A_BU + 4
A_END = A_BD + 1
BIG = 1e30
TOP = 8
SPAN = {0: 0, 1: 512, 3: 896, 2: 1024}
SPANS = 1280


def level0(nc, x, w_dram, const, seqs):
    with ExitStack() as ctx:
        def sb(name, shape, dt=F32):
            return ctx.enter_context(nc.sbuf_tensor("a_" + name, shape, dt))

        def sig(name, per=0, primed=0):
            return Signal(ctx.enter_context(nc.semaphore("a_" + name)), per, primed)

        ident, ones_mean, ones_head, col = const.ident, const.mean, const.head, const.col
        W = sb("W", [P, A_END])
        Wsim = sb("Wsim", [P, 512])
        cen = sb("cen", [P, SEQ])
        csq = sb("csq", [P, SEQ])
        lnv_ = sb("lnv", [P, SEQ])
        rstd = sb("rstd", [P, SEQ])
        xn = sb("xn", [P, SEQ])
        QT = sb("QT", [P, 4, SEQ])
        KT = sb("KT", [P, 4, SEQ])
        V = sb("V", [P, TILES, HEADS, 9])
        AT = sb("AT", [P, 2, SPANS])
        sim = sb("sim", [P, TILES, 8, 64])
        sg = sb("sg", [P, TILES, 512])
        m8 = sb("m8", [P, 8, TOP])
        cand = sb("cand", [P, 4, TOP, TOP])
        c8 = sb("c8", [P, 4, TOP])
        nmax = sb("nmax", [P, 4])
        dlt = sb("dlt", [P, 4, TOP])
        ex8 = sb("ex8", [P, 4, TOP])
        Z = sb("Z", [P, 4])
        rZ = sb("rZ", [P, 4])
        penx = sb("penx", [P, 4, TOP])
        peny = sb("peny", [P, 4, 64])
        xm = sb("xm", [P, 4, TOP])
        ym = sb("ym", [P, 4, 64])
        D = sb("D", [P, 4, TOP, 64])
        E = sb("E", [P, 4, 512])
        pacc = sb("pacc", [P, 512])
        tot = sb("tot", [P, 1])
        rest = sb("rest", [P, 1])
        M = sb("M", [P, TILES, 512])
        MT = sb("MT", [P, 4, SEQ])
        den = sb("den", [P, TILES * HEADS])
        rden = sb("rden", [P, TILES * HEADS])
        o = sb("o", [P, TILES * HEADS, 8])
        oT = sb("oT", [P, SEQ])
        gs = sb("gs", [P, 4, SEQ])
        hT = sb("hT", [P, 4, SEQ])
        gate = sb("gate", [P, SEQ])
        sgate = sb("sgate", [P, SEQ])
        B = ctx.enter_context(nc.psum_tensor("a_B", [P, 8, 512], F32))

        PD = 31 * TILES
        w_in = sig("w_in")
        ones_set = sig("ones_set")
        folded = sig("folded")
        wsim_ready = sig("wsim_ready")
        out_done = sig("out_done", 1, 1)
        mean_done = sig("mean_done", 1)
        centred = sig("centred", 1)
        squared = sig("squared", 1)
        var_done = sig("var_done", 1)
        lnv = sig("lnv", 1)
        rstd_ready = sig("rstd_ready", 1)
        xn_ready = sig("xn_ready", 1)
        act_job = sig("act_job", 9)
        act_out = sig("act_out", 9)
        dve_job = sig("dve_job", 8)
        dve_out = sig("dve_out", 8)
        scored = sig("scored", HEADS)
        weighed = sig("weighed", HEADS)
        masked = sig("masked", 2 * HEADS)
        av_done = sig("av_done", HEADS)
        peer = sig("peer", PD)
        ex8_ready = sig("ex8_ready", TILES)
        e_ready = sig("e_ready", TILES)
        d_ready = sig("d_ready", TILES)
        dlt_ready = sig("dlt_ready", TILES)
        m_ready = sig("m_ready", TILES)
        den_ready = sig("den_ready", 2)
        rden_ready = sig("rden_ready", 1)
        o_ready = sig("o_ready", 2)
        gate_done = sig("gate_done", 4)
        gs_ready = sig("gs_ready", 4)
        up_done = sig("up_done", 4)
        h_ready = sig("h_ready", 4)
        oT_done = sig("oT_done", 1)
        oT_ready = sig("oT_ready", 1)
        s_done = sig("s_done", 1)
        mt_done = sig("mt_done", TILES)
        mt_ready = sig("mt_ready", TILES)
        ffn_done = sig("ffn_done", 1)
        gate_ready = sig("gate_ready", 1)
        gated = sig("gated", 1)

        jobs = []
        for b in range(4):
            jobs += [("act", "q", b), ("dve", "k", b)]
        jobs.append(("act", "v", 0))
        for t in range(TILES):
            jobs += [("dve", "sim", t), ("act", "down", t)]
        for_act = [j for j in jobs if j[0] == "act"]
        for_dve = [j for j in jobs if j[0] == "dve"]

        def bank(who, i):
            return B[:, (0 if who == "act" else 3) + i % 3, :]

        with nc.Block() as block:
            @block.sync
            def _(sp):
                sp.dma_start(W[:, :], w_dram).then_inc(w_in.sem, 16)

            @block.gpsimd
            def _(pool):
                nc.gpsimd.memset(V[:, :, :, :], 1.0).then_inc(*ones_set.up())
                both = const.tri.unsqueeze(1).broadcast_to([P, 2, P])
                with pool.Fori(0, seqs) as turn:
                    masked.n = 0
                    for h in range(HEADS):
                        pool.wait_ge(*weighed.nth(h + 1, turn))
                        a = AT[:, h % 2, 0:1024].rearrange("p (i t) -> p i t", i=2)[:, :, 0:P]
                        b = AT[:, h % 2, 896:1152].rearrange("p (i t) -> p i t", i=2)
                        nc.gpsimd.tensor_tensor(a, a, both, ALU.mult).then_inc(*masked.up())
                        nc.gpsimd.tensor_tensor(b, b, both, ALU.mult).then_inc(*masked.up())
                    masked.full()

            @block.scalar
            def _(act):
                nc.scalar.preload_act_table_set("natural_log_exp_and_others")
                act.wait_ge(*folded.nth(2))
                nc.scalar.activation(Wsim[:, 0:256], B[:, 0, 0:256], ACT.Copy).then_inc(*wsim_ready.up())
                nc.scalar.activation(Wsim[:, 256:512], B[:, 1, 0:256], ACT.Copy).then_inc(*wsim_ready.up())
                act.wait_ge(*ones_set.nth(1))

                def routing(t, turn):
                    act.wait_ge(*dlt_ready.nth(t + 1, turn))
                    nc.scalar.activation(ex8[:, :, :], dlt[:, :, :], ACT.Exp).then_inc(*ex8_ready.up())
                    act.wait_ge(*d_ready.nth(t + 1, turn))
                    for h in range(4):
                        mm = nc.scalar.activation(E[:, h, :], D[:, h].rearrange("p a b -> p (a b)"), ACT.Exp, bias=nmax[:, h:h + 1])
                    mm.then_inc(*e_ready.up())

                with act.Fori(0, seqs) as turn:
                    mine = (squared, lnv, rstd_ready, act_out, weighed, ex8_ready, e_ready, gs_ready, oT_ready, mt_ready, gate_ready)
                    for q in mine:
                        q.n = 0
                    act.wait_ge(*centred.nth(1, turn))
                    nc.scalar.activation(csq[:, :], cen[:, :], ACT.Square).then_inc(*squared.up())
                    act.wait_ge(*var_done.nth(1, turn))
                    nc.scalar.activation(lnv_[:, :], B[:, 7, :], ACT.Ln, bias=col["eps5"]).then_inc(*lnv.up())
                    act.wait_ge(*lnv.nth(1, turn))
                    nc.scalar.activation(rstd[:, :], lnv_[:, :], ACT.Exp, scale=-0.5).then_inc(*rstd_ready.up())
                    for i, (_, what, b) in enumerate(for_act):
                        act.wait_ge(*act_job.nth(i + 1, turn))
                        src = bank("act", i)
                        if what == "q":
                            nc.scalar.activation(QT[:, b, :], src, ACT.Copy).then_inc(*act_out.up())
                        elif what == "v":
                            nc.scalar.activation(V[:, :, :, 0:8].rearrange("p t h d -> p (t h) d"),
                                                            src.rearrange("p (a d) -> p a d", d=8), ACT.Copy).then_inc(*act_out.up())
                        else:
                            nc.scalar.activation(sg[:, b, :], src, ACT.Silu).then_inc(*act_out.up())
                    for h in range(HEADS):
                        act.wait_ge(*scored.nth(h + 1, turn))
                        if h >= 2:
                            act.wait_ge(*av_done.nth(h - 1, turn))
                        s = 3 * (h % 2)
                        nc.scalar.activation(AT[:, h % 2, :], B[:, s:s + 3, :].rearrange("p a b -> p (a b)")[:, 0:SPANS],
                                                        ACT.Square, scale=0.25).then_inc(*weighed.up())
                        if h % 4 == 3:
                            routing(h // 4, turn)
                    for c in range(4):
                        act.wait_ge(*gate_done.nth(c + 1, turn))
                        nc.scalar.activation(gs[:, c, :], B[:, c, :], ACT.Silu, bias=W[:, A_BG + c:A_BG + c + 1]).then_inc(*gs_ready.up())
                    act.wait_ge(*oT_done.nth(1, turn))
                    nc.scalar.activation(oT[:, :], B[:, 0, :], ACT.Copy).then_inc(*oT_ready.up())
                    for t in range(TILES):
                        act.wait_ge(*mt_done.nth(t + 1, turn))
                        nc.scalar.activation(MT[:, :, t * TILE:(t + 1) * TILE],
                                                         B[:, 6 + t % 2, :].rearrange("p (b t) -> p b t", b=4), ACT.Copy).then_inc(*mt_ready.up())
                    act.wait_ge(*ffn_done.nth(1, turn))
                    nc.scalar.activation(sgate[:, :], B[:, 2, :], ACT.Silu, bias=W[:, A_BD:A_BD + 1]).then_inc(*gate_ready.up())
                    for q in mine:
                        q.full()

            @block.tensor
            def _(pe):
                pe.wait_ge(w_in.sem, 16)
                for p in range(2):
                    r = slice(64 * p, 64 * p + 64)
                    for h in range(4):
                        mm = nc.tensor.matmul(B[:, p, h * 64:(h + 1) * 64], W[r, A_WQT + h * P:A_WQT + (h + 1) * P],
                                              W[r, A_KEYS + h * 64:A_KEYS + (h + 1) * 64], start=True, stop=True)
                    mm.then_inc(*folded.up())
                pe.wait_ge(*wsim_ready.nth(2))
                with pe.Fori(0, seqs) as turn:
                    mine = (mean_done, var_done, act_job, dve_job, scored, av_done, gate_done, up_done, oT_done, s_done, mt_done, ffn_done)
                    for q in mine:
                        q.n = 0
                    xin = x[:, bass.ds(turn * SEQ, SEQ)]
                    pe.wait_ge(*out_done.nth(0, turn))
                    nc.tensor.matmul(B[:, 6, :], ones_mean, xin, start=True, stop=True).then_inc(*mean_done.up())
                    pe.wait_ge(*squared.nth(1, turn))
                    nc.tensor.matmul(B[:, 7, :], ones_mean, csq[:, :], start=True, stop=True).then_inc(*var_done.up())
                    pe.wait_ge(*xn_ready.nth(1, turn))
                    n_act = n_dve = 0
                    for who, what, b in jobs:
                        if who == "act":
                            if n_act >= 3:
                                pe.wait_ge(*act_out.nth(n_act - 2, turn))
                            dst = bank(who, n_act)
                            n_act += 1
                        else:
                            if n_dve >= 3:
                                pe.wait_ge(*dve_out.nth(n_dve - 2, turn))
                            dst = bank(who, n_dve)
                            n_dve += 1
                        tok = slice(b * TILE, (b + 1) * TILE)
                        if what in "qk":
                            c = (A_Q if what == "q" else A_K) + b * P
                            mm = nc.tensor.matmul(dst, W[:, c:c + P], xn[:, :], start=True, stop=True)
                        elif what == "v":
                            for t in range(TILES):
                                mm = nc.tensor.matmul(dst[:, t * P:(t + 1) * P], xn[:, t * TILE:(t + 1) * TILE], W[:, A_V:A_V + P],
                                                      start=True, stop=True)
                        elif what == "sim":
                            mm = nc.tensor.matmul(dst, xn[:, tok], Wsim[:, :], start=True, stop=True)
                        else:
                            mm = nc.tensor.matmul(dst, xn[:, tok], W[:, A_DOWN:A_DOWN + 512], start=True, stop=True)
                        mm.then_inc(*(act_job if who == "act" else dve_job).up())

                    def head_scores(h):
                        if h < 2:
                            pe.wait_ge(*act_out.nth(9, turn))
                            pe.wait_ge(*dve_out.nth(8, turn))
                        else:
                            pe.wait_ge(*weighed.nth(h - 1, turn))
                        r = slice(32 * (h % 4), 32 * (h % 4) + 32)
                        flat = B[:, 3 * (h % 2):3 * (h % 2) + 3, :].rearrange("p a b -> p (a b)")
                        for i in range(TILES):
                            n = SEQ - i * TILE
                            mm = nc.tensor.matmul(flat[:, SPAN[i]:SPAN[i] + n], KT[r, h // 4, i * TILE:(i + 1) * TILE],
                                                  QT[r, h // 4, i * TILE:SEQ], start=True, stop=True)
                        mm.then_inc(*scored.up())

                    def head_values(h):
                        pe.wait_ge(*masked.nth(2 * h + 2, turn))
                        for t in range(TILES):
                            dst = B[:, 6 + t // 2, (t % 2) * 144 + h * 9:(t % 2) * 144 + h * 9 + 9]
                            for i in range(t + 1):
                                a = SPAN[i] + (t - i) * TILE
                                mm = nc.tensor.matmul(dst, AT[:, h % 2, a:a + TILE], V[:, i, h, :], start=i == 0, stop=i == t)
                        mm.then_inc(*av_done.up())

                    for h in range(HEADS):
                        head_scores(h)
                        if h:
                            head_values(h - 1)
                    head_values(HEADS - 1)
                    pe.wait_ge(*weighed.nth(HEADS, turn))
                    for c in range(4):
                        nc.tensor.matmul(B[:, c, :], W[:, A_G + c * P:A_G + (c + 1) * P], xn[:, :], start=True, stop=True).then_inc(*gate_done.up())
                    for c in range(4):
                        if c >= 2:
                            pe.wait_ge(*h_ready.nth(c - 1, turn))
                        nc.tensor.matmul(B[:, 4 + c % 2, :], W[:, A_U + c * P:A_U + (c + 1) * P], xn[:, :], start=True, stop=True).then_inc(*up_done.up())
                    pe.wait_ge(*o_ready.nth(2, turn))
                    pe.wait_ge(*gs_ready.nth(4, turn))
                    for t in range(TILES):
                        mm = nc.tensor.transpose(B[:, 0, t * TILE:(t + 1) * TILE],
                                                 o[:, t * HEADS:(t + 1) * HEADS, :].rearrange("p h d -> p (h d)"), ident)
                    mm.then_inc(*oT_done.up())
                    pe.wait_ge(*oT_ready.nth(1, turn))
                    nc.tensor.matmul(B[:, 1, :], W[:, A_O:A_O + P], oT[:, :], start=True, stop=True).then_inc(*s_done.up())
                    for t in range(TILES):
                        pe.wait_ge(*m_ready.nth(t + 1, turn))
                        if t >= 2:
                            pe.wait_ge(*mt_ready.nth(t - 1, turn))
                        for b in range(4):
                            mm = nc.tensor.transpose(B[:, 6 + t % 2, b * P:(b + 1) * P], M[:, t, b * P:(b + 1) * P], ident)
                        mm.then_inc(*mt_done.up())
                    pe.wait_ge(*h_ready.nth(4, turn))
                    for c in range(4):
                        nc.tensor.matmul(B[:, 2, :], W[:, A_D + c * P:A_D + (c + 1) * P], hT[:, c, :], start=c == 0, stop=False)
                    pe.wait_ge(*mt_ready.nth(4, turn))
                    for b in range(4):
                        mm = nc.tensor.matmul(B[:, 2, :], W[:, A_UP + b * P:A_UP + (b + 1) * P], MT[:, b, :], start=False, stop=b == 3)
                    mm.then_inc(*ffn_done.up())
                    for q in mine:
                        q.full()

            @block.vector
            def _(dve):
                def route(t, turn):
                    for g in range(8):
                        nc.vector.max(m8[:, g, :], sim[:, t, g, :]).then_inc(*peer.up())
                    dve.wait_ge(*peer.last(turn))
                    mx_, my_ = m8[:, 0:4, :], m8[:, 4:8, :]
                    nc.vector.tensor_tensor(cand[:, :, :, :], mx_.unsqueeze(3).broadcast_to([P, 4, TOP, TOP]),
                                                    my_.unsqueeze(2).broadcast_to([P, 4, TOP, TOP]), ALU.add).then_inc(*peer.up())
                    thx = m8[:, 0:4, 7:8].broadcast_to([P, 4, TOP])
                    thy = m8[:, 4:8, 7:8].broadcast_to([P, 4, 64])
                    nc.vector.tensor_tensor(penx[:, :, :], sim[:, t, 0:4, 0:TOP], thx, ALU.is_lt).then_inc(*peer.up())
                    nc.vector.tensor_tensor(peny[:, :, :], sim[:, t, 4:8, :], thy, ALU.is_lt).then_inc(*peer.up())
                    dve.wait_ge(*peer.last(turn))
                    nc.vector.scalar_tensor_tensor(out=xm[:, :, :], in0=penx[:, :, :], scalar=-BIG, in1=sim[:, t, 0:4, 0:TOP],
                                                           op0=ALU.mult, op1=ALU.add).then_inc(*peer.up())
                    nc.vector.scalar_tensor_tensor(out=ym[:, :, :], in0=peny[:, :, :], scalar=-BIG, in1=sim[:, t, 4:8, :],
                                                           op0=ALU.mult, op1=ALU.add).then_inc(*peer.up())
                    for h in range(4):
                        nc.vector.max(c8[:, h, :], cand[:, h].rearrange("p a b -> p (a b)")).then_inc(*peer.up())
                    dve.wait_ge(*peer.last(turn))
                    if t:
                        dve.wait_ge(*e_ready.nth(t, turn))
                    nc.vector.tensor_scalar(nmax[:, :], c8[:, :, 0], -1.0, None, ALU.mult).then_inc(*peer.up())
                    dve.wait_ge(*peer.last(turn))
                    nc.vector.tensor_tensor(dlt[:, :, :], c8[:, :, :], nmax[:, :].unsqueeze(2).broadcast_to([P, 4, TOP]), ALU.add).then_inc(*dlt_ready.up())
                    nc.vector.tensor_tensor(D[:, :, :, :], xm[:, :, :].unsqueeze(3).broadcast_to([P, 4, TOP, 64]),
                                                       ym[:, :, :].unsqueeze(2).broadcast_to([P, 4, TOP, 64]), ALU.add).then_inc(*d_ready.up())
                    dve.wait_ge(*ex8_ready.nth(t + 1, turn))
                    nc.vector.tensor_reduce(Z[:, :], ex8[:, :, :], AX.X, ALU.add).then_inc(*peer.up())
                    dve.wait_ge(*peer.last(turn))
                    nc.vector.reciprocal(rZ[:, :], Z[:, :]).then_inc(*peer.up())
                    dve.wait_ge(*e_ready.nth(t + 1, turn))
                    for h in range(4):
                        mm = nc.vector.scalar_tensor_tensor(out=E[:, h, :], in0=D[:, h].rearrange("p a b -> p (a b)"), scalar=c8[:, h, 7:8],
                                                            in1=E[:, h, :], op0=ALU.is_ge, op1=ALU.mult)
                        mm.then_inc(*peer.up())
                    dve.wait_ge(*peer.last(turn))
                    nc.vector.tensor_scalar(pacc[:, :], E[:, 0, :], rZ[:, 0:1], None, ALU.mult).then_inc(*peer.up())
                    for h in range(1, 4):
                        dve.wait_ge(*peer.last(turn))
                        nc.vector.scalar_tensor_tensor(out=pacc[:, :], in0=E[:, h, :], scalar=rZ[:, h:h + 1], in1=pacc[:, :],
                                                               op0=ALU.mult, op1=ALU.add).then_inc(*peer.up())
                    dve.wait_ge(*peer.last(turn))
                    nc.vector.tensor_reduce(tot[:, :], pacc[:, :], AX.X, ALU.add).then_inc(*peer.up())
                    dve.wait_ge(*peer.last(turn))
                    nc.vector.tensor_scalar(rest[:, :], tot[:, :], -1.0, 4.0, ALU.mult, ALU.add).then_inc(*peer.up())
                    dve.wait_ge(*peer.last(turn))
                    nc.vector.tensor_tensor(pacc[:, 511:512], pacc[:, 511:512], rest[:, :], ALU.add).then_inc(*peer.up())
                    dve.wait_ge(*peer.last(turn))
                    nc.vector.tensor_tensor(M[:, t, :], pacc[:, :], sg[:, t, :], ALU.mult).then_inc(*m_ready.up())

                nc.vector.memset(tot[:, :], 0.0).then_inc(*out_done.prime())
                with dve.Fori(0, seqs) as turn:
                    mine = (centred, xn_ready, dve_out, d_ready, dlt_ready, m_ready, den_ready, rden_ready, o_ready, h_ready, gated, out_done)
                    for q in mine + (peer,):
                        q.n = 0
                    xin = x[:, bass.ds(turn * SEQ, SEQ)]
                    dve.wait_ge(*mean_done.nth(1, turn))
                    nc.vector.tensor_tensor(cen[:, :], xin, B[:, 6, :], ALU.subtract).then_inc(*centred.up())
                    dve.wait_ge(*rstd_ready.nth(1, turn))
                    nc.vector.tensor_tensor(xn[:, :], cen[:, :], rstd[:, :], ALU.mult).then_inc(*xn_ready.up())
                    for i, (_, what, b) in enumerate(for_dve):
                        dve.wait_ge(*dve_job.nth(i + 1, turn))
                        dst = KT[:, b, :] if what == "k" else sim[:, b].rearrange("p g k -> p (g k)")
                        nc.vector.tensor_copy(dst, bank("dve", i)).then_inc(*dve_out.up())
                    dve.wait_ge(*dve_out.nth(8, turn))
                    dve.wait_ge(*act_out.nth(9, turn))
                    nc.vector.memset(tot[:, :], 0.0)
                    for t in range(TILES):
                        route(t, turn)
                    dve.wait_ge(*av_done.nth(HEADS, turn))
                    O = [B[:, 6 + b, 0:288].rearrange("p (a d) -> p a d", d=9) for b in range(2)]
                    for b in range(2):
                        nc.vector.tensor_scalar(den[:, 32 * b:32 * b + 32], O[b][:, :, 8], 1e-5, None, ALU.add).then_inc(*den_ready.up())
                    dve.wait_ge(*den_ready.nth(2, turn))
                    nc.vector.reciprocal(rden[:, :], den[:, :]).then_inc(*rden_ready.up())
                    dve.wait_ge(*rden_ready.nth(1, turn))
                    for b in range(2):
                        nc.vector.tensor_tensor(o[:, 32 * b:32 * b + 32, :], O[b][:, :, 0:8],
                                                           rden[:, 32 * b:32 * b + 32].unsqueeze(2).broadcast_to([P, 32, 8]), ALU.mult).then_inc(*o_ready.up())
                    for c in range(4):
                        dve.wait_ge(*up_done.nth(c + 1, turn))
                        dve.wait_ge(*gs_ready.nth(c + 1, turn))
                        nc.vector.scalar_tensor_tensor(out=hT[:, c, :], in0=B[:, 4 + c % 2, :], scalar=W[:, A_BU + c:A_BU + c + 1],
                                                                  in1=gs[:, c, :], op0=ALU.add, op1=ALU.mult).then_inc(*h_ready.up())
                    dve.wait_ge(*gate_ready.nth(1, turn))
                    nc.vector.tensor_tensor(gate[:, :], B[:, 1, :], sgate[:, :], ALU.mult).then_inc(*gated.up())
                    dve.wait_ge(*gated.nth(1, turn))
                    nc.vector.tensor_tensor(xin, xin, gate[:, :], ALU.add).then_inc(*out_done.up())
                    for q in mine:
                        q.full()
                    peer.full()


STATES, EXPERTS, HID = 64, 4, 512
B_IN = 0
B_DT = B_IN + 512
B_BP = B_DT + 2 * STATES
B_CP = B_BP + 2 * STATES
B_OUT = B_CP + 2 * STATES
B_GW = B_OUT + 2 * P
B_W1 = B_GW + EXPERTS
B_W2 = B_W1 + EXPERTS * HID
B_S2I = B_W2 + EXPERTS * 4 * P
B_B2 = B_S2I + 2 * P
B_GB = B_B2 + P
B_LT = B_GB + TILES * EXPERTS
B_SEL = B_LT + TILES * EXPERTS * EXPERTS
B_P = B_SEL + EXPERTS * P
BP = {"inb": 0, "conv": 4, "convb": 10, "dtb": 12, "bpb": 13, "cpb": 14, "s2ib": 15, "D": 17, "outb": 19, "n1": 20, "n2": 21, "b1": 22}
B_END = B_P + 22 + EXPERTS * 4


def level1(nc, x, xf, s1, w_dram, const, seqs):
    with ExitStack() as ctx:
        def sb(name, shape, dt=F32):
            return ctx.enter_context(nc.sbuf_tensor("b_" + name, shape, dt))

        def sig(name, per=0, primed=0):
            return Signal(ctx.enter_context(nc.semaphore("b_" + name)), per, primed)

        ident, ones_mean, ones_head, col = const.ident, const.mean, const.head, const.col
        T = [P, SEQ]
        W = sb("W", [P, B_END])
        cen, csq, lns, rstd, xn, nr, h1 = (sb(n, T) for n in ("cen", "csq", "lns", "rstd", "xn", "nr", "h1"))
        xc = sb("xc", [P, 2, 2 + SEQ])
        ca = sb("ca", [P, 2, SEQ])
        cb = sb("cb", [P, 2, SEQ])
        sgt = sb("sgt", [P, 2, SEQ])
        xm = sb("xm", [P, 2, SEQ])
        S = [STATES, SEQ]
        dt_, omd, db, st, y, yc, ysq, yln, yrs, yn = (sb(n, S) for n in ("dt", "omd", "db", "st", "y", "yc", "ysq", "yln", "yrs", "yn"))
        u1 = sb("u1", [P, 2, SEQ])
        u2 = sb("u2", [P, 2, SEQ])
        x2, x2sq, nr2, h2 = (sb(n, T) for n in ("x2", "x2sq", "nr2", "h2"))
        TE = TILES * EXPERTS
        lg, ls, ex, exs, rank, sel, wt = (sb(n, [P, TE]) for n in ("lg", "ls", "ex", "exs", "rank", "sel", "wt"))
        mxl, zz, rz = (sb(n, [P, TILES]) for n in ("mxl", "zz", "rz"))
        gt, eq = (sb(n, [P, TE, EXPERTS]) for n in ("gt", "eq"))
        wT = sb("wT", [EXPERTS, SEQ])
        spare = sb("spare", [P, 1])
        gl = sb("gl", [P, 3, SEQ])
        wb = sb("wb", [P, EXPERTS, SEQ])
        hw = sb("hw", [P, 3, SEQ])
        B = ctx.enter_context(nc.psum_tensor("b_B", [P, 8, 512], F32))

        def par(name, k=0, rows=P):
            c = B_P + BP[name] + k
            return W[0:rows, c:c + 1]

        NK = EXPERTS * 4
        w_in = sig("w_in")
        zeroed = sig("zeroed")
        out_done = sig("out_done", 1, 1)
        sums = sig("sums", 6)
        sq_ready = sig("sq_ready", 4)
        lnd = sig("lnd", 4)
        inv = sig("inv", 4)
        cen_ready = sig("cen_ready", 2)
        xn_ready = sig("xn_ready", 1)
        xf_ready = sig("xf_ready", 1, 1)
        n_ready = sig("n_ready", 4)
        in_done = sig("in_done", 4)
        xc_ready = sig("xc_ready", 2)
        gates = sig("gates", 2)
        conv = sig("conv", 6)
        xm_ready = sig("xm_ready", 2)
        dbc = sig("dbc", 3)
        dt_ready = sig("dt_ready", 1)
        ssm = sig("ssm", 5)
        s2i = sig("s2i", 2)
        u_ready = sig("u_ready", 4)
        out_p = sig("out_p", 1)
        x2_ready = sig("x2_ready", 1)
        logits = sig("logits", 1)
        ls_ready = sig("ls_ready", 1)
        route = sig("route", 10)
        ex_ready = sig("ex_ready", 1)
        wt_done = sig("wt_done", 1)
        wT_ready = sig("wT_ready", 1)
        wb_done = sig("wb_done", EXPERTS)
        wb_ready = sig("wb_ready", EXPERTS)
        hid = sig("hid", NK)
        gelus = sig("gelus", NK)
        hw_ready = sig("hw_ready", NK)
        eo_used = sig("eo_used", NK)
        step = sig("step", 1)

        with nc.Block() as block:
            @block.sync
            def _(sp):
                sp.dma_start(W[:, :], w_dram).then_inc(w_in.sem, 16)

            @block.gpsimd
            def _(pool):
                nc.gpsimd.memset(xc[:, :, 0:2], 0.0).then_inc(*zeroed.up())
                nc.gpsimd.memset(spare[:, :], 0.0).then_inc(*xf_ready.prime())
                nc.gpsimd.memset(xf[:, :].rearrange("p (s t) -> p s t", s=seqs)[:, :, 0:1], 0.0).then_inc(*zeroed.up())
                with pool.Fori(0, seqs) as turn:
                    xf_ready.n = 0
                    pool.wait_ge(*xn_ready.nth(1, turn))
                    nc.gpsimd.tensor_copy(xf[:, bass.ds(turn * (SEQ + 1) + 1, SEQ)], xn[:, :]).then_inc(*xf_ready.up())
                    xf_ready.full()

            @block.scalar
            def _(act):
                nc.scalar.preload_act_table_set("natural_log_exp_and_others")
                act.wait_ge(w_in.sem, 16)
                with act.Fori(0, seqs) as turn:
                    mine = (sq_ready, lnd, inv, gates, xm_ready, dt_ready, ex_ready, gelus)
                    for q in mine:
                        q.n = 0

                    def inverse_root(out, ln_out, src, eps, n):
                        act.wait_ge(*sums.nth(n, turn))
                        nc.scalar.activation(ln_out, src, ACT.Ln, bias=eps).then_inc(*lnd.up())
                        act.wait_ge(*lnd.last(turn))
                        nc.scalar.activation(out, ln_out, ACT.Exp, scale=-0.5).then_inc(*inv.up())

                    act.wait_ge(*cen_ready.nth(1, turn))
                    nc.scalar.activation(csq[:, :], cen[:, :], ACT.Square).then_inc(*sq_ready.up())
                    inverse_root(rstd[:, :], lns[:, :], B[:, 1, :], col["eps5"], 2)
                    act.wait_ge(*xn_ready.nth(1, turn))
                    nc.scalar.activation(csq[:, :], xn[:, :], ACT.Square).then_inc(*sq_ready.up())
                    act.wait_ge(*inv.nth(1, turn))
                    inverse_root(nr[:, :], lns[:, :], B[:, 2, :], col["eps6"], 3)
                    for b in range(2):
                        act.wait_ge(*in_done.nth(3 + b, turn))
                        nc.scalar.activation(sgt[:, b, :], B[:, 5 + b, :], ACT.Sigmoid, bias=par("inb", 2 + b)).then_inc(*gates.up())
                    for b in range(2):
                        act.wait_ge(*conv.nth(3 * b + 3, turn))
                        nc.scalar.activation(xm[:, b, :], ca[:, b, :], ACT.Silu, bias=par("convb", b)).then_inc(*xm_ready.up())
                    act.wait_ge(*dbc.nth(1, turn))
                    nc.scalar.activation(dt_[:, :], B[0:STATES, 0, :], ACT.Sigmoid, bias=par("dtb", 0, STATES)).then_inc(*dt_ready.up())
                    act.wait_ge(*cen_ready.nth(2, turn))
                    nc.scalar.activation(ysq[:, :], yc[:, :], ACT.Square).then_inc(*sq_ready.up())
                    inverse_root(yrs[:, :], yln[:, :], B[0:STATES, 4, :], col["eps5"][0:STATES, :], 5)
                    act.wait_ge(*x2_ready.nth(1, turn))
                    nc.scalar.activation(x2sq[:, :], x2[:, :], ACT.Square).then_inc(*sq_ready.up())
                    inverse_root(nr2[:, :], lns[:, :], B[:, 0, :], col["eps6"], 6)
                    act.wait_ge(*ls_ready.nth(1, turn))
                    nc.scalar.activation(ex[:, :], ls[:, :], ACT.Exp).then_inc(*ex_ready.up())
                    for k in range(NK):
                        act.wait_ge(*hid.nth(k + 1, turn))
                        if k >= 3:
                            act.wait_ge(*hw_ready.nth(k - 2, turn))
                        nc.scalar.activation(gl[:, k % 3, :], B[:, k % 3, :], ACT.Gelu, bias=par("b1", k)).then_inc(*gelus.up())
                    for q in mine:
                        q.full()

            @block.tensor
            def _(pe):
                pe.wait_ge(w_in.sem, 16)
                with pe.Fori(0, seqs) as turn:
                    mine = (sums, in_done, dbc, s2i, out_p, logits, wt_done, wb_done, hid, eo_used)
                    for q in mine:
                        q.n = 0
                    mean_s = const.mean64
                    pe.wait_ge(*out_done.nth(0, turn))
                    nc.tensor.matmul(B[:, 0, :], ones_mean, x[:, bass.ds(turn * SEQ, SEQ)], start=True, stop=True).then_inc(*sums.up())
                    pe.wait_ge(*sq_ready.nth(1, turn))
                    nc.tensor.matmul(B[:, 1, :], ones_mean, csq[:, :], start=True, stop=True).then_inc(*sums.up())
                    pe.wait_ge(*sq_ready.nth(2, turn))
                    nc.tensor.matmul(B[:, 2, :], ones_mean, csq[:, :], start=True, stop=True).then_inc(*sums.up())
                    pe.wait_ge(*n_ready.nth(2, turn))
                    for b in range(4):
                        nc.tensor.matmul(B[:, 3 + b, :], W[:, B_IN + b * P:B_IN + (b + 1) * P], h1[:, :], start=True, stop=True).then_inc(*in_done.up())
                    pe.wait_ge(*xm_ready.nth(2, turn))
                    for i, c in enumerate((B_DT, B_BP, B_CP)):
                        for b in range(2):
                            mm = nc.tensor.matmul(B[0:STATES, i, :], W[:, c + b * STATES:c + (b + 1) * STATES], xm[:, b, :], start=b == 0, stop=b == 1)
                        mm.then_inc(*dbc.up())
                    pe.wait_ge(*ssm.nth(4, turn))
                    nc.tensor.matmul(B[:, 3, :], mean_s, y[:, :], start=True, stop=True).then_inc(*sums.up())
                    pe.wait_ge(*sq_ready.nth(3, turn))
                    nc.tensor.matmul(B[:, 4, :], mean_s, ysq[:, :], start=True, stop=True).then_inc(*sums.up())
                    pe.wait_ge(*ssm.nth(5, turn))
                    for b in range(2):
                        nc.tensor.matmul(B[:, 5 + b, :], W[0:STATES, B_S2I + b * P:B_S2I + (b + 1) * P], yn[:, :], start=True, stop=True).then_inc(*s2i.up())
                    pe.wait_ge(*u_ready.nth(4, turn))
                    for b in range(2):
                        mm = nc.tensor.matmul(B[:, 7, :], W[:, B_OUT + b * P:B_OUT + (b + 1) * P], u2[:, b, :], start=b == 0, stop=b == 1)
                    mm.then_inc(*out_p.up())
                    pe.wait_ge(*sq_ready.nth(4, turn))
                    nc.tensor.matmul(B[:, 0, :], ones_mean, x2sq[:, :], start=True, stop=True).then_inc(*sums.up())
                    pe.wait_ge(*n_ready.nth(4, turn))
                    for t in range(TILES):
                        mm = nc.tensor.matmul(B[:, 1, t * EXPERTS:(t + 1) * EXPERTS], h2[:, t * TILE:(t + 1) * TILE], W[:, B_GW:B_GW + EXPERTS],
                                              start=True, stop=True)
                    mm.then_inc(*logits.up())
                    pe.wait_ge(*route.nth(10, turn))
                    for t in range(TILES):
                        mm = nc.tensor.transpose(B[0:EXPERTS, 2, t * TILE:(t + 1) * TILE], wt[:, t * EXPERTS:(t + 1) * EXPERTS], ident)
                    mm.then_inc(*wt_done.up())
                    pe.wait_ge(*wT_ready.nth(1, turn))
                    nc.tensor.matmul(B[:, 7, :], W[0:EXPERTS, B_B2:B_B2 + P], wT[:, :], start=True, stop=False, skip_group_check=True)
                    for e in range(EXPERTS):
                        nc.tensor.matmul(B[:, 3 + e, :], W[0:EXPERTS, B_SEL + e * P:B_SEL + (e + 1) * P], wT[:, :], start=True, stop=True).then_inc(*wb_done.up())

                    def result(k):
                        pe.wait_ge(*hw_ready.nth(k + 1, turn))
                        nc.tensor.matmul(B[:, 7, :], W[:, B_W2 + k * P:B_W2 + (k + 1) * P], hw[:, k % 3, :],
                                                    start=False, stop=k == NK - 1, skip_group_check=True).then_inc(*eo_used.up())

                    for k in range(NK):
                        if k >= 3:
                            pe.wait_ge(*gelus.nth(k - 2, turn))
                        nc.tensor.matmul(B[:, k % 3, :], W[:, B_W1 + k * P:B_W1 + (k + 1) * P], h2[:, :], start=True, stop=True).then_inc(*hid.up())
                        if k >= 2:
                            result(k - 2)
                    result(NK - 2)
                    result(NK - 1)
                    for q in mine:
                        q.full()

            @block.vector
            def _(dve):
                nc.vector.memset(rz[:, :], 0.0).then_inc(*out_done.prime())
                dve.wait_ge(w_in.sem, 16)
                dve.wait_ge(*zeroed.nth(2))
                TT, STT, TSC = nc.vector.tensor_tensor, nc.vector.scalar_tensor_tensor, nc.vector.tensor_scalar
                with dve.Fori(0, seqs) as turn:
                    mine = (cen_ready, xn_ready, n_ready, xc_ready, conv, ssm, u_ready, x2_ready, ls_ready, route, wT_ready, wb_ready,
                            hw_ready, out_done)
                    for q in mine:
                        q.n = 0
                    dve.wait_ge(*sums.nth(1, turn))
                    TT(cen[:, :], x[:, bass.ds(turn * SEQ, SEQ)], B[:, 0, :], ALU.subtract).then_inc(*cen_ready.up())
                    dve.wait_ge(*inv.nth(1, turn))
                    dve.wait_ge(*xf_ready.nth(0, turn))
                    TT(xn[:, :], cen[:, :], rstd[:, :], ALU.mult).then_inc(*xn_ready.up())
                    dve.wait_ge(*xn_ready.nth(1, turn))
                    TSC(h1[:, :], xn[:, :], par("n1"), None, ALU.mult).then_inc(*n_ready.up())
                    dve.wait_ge(*n_ready.nth(1, turn))
                    dve.wait_ge(*inv.nth(2, turn))
                    TT(h1[:, :], h1[:, :], nr[:, :], ALU.mult).then_inc(*n_ready.up())
                    for b in range(2):
                        dve.wait_ge(*in_done.nth(b + 1, turn))
                        TSC(xc[:, b, 2:], B[:, 3 + b, :], par("inb", b), None, ALU.add).then_inc(*xc_ready.up())
                    for b in range(2):
                        dve.wait_ge(*xc_ready.nth(b + 1, turn))
                        TSC(ca[:, b, :], xc[:, b, 2:], par("conv", 3 * b + 2), None, ALU.mult).then_inc(*conv.up())
                        dve.wait_ge(*conv.last(turn))
                        STT(out=cb[:, b, :], in0=xc[:, b, 1:1 + SEQ], scalar=par("conv", 3 * b + 1), in1=ca[:, b, :], op0=ALU.mult, op1=ALU.add).then_inc(*conv.up())
                        dve.wait_ge(*conv.last(turn))
                        STT(out=ca[:, b, :], in0=xc[:, b, 0:SEQ], scalar=par("conv", 3 * b), in1=cb[:, b, :], op0=ALU.mult, op1=ALU.add).then_inc(*conv.up())
                    dve.wait_ge(*dt_ready.nth(1, turn))
                    TSC(omd[:, :], dt_[:, :], -1.0, 1.0, ALU.mult, ALU.add).then_inc(*ssm.up())
                    dve.wait_ge(*dbc.nth(3, turn))
                    STT(out=db[:, :], in0=B[0:STATES, 1, :], scalar=par("bpb", 0, STATES), in1=dt_[:, :], op0=ALU.add, op1=ALU.mult).then_inc(*ssm.up())
                    dve.wait_ge(*ssm.last(turn))
                    nc.vector.tensor_tensor_scan(st[:, :], omd[:, :], db[:, :], 0.0, ALU.mult, ALU.add).then_inc(*ssm.up())
                    dve.wait_ge(*ssm.last(turn))
                    STT(out=y[:, :], in0=B[0:STATES, 2, :], scalar=par("cpb", 0, STATES), in1=st[:, :], op0=ALU.add, op1=ALU.mult).then_inc(*ssm.up())
                    dve.wait_ge(*ssm.last(turn))
                    dve.wait_ge(*sums.nth(4, turn))
                    TT(yc[:, :], y[:, :], B[0:STATES, 3, :], ALU.subtract).then_inc(*cen_ready.up())
                    dve.wait_ge(*cen_ready.nth(2, turn))
                    dve.wait_ge(*inv.nth(3, turn))
                    TT(yn[:, :], yc[:, :], yrs[:, :], ALU.mult).then_inc(*ssm.up())
                    for b in range(2):
                        dve.wait_ge(*s2i.nth(b + 1, turn))
                        dve.wait_ge(*gates.nth(b + 1, turn))
                        STT(out=u1[:, b, :], in0=xm[:, b, :], scalar=par("D", b), in1=B[:, 5 + b, :], op0=ALU.mult, op1=ALU.add).then_inc(*u_ready.up())
                        dve.wait_ge(*u_ready.last(turn))
                        STT(out=u2[:, b, :], in0=u1[:, b, :], scalar=par("s2ib", b), in1=sgt[:, b, :], op0=ALU.add, op1=ALU.mult).then_inc(*u_ready.up())
                    dve.wait_ge(*out_p.nth(1, turn))
                    STT(out=x2[:, :], in0=B[:, 7, :], scalar=par("outb"), in1=xn[:, :], op0=ALU.add, op1=ALU.add).then_inc(*x2_ready.up())
                    dve.wait_ge(*x2_ready.nth(1, turn))
                    TSC(h2[:, :], x2[:, :], par("n2"), None, ALU.mult).then_inc(*n_ready.up())
                    dve.wait_ge(*n_ready.nth(3, turn))
                    dve.wait_ge(*inv.nth(4, turn))
                    TT(h2[:, :], h2[:, :], nr2[:, :], ALU.mult).then_inc(*n_ready.up())
                    dve.wait_ge(*logits.nth(1, turn))
                    TT(lg[:, :], B[:, 1, 0:TE], W[:, B_GB:B_GB + TE], ALU.add).then_inc(*route.up())
                    dve.wait_ge(*route.last(turn))
                    lt = lg[:, :].rearrange("p (t e) -> p t e", t=TILES)
                    for t in range(TILES):
                        other = lg[:, t * EXPERTS:(t + 1) * EXPERTS].unsqueeze(1).broadcast_to([P, EXPERTS, EXPERTS])
                        own = lg[:, t * EXPERTS:(t + 1) * EXPERTS].unsqueeze(2).broadcast_to([P, EXPERTS, EXPERTS])
                        rows = slice(t * EXPERTS, (t + 1) * EXPERTS)
                        nc.vector.tensor_tensor(gt[:, rows, :], other, own, ALU.is_gt)
                        mm = nc.vector.tensor_tensor(eq[:, rows, :], other, own, ALU.is_equal)
                    mm.then_inc(*route.up())
                    nc.vector.tensor_reduce(mxl[:, :], lt, AX.X, ALU.max).then_inc(*route.up())
                    dve.wait_ge(*route.last(turn))
                    TT(ls[:, :].rearrange("p (t e) -> p t e", t=TILES), lt, mxl[:, :].unsqueeze(2).broadcast_to([P, TILES, EXPERTS]), ALU.subtract).then_inc(*ls_ready.up())
                    flat = lambda a: a.rearrange("p a b -> p (a b)")
                    TT(flat(eq[:, :, :]), flat(eq[:, :, :]), W[:, B_LT:B_LT + TE * EXPERTS], ALU.mult).then_inc(*route.up())
                    dve.wait_ge(*route.last(turn))
                    TT(flat(gt[:, :, :]), flat(gt[:, :, :]), flat(eq[:, :, :]), ALU.add).then_inc(*route.up())
                    dve.wait_ge(*route.last(turn))
                    nc.vector.tensor_reduce(rank[:, :], gt[:, :, :], AX.X, ALU.add).then_inc(*route.up())
                    dve.wait_ge(*route.last(turn))
                    dve.wait_ge(*ex_ready.nth(1, turn))
                    STT(out=exs[:, :], in0=rank[:, :], scalar=2.0, in1=ex[:, :], op0=ALU.is_lt, op1=ALU.mult).then_inc(*route.up())
                    dve.wait_ge(*route.last(turn))
                    nc.vector.tensor_reduce(zz[:, :], exs[:, :].rearrange("p (t e) -> p t e", t=TILES), AX.X, ALU.add).then_inc(*route.up())
                    dve.wait_ge(*route.last(turn))
                    nc.vector.reciprocal(rz[:, :], zz[:, :]).then_inc(*route.up())
                    dve.wait_ge(*route.last(turn))
                    TT(wt[:, :].rearrange("p (t e) -> p t e", t=TILES), exs[:, :].rearrange("p (t e) -> p t e", t=TILES),
                                rz[:, :].unsqueeze(2).broadcast_to([P, TILES, EXPERTS]), ALU.mult).then_inc(*route.up())
                    dve.wait_ge(*wt_done.nth(1, turn))
                    nc.vector.tensor_copy(wT[:, :], B[0:EXPERTS, 2, :]).then_inc(*wT_ready.up())
                    for e in range(EXPERTS):
                        dve.wait_ge(*wb_done.nth(e + 1, turn))
                        nc.vector.tensor_copy(wb[:, e, :], B[:, 3 + e, :]).then_inc(*wb_ready.up())
                    dve.wait_ge(*wb_ready.nth(EXPERTS, turn))
                    for k in range(NK):
                        dve.wait_ge(*gelus.nth(k + 1, turn))
                        if k >= 3:
                            dve.wait_ge(*eo_used.nth(k - 2, turn))
                        TT(hw[:, k % 3, :], gl[:, k % 3, :], wb[:, k // 4, :], ALU.mult).then_inc(*hw_ready.up())
                    dve.wait_ge(*eo_used.nth(NK, turn))
                    TT(s1[:, bass.ds(turn * SEQ, SEQ)], x2[:, :], B[:, 7, :], ALU.add).then_inc(*out_done.up())
                    for q in mine:
                        q.full()


C_ID, C_MEAN, C_HEAD, C_M64, C_TRI, C_MASK = (i * P for i in range(6))
C_COL = C_MASK + BAND
COLS = {"tiny": 2.0 ** -64, "shift": LN_SHIFT / 2 * float(np.log(2.0)), "eps5": 1e-5, "eps6": 1e-6}
C_END = C_COL + len(COLS)


class Constants:
    def __init__(self, c32, c16):
        self.ident = c32[:, C_ID:C_ID + P]
        self.mean = c32[:, C_MEAN:C_MEAN + P]
        self.head = c32[:, C_HEAD:C_HEAD + P]
        self.mean64 = c32[0:STATES, C_M64:C_M64 + P]
        self.tri = c32[:, C_TRI:C_TRI + P]
        self.col = {n: c32[:, C_COL + i:C_COL + i + 1] for i, n in enumerate(COLS)}
        self.identb = c16[:, 0:P]
        self.mask = c16[:, P:P + BAND]


def keep(nc, pairs):
    with ExitStack() as ctx:
        stored = ctx.enter_context(nc.semaphore("kept"))
        with nc.Block() as block:
            @block.sync
            def _(sp):
                for dram, sbuf in pairs:
                    sp.dma_start(dram, sbuf).then_inc(stored, 16)
                sp.wait_ge(stored, 16 * len(pairs))


def result(nc, x_kept, s1_kept, xf, out_dram, seqs):
    with ExitStack() as ctx:
        def sb(name):
            return ctx.enter_context(nc.sbuf_tensor("d_" + name, [P, seqs * SEQ], F32))

        def sig(name):
            return Signal(ctx.enter_context(nc.semaphore("d_" + name)))

        x, s1, g = sb("x"), sb("s1"), sb("g")
        loads = [ctx.enter_context(nc.semaphore(f"d_load{i}")) for i in range(seqs)]
        gates, prod, total, stored = sig("silu"), sig("product"), sig("total"), sig("stored")
        part = [slice(i * SEQ, (i + 1) * SEQ) for i in range(seqs)]
        with nc.Block() as block:
            @block.scalar
            def _(act):
                for i in range(seqs):
                    f = xf[:, i * (SEQ + 1) + 1:(i + 1) * (SEQ + 1)]
                    nc.scalar.activation(g[:, part[i]], f, ACT.Silu).then_inc(*gates.up())

            @block.vector
            def _(dve):
                for i in range(seqs):
                    dve.wait_ge(*gates.nth(i + 1))
                    dve.wait_ge(loads[i], 32)
                    nc.vector.tensor_tensor(g[:, part[i]], g[:, part[i]], s1[:, part[i]], ALU.mult).then_inc(*prod.up())
                    dve.wait_ge(*prod.nth(i + 1))
                    nc.vector.tensor_tensor(g[:, part[i]], g[:, part[i]], x[:, part[i]], ALU.add).then_inc(*total.up())

            @block.sync
            def _(sp):
                for i in range(seqs):
                    sp.dma_start(s1[:, part[i]], s1_kept[:, part[i]]).then_inc(loads[i], 16)
                    sp.dma_start(x[:, part[i]], x_kept[:, part[i]]).then_inc(loads[i], 16)
                for i in range(seqs):
                    sp.wait_ge(*total.nth(i + 1))
                    sp.dma_start(out_dram[:, part[i]], g[:, part[i]]).then_inc(stored.sem, 16)
                sp.wait_ge(stored.sem, 16 * seqs)


def program(nc, x_dram, wa, wb, wc, tab, c32_dram, out_dram):
    with ExitStack() as ctx:
        def sb(name, shape, dt=F32, at=ctx):
            return at.enter_context(nc.sbuf_tensor(name, shape, dt))

        xf = sb("xf", [P, SEQS * (SEQ + 1)])
        c32 = sb("c32", [P, C_END])
        c16 = sb("c16", [P, P + BAND], BF16)
        x_kept = nc.dram_tensor("x_kept", (P, SEQS * SEQ), F32).ap()
        s1_kept = nc.dram_tensor("s1_kept", (P, SEQS * SEQ), F32).ap()
        loaded = ctx.enter_context(nc.semaphore("loaded"))
        const = Constants(c32, c16)
        with ExitStack() as early:
            x = sb("x", [P, SEQS * SEQ], at=early)
            s1 = sb("s1", [P, SEQS * SEQ], at=early)
            with nc.Block() as block:
                @block.sync
                def _(sp):
                    sp.dma_start(x[:, :], x_dram).then_inc(loaded, 16)
                    sp.dma_start(c32[:, :], c32_dram).then_inc(loaded, 16)
                    sp.wait_ge(loaded, 32)

                @block.vector
                def _(dve):
                    dve.wait_ge(loaded, 32)
                    nc.vector.tensor_copy(c16[:, 0:P], const.ident)
                    nc.vector.tensor_copy(c16[:, P:], c32[:, C_MASK:C_MASK + BAND])
            level0(nc, x, wa, const, SEQS)
            level1(nc, x, xf, s1, wb, const, SEQS)
            keep(nc, [(x_kept, x[:, :]), (s1_kept, s1[:, :])])
        network(nc, xf, wc, tab, const, DEPTH, SEQS)
        result(nc, x_kept, s1_kept, xf, out_dram, SEQS)



def rows(a):
    return a.reshape(-1, P, a.shape[1]).transpose(1, 0, 2).reshape(P, -1)


def pack_level0(d):
    W = np.zeros((P, A_END), np.float32)
    for c, n in ((A_Q, "Wq"), (A_K, "Wk")):
        W[:, c:c + 512].reshape(P, HEADS, 32)[:, :, 0:16] = d["L0_attn_" + n].reshape(P, HEADS, 16)
    f = {n: d["L0_ffn_" + n] for n in ("Wg", "bg", "Wu", "bu", "Wd", "bd", "Wq", "keys", "down_embed", "up_embed")}
    W[:, A_V:A_V + P] = d["L0_attn_Wv"]
    W[:, A_O:A_O + P] = d["L0_attn_Wo"]
    W[:, A_G:A_G + 512] = f["Wg"]
    W[:, A_U:A_U + 512] = f["Wu"]
    W[:, A_D:A_D + 512] = rows(f["Wd"])
    W[:, A_DOWN:A_DOWN + 512] = f["down_embed"].T
    W[:, A_UP:A_UP + 512] = rows(f["up_embed"])
    W[:, A_WQT:A_WQT + 512] = f["Wq"].reshape(P, 2, 4, 64).transpose(1, 3, 2, 0).reshape(P, 512)
    W[:, A_KEYS:A_KEYS + 256] = f["keys"].transpose(2, 3, 0, 1).reshape(P, 256)
    W[:, A_BG:A_BG + 4] = f["bg"].reshape(4, P).T
    W[:, A_BU:A_BU + 4] = f["bu"].reshape(4, P).T
    W[:, A_BD] = f["bd"]
    return W


def pack_level1(d):
    W = np.zeros((P, B_END), np.float32)
    a = {n[8:]: v for n, v in d.items() if n.startswith("L1_attn_")}
    W[:, B_IN:B_IN + 512] = a["in_proj_w"]
    for c, n in ((B_DT, "dt_w"), (B_BP, "bp_w"), (B_CP, "cp_w")):
        W[:, c:c + 2 * STATES] = rows(a[n])
    W[:, B_OUT:B_OUT + 2 * P] = rows(a["out_w"])
    W[:, B_GW:B_GW + EXPERTS] = a["gate_w"]
    W[:, B_W1:B_W1 + EXPERTS * HID] = a["e_w1"].transpose(1, 0, 2).reshape(P, -1)
    W[:, B_W2:B_W2 + EXPERTS * HID] = a["e_w2"].reshape(EXPERTS, 4, P, P).transpose(2, 0, 1, 3).reshape(P, -1)
    W[0:STATES, B_S2I:B_S2I + 2 * P] = a["s2i_w"]
    W[0:EXPERTS, B_B2:B_B2 + P] = a["e_b2"]
    W[:, B_GB:B_GB + TILES * EXPERTS] = np.tile(a["gate_b"], (P, TILES))
    before = np.tril(np.ones((EXPERTS, EXPERTS)), -1).reshape(1, -1)
    W[:, B_LT:B_LT + TILES * EXPERTS * EXPERTS] = np.tile(before, (P, TILES))
    for e in range(EXPERTS):
        W[e, B_SEL + e * P:B_SEL + (e + 1) * P] = 1

    def put(name, block, height=P):
        c = B_P + BP[name]
        W[0:height, c:c + block.shape[1]] = block

    put("inb", a["in_proj_b"].reshape(4, P).T)
    put("conv", a["conv_w"].reshape(2, P, 3).transpose(1, 0, 2).reshape(P, 6))
    for name, n in (("convb", "conv_b"), ("s2ib", "s2i_b"), ("D", "D_param"), ("outb", "out_b"), ("n1", "norm1_w"), ("n2", "norm2_w")):
        put(name, a[n].reshape(-1, P).T)
    for name, n in (("dtb", "dt_b"), ("bpb", "bp_b"), ("cpb", "cp_b")):
        put(name, a[n].reshape(STATES, 1), STATES)
    put("b1", a["e_b1"].reshape(EXPERTS * 4, P).T)
    return W


def pack_network(d):
    a = {n[7:]: v for n, v in d.items() if n.startswith("L1_ffn_")}
    W = np.zeros((DEPTH, P, W_END), np.float32)
    qkv, n = a["Wqkv"], HEADS * DH
    for kind in range(2):
        part = qkv[:, :, kind * n:(kind + 1) * n].reshape(DEPTH, P, 4, 4, 2, HALF)
        W[:, :, kind * n:(kind + 1) * n] = part.transpose(0, 1, 2, 4, 3, 5).reshape(DEPTH, P, n)
    W[:, :, W_V:W_V + n] = qkv[:, :, 2 * n:]
    W[:, :, W_O:W_O + n] = a["Wo"].reshape(DEPTH, n // P, P, P).transpose(0, 2, 1, 3).reshape(DEPTH, P, n)
    W[:, :, W_1:W_1 + 2 * FF] = a["W1"]
    for c, (f, m) in enumerate(FCH):
        W[:, 0:m, W_2 + c * P:W_2 + (c + 1) * P] = a["W2"][:, f:f + m]
        W[:, 0:m, W_P + PAR["b1"] + c] = a["b1"][:, f:f + m]
        W[:, 0:m, W_P + PAR["b1"] + 3 + c] = a["b1"][:, FF + f:FF + f + m]
    for i, name in enumerate(("qA", "qB", "kA", "kB")):
        s = a["q_scale" if i < 2 else "k_scale"]
        h = HALF * (i % 2)
        W[:, :, W_P + PAR[name]] = np.tile(s[:, h:h + HALF], (1, 4))
    W[:, :, W_P + PAR["g"]] = a["ln_g"]
    W[:, :, W_P + PAR["b"]] = a["ln_b"]
    W[:, :, W_P + PAR["b2"]] = a["b2"]
    return W


def rotary_tables():
    f = np.float32
    half = np.arange(0, DH, 2, dtype=f)
    inv_freq = f(1.0) / f(10000.0) ** (half / f(DH))
    t = np.arange(SEQ, dtype=f)
    angle = t[:, None] * inv_freq[None, :]
    base = (half + f(0.4 * DH)) / f(1.4 * DH)
    scale = base[None, :] ** ((t - f(SEQ // 2)) / f(LOOK // 2))[:, None]
    c, s = np.cos(angle), np.sin(angle)
    tables = np.stack([c * scale, s * scale, c / scale, s / scale]).astype(f)
    return np.tile(tables.transpose(2, 0, 1), (4, 1, 1))


def constants():
    c = np.zeros((P, C_END), np.float32)
    c[:, C_ID:C_ID + P] = np.eye(P)
    c[:, C_MEAN:C_MEAN + P] = 1.0 / P
    c[:, C_HEAD:C_HEAD + P] = np.kron(np.eye(4), np.ones((HALF, HALF)))
    c[:, C_M64:C_M64 + P] = 1.0 / STATES
    c[:, C_TRI:C_TRI + P] = np.triu(np.ones((P, P)))
    i, k = np.arange(P)[:, None], np.arange(BAND)[None, :]
    c[:, C_MASK:C_MASK + BAND] = np.where((k >= i) & (k <= i + LOOK), 0.0, -BIG)
    for i, v in enumerate(COLS.values()):
        c[:, C_COL + i] = v
    return c


def kernel(**inputs):
    import concourse.bacc as bacc
    from concourse.bass_utils import run_bass_kernel_spmd

    d = {n: np.asarray(v) for n, v in inputs.items()}
    x = d["L0_attn_hidden_states"]
    arrays = {
        "x": x.transpose(2, 0, 1).reshape(P, SEQS * SEQ),
        "w_level0": pack_level0(d),
        "w_level1": pack_level1(d),
        "w_network": pack_network(d),
        "tables": rotary_tables(),
        "consts": constants(),
    }
    nc = bacc.Bacc("TRN2", target_bir_lowering=False, num_devices=1)
    given, args = {}, []
    for name, a in arrays.items():
        a = np.ascontiguousarray(a)
        given[f"in_{name}"] = a
        args.append(nc.dram_tensor(f"in_{name}", a.shape, mybir.dt.from_np(a.dtype), kind="ExternalInput").ap())
    out = nc.dram_tensor("out", (P, SEQS * SEQ), F32, kind="ExternalOutput").ap()
    program(nc, *args, out)
    r = run_bass_kernel_spmd(nc, [given], core_ids=[0])
    y = r.results[0]["out"]
    return np.ascontiguousarray(y.reshape(P, SEQS, SEQ).transpose(1, 2, 0)).reshape(x.shape)
```

```python
from contextlib import ExitStack

import numpy as np

import concourse.bass as bass
from concourse import mybir
from concourse.alu_op_type import AluOpType as ALU

ACT = mybir.ActivationFunctionType
F32 = mybir.dt.float32
BF16 = mybir.dt.bfloat16
AX = mybir.AxisListType

P = 128
SEQS, SEQ = 8, 512
TILE = 128
TILES = SEQ // TILE
DEPTH = 6
HEADS, DH = 16, 64
HALF = DH // 2
LOOK = 32
BAND = LOOK + TILE
FF = 341
FCH = [(0, 128), (128, 128), (256, FF - 256)]
QK_SCALE = 8.0
NORM_MIN = 1e-12
LN_SHIFT = 20

PAIRS = HEADS // 2

NU = 2 * PAIRS
UNIT = [(u % 4 // 2, 2 * (u // 4) + u % 2) for u in range(NU)]
CARRY = 4

H_V = 0
H_P = H_V + HEADS * DH
H_QK = H_P + 4
H_FIRST = H_QK + CARRY * 2 * P
H_END = H_QK + NU * 2 * P
T_O = 0
T_1 = T_O + HEADS * DH
T_2 = T_1 + 2 * FF
T_P = T_2 + 3 * P
PAR = {"g": 0, "b": 1, "b1": 2, "b2": 8}
T_END = T_P + 9


class Signal:

    def __init__(self, sem, per=0, primed=0):
        self.sem, self.per, self.primed, self.n = sem, per, primed, 0

    def prime(self):
        assert self.primed
        return self.sem, 1

    def up(self):
        self.n += 1
        return self.sem, 1

    def nth(self, n, turn=0):
        value = turn * self.per + (n + self.primed) if self.per else n
        assert not isinstance(value, int) or value > 0
        return self.sem, value

    def last(self, turn=0):
        return self.nth(self.n, turn)

    def full(self):
        assert self.n == self.per, (self.n, self.per)


def network(nc, xf, wh_dram, wt_dram, tab_dram, const, depth, seqs):
    with ExitStack() as ctx:
        def sb(name, shape, dt=F32):
            return ctx.enter_context(nc.sbuf_tensor("c_" + name, shape, dt))

        def sig(name, per=0, primed=0):
            return Signal(ctx.enter_context(nc.semaphore("c_" + name)), per, primed)

        ident, ones_mean, ones_head, col = const.ident, const.mean, const.head, const.col
        WH = sb("WH", [P, H_END])
        WT = sb("WT", [P, T_END])
        base = sb("base", [P, 4, SEQ])
        TC = sb("TC", [P, 2, SEQ])
        TS = sb("TS", [P, 2, SEQ])
        xs = sb("xs", [P, SEQ])
        sq = sb("sq", [P, 2, SEQ])
        lnr = sb("lnr", [P, SEQ])
        rinv = sb("rinv", [P, 2, SEQ])
        tcs = sb("tcs", [P, 2, 2, SEQ])
        rot = sb("rot", [P, 2, SEQ])
        QK = sb("QK", [P, 2, PAIRS, SEQ])
        V = sb("V", [P, TILES, HEADS * DH])
        OT = sb("OT", [P, PAIRS, SEQ])
        mx = sb("mx", [P, 2, 4])
        nb = sb("nb", [P, 2, 4])
        sums = sb("sums", [P, 2, 4])
        rs = sb("rs", [P, 2, 4])
        Pb = sb("Pb", [P, 3, 4, 96 + BAND])
        PTs = sb("PTs", [P, 2, 4, TILE])
        PT2s = sb("PT2s", [P, 2, 4, LOOK])
        x1 = sb("x1", [P, 1 + SEQ])
        xs2 = sb("xs2", [P, SEQ])
        cen = sb("cen", [P, SEQ])
        csq = sb("csq", [P, SEQ])
        lnv_ = sb("lnv", [P, SEQ])
        rstd = sb("rstd", [P, SEQ])
        xn = sb("xn", [P, SEQ])
        gl = sb("gl", [P, 3, SEQ])
        hh = sb("hh", [P, 3, SEQ])
        S = ctx.enter_context(nc.psum_tensor("c_S", [P, 4, 512], F32))
        PAB = ctx.enter_context(nc.psum_tensor("c_PAB", [P, 2, 512], F32))
        PT = ctx.enter_context(nc.psum_tensor("c_PT", [P, 512], F32))
        PX = ctx.enter_context(nc.psum_tensor("c_PX", [P, 512], F32))

        def par(name, k=0):
            return WT[:, T_P + PAR[name] + k:T_P + PAR[name] + k + 1]

        NS = 16
        wh_in = sig("wh_in")
        wt_in = sig("wt_in")
        base_in = sig("base_in")
        layer_done = sig("layer_done", 1, 1)
        tables = sig("tables", 4)
        zeroed = sig("zeroed")
        shifted = sig("shifted", 2)
        projected = sig("projected", NU)
        squared = sig("squared", NU)
        prods = sig("prods", 2 * NU)
        summed = sig("summed", NU)
        logs = sig("logs", NU)
        rinvs = sig("rinvs", NU)
        rotated = sig("rotated", NU)
        qk_ready = sig("qk_ready", NU)
        v_done = sig("v_done", 8)
        v_even = sig("v_even", 4)
        v_odd = sig("v_odd", 4)
        s_done = sig("s_done", NS)
        maxed = sig("maxed", NS)
        nb_ready = sig("nb_ready", NS)
        exps = sig("exps", NS)
        rs_ready = sig("rs_ready", NS)
        p_ready = sig("p_ready", NS)
        pt_done = sig("pt_done", NS)
        pt_copied = sig("pt_copied", NS)
        px_copied = sig("px_copied", 12)
        pv_done = sig("pv_done", NS)
        po_copied = sig("po_copied", NS)
        wo_done = sig("wo_done", 1)
        x1_ready = sig("x1_ready", 1)
        xs2_ready = sig("xs2_ready", 2)
        mean_done = sig("mean_done", 1)
        centred = sig("centred", 1)
        csq_ready = sig("csq_ready", 1)
        var_done = sig("var_done", 1)
        lnv = sig("lnv", 1)
        rstd_ready = sig("rstd_ready", 1)
        xnorm = sig("xnorm", 1)
        xn_ready = sig("xn_ready", 1)
        hg_done = sig("hg_done", 3)
        gelus = sig("gelus", 3)
        h_ready = sig("h_ready", 3)
        w2_done = sig("w2_done", 1)

        def prevs(n):
            return (n // 4) * 3 + n % 4

        def first(turn):
            return isinstance(turn, int) and turn == 0

        def beside(n, turn, last):
            if n < NU - CARRY:
                return [(n + CARRY, turn)]
            return [] if last else [(n + CARRY - NU, turn + 1)]

        WO, MEAN, VAR, OUT = PT[:, :], PX[:, :], PT[:, :], S[:, 2, :]
        GATE = [PX, S[:, 2, :], PX]
        VAL = [PT, S[:, 3, :], PT]

        with nc.Block() as block:
            @block.sync
            def _(sp):
                sp.dma_start(WH[:, 0:H_FIRST], wh_dram[0][:, 0:H_FIRST]).then_inc(wh_in.sem, 16)
                sp.dma_start(base[:, :, :], tab_dram).then_inc(base_in.sem, 16)
                sp.wait_ge(wh_in.sem, 16)
                sp.dma_start(WH[:, H_FIRST:], wh_dram[0][:, H_FIRST:]).then_inc(wh_in.sem, 16)
                sp.dma_start(WT[:, :], wt_dram[0]).then_inc(wt_in.sem, 16)
                with sp.Fori(1, depth) as l:
                    wh = wh_dram[bass.ds(l, 1)].rearrange("a p c -> (a p) c")
                    sp.wait_ge(*projected.nth(CARRY + 1 - NU, l * seqs))
                    sp.dma_start(WH[:, 0:H_FIRST], wh[:, 0:H_FIRST]).then_inc(wh_in.sem, 16)
                    sp.wait_ge(*projected.nth(1, l * seqs))
                    sp.dma_start(WH[:, H_FIRST:], wh[:, H_FIRST:]).then_inc(wh_in.sem, 16)
                    sp.wait_ge(*layer_done.nth(0, l * seqs))
                    sp.dma_start(WT[:, :], wt_dram[bass.ds(l, 1)].rearrange("a p c -> (a p) c")).then_inc(wt_in.sem, 16)

            def turns(eng, head, main, both, tail):
                head()
                with eng.Fori(0, depth - 1) as l:
                    with eng.Fori(0, seqs - 1) as s:
                        main(l * seqs + s, s + 1, None, False)
                        both(l * seqs + s, s, l, s + 1, l)
                    main(l * seqs + (seqs - 1), 0, l + 1, False)
                    both(l * seqs + (seqs - 1), seqs - 1, l, 0, l + 1)
                l = depth - 1
                with eng.Fori(0, seqs - 1) as s:
                    main(s + l * seqs, s + 1, None, False)
                    both(s + l * seqs, s, l, s + 1, l)
                main(l * seqs + seqs - 1, None, None, True)
                tail(l * seqs + seqs - 1, seqs - 1, l)

            @block.gpsimd
            def _(pool):
                nc.gpsimd.memset(Pb[:, :, :, 0:128], 0.0).then_inc(*zeroed.up())
                nc.gpsimd.memset(x1[:, 0:1], 0.0).then_inc(*zeroed.up())

                def rotate(u, turn):
                    pool.wait_ge(*prods.nth(2 * u + 2, turn))
                    if u >= 2 or not first(turn):
                        pool.wait_ge(*qk_ready.nth(u - 1, turn))
                    nc.gpsimd.tensor_tensor(rot[:, u % 2], tcs[:, u % 2, 0], tcs[:, u % 2, 1], ALU.add).then_inc(*rotated.up())

                def normalise(n, turn):
                    pool.wait_ge(*rs_ready.nth(n + 1, turn))
                    lo = 96 if n % 4 else 128
                    p = Pb[:, n % 3, :, lo:]
                    r = rs[:, n % 2, :].unsqueeze(2).broadcast_to([P, 4, 96 + BAND - lo])
                    nc.gpsimd.tensor_tensor(p, p, r, ALU.mult).then_inc(*p_ready.up())

                def head():
                    for u in range(CARRY + 1):
                        rotate(u, 0)

                def main(turn, s_next, new, last):
                    for n in range(1, NS):
                        normalise(n - 1, turn)
                        for u in beside(n, turn, last):
                            rotate(*u)

                def tail(turn, s, l):
                    normalise(NS - 1, turn)

                def both(turn, s, l, s_next, l_next):
                    normalise(NS - 1, turn)
                    rotate(CARRY, turn + 1)

                turns(pool, head, main, both, tail)

            @block.scalar
            def _(act):
                def square(u, turn):
                    act.wait_ge(*projected.nth(u + 1, turn))
                    if u >= 2 or not first(turn):
                        act.wait_ge(*summed.nth(u - 1, turn))
                    nc.scalar.activation(sq[:, u % 2], PAB[:, 0, :], ACT.Square).then_inc(*squared.up())

                def inverse_norm(u, turn):
                    act.wait_ge(*summed.nth(u + 1, turn))
                    if u >= 2 or not first(turn):
                        act.wait_ge(*qk_ready.nth(u - 1, turn))
                    nc.scalar.activation(lnr[:, :], PAB[:, 0, :], ACT.Ln, bias=col["tiny"], scale=float(2 ** LN_SHIFT)).then_inc(*logs.up())
                    act.wait_ge(*logs.nth(u + 1, turn))
                    nc.scalar.activation(rinv[:, u % 2], lnr[:, :], ACT.Exp, bias=col["shift"], scale=-0.5).then_inc(*rinvs.up())

                def v_copy(t, turn):
                    act.wait_ge(*v_done.nth(2 * t + 1, turn))
                    if not first(turn):
                        act.wait_ge(*pv_done.nth(min(t - 2, 0), turn))
                    nc.scalar.activation(V[:, t, 0:512], S[:, 2 * t % 4, :], ACT.Copy).then_inc(*v_even.up())

                def exp(n, turn):
                    act.wait_ge(*nb_ready.nth(n + 1, turn))
                    if n == 0 and not first(turn):
                        act.wait_ge(*pt_done.nth(0, turn))
                    if n >= 3:
                        act.wait_ge(*pt_done.nth(n - 2, turn))
                    if n >= 2:
                        act.wait_ge(*rs_ready.nth(n - 1, turn))
                    lo = 0 if n % 4 else LOOK
                    for j in range(4):
                        b, c = 2 * (n % 2) + j % 2, (j // 2) * BAND
                        i = 2 * (j % 2) + j // 2
                        e = nc.scalar.activation(Pb[:, n % 3, i, 96 + lo:], S[:, b, c + lo:c + BAND], ACT.Exp,
                                                 bias=nb[:, n % 2, i:i + 1], scale=QK_SCALE, accum_out=sums[:, n % 2, i:i + 1])
                    e.then_inc(*exps.up())

                def prev_copy(n, turn):
                    if n % 4:
                        act.wait_ge(*pt_done.nth(n + 1, turn))
                        if n >= 2:
                            act.wait_ge(*pv_done.nth(n - 1, turn))
                        nc.scalar.activation(PT2s[:, n % 2], PX[:, 256:384].rearrange("p (j q) -> p j q", j=4), ACT.Copy)\
                            .then_inc(*px_copied.up())

                def out_copy(n, turn):
                    g, t = n // 4, n % 4
                    act.wait_ge(*pv_done.nth(n + 1, turn))
                    nc.scalar.activation(OT[:, 2 * g:2 * g + 2, t * TILE:(t + 1) * TILE],
                                         PX[:, 0:256].rearrange("p (j q) -> p j q", j=2), ACT.Copy).then_inc(*po_copied.up())

                def norm_squares(turn):
                    act.wait_ge(*centred.nth(1, turn))
                    nc.scalar.activation(csq[:, :], cen[:, :], ACT.Square).then_inc(*csq_ready.up())

                def norm_root(turn):
                    act.wait_ge(*var_done.nth(1, turn))
                    nc.scalar.activation(lnv_[:, :], VAR, ACT.Ln, bias=col["eps5"]).then_inc(*lnv.up())
                    act.wait_ge(*lnv.nth(1, turn))
                    nc.scalar.activation(rstd[:, :], lnv_[:, :], ACT.Exp, scale=-0.5).then_inc(*rstd_ready.up())

                def gates(turn):
                    for c, (_, m) in enumerate(FCH):
                        act.wait_ge(*hg_done.nth(c + 1, turn))
                        nc.scalar.activation(gl[0:m, c], GATE[c][0:m, :], ACT.Gelu, bias=par("b1", 3 + c)[0:m, :]).then_inc(*gelus.up())
                    nc.scalar.preload_act_table_set("natural_log_exp_and_others")

                def head():
                    for u in range(CARRY):
                        square(u, 0)
                        inverse_norm(u, 0)
                    for t in range(TILES):
                        v_copy(t, 0)
                    square(CARRY, 0)
                    inverse_norm(CARRY, 0)
                    exp(0, 0)

                def main(turn, s_next, new, last):
                    for n in range(1, NS):
                        units = beside(n, turn, last)
                        for u in units:
                            square(*u)
                        if n >= 2:
                            prev_copy(n - 2, turn)
                        for u in units:
                            inverse_norm(*u)
                        exp(n, turn)
                        if n >= 2:
                            out_copy(n - 2, turn)

                def tail(turn, s, l):
                    for n in (NS - 2, NS - 1):
                        prev_copy(n, turn)
                        out_copy(n, turn)
                    norm_squares(turn)
                    norm_root(turn)
                    gates(turn)

                def both(turn, s, l, s_next, l_next):
                    nxt = turn + 1
                    prev_copy(NS - 2, turn)
                    v_copy(0, nxt)
                    out_copy(NS - 2, turn)
                    prev_copy(NS - 1, turn)
                    v_copy(1, nxt)
                    out_copy(NS - 1, turn)
                    v_copy(2, nxt)
                    v_copy(3, nxt)
                    norm_squares(turn)
                    norm_root(turn)
                    square(CARRY, nxt)
                    inverse_norm(CARRY, nxt)
                    gates(turn)
                    exp(0, nxt)

                nc.scalar.preload_act_table_set("natural_log_exp_and_others")
                act.wait_ge(*zeroed.nth(2))
                turns(act, head, main, both, tail)

            @block.tensor
            def _(pe):
                def proj(u, turn):
                    if u == 0:
                        pe.wait_ge(*shifted.nth(2, turn))
                    if u or not first(turn):
                        pe.wait_ge(*prods.nth(2 * u, turn))
                        pe.wait_ge(*logs.nth(u, turn))
                    c = H_QK + u * 2 * P
                    nc.tensor.matmul(PAB[:, 0, :], WH[:, c:c + P], xs[:, :], start=True, stop=True)
                    nc.tensor.matmul(PAB[:, 1, :], WH[:, c + P:c + 2 * P], xs[:, :], start=True, stop=True).then_inc(*projected.up())

                def sumsq(u, turn):
                    pe.wait_ge(*squared.nth(u + 1, turn))
                    pe.wait_ge(*prods.nth(2 * u + 1, turn))
                    nc.tensor.matmul(PAB[:, 0, :], ones_head, sq[:, u % 2], start=True, stop=True).then_inc(*summed.up())

                def v_proj(i, turn):
                    if i >= 4:
                        pe.wait_ge(*(v_even, v_odd)[i % 2].nth((i - 4) // 2 + 1, turn))
                    elif not first(turn):
                        pe.wait_ge(*exps.nth(i // 2 - 1, turn))
                    t, h = i // 2, i % 2
                    nc.tensor.matmul(S[:, i % 4, :], xs[:, t * TILE:(t + 1) * TILE],
                                     WH[:, H_V + h * 512:H_V + h * 512 + 512], start=True, stop=True).then_inc(*v_done.up())

                def scores(n, turn):
                    g, t = n // 4, n % 4
                    if t == 0:
                        pe.wait_ge(*qk_ready.nth(4 * g + 4, turn))
                    if n >= 2:
                        pe.wait_ge(*exps.nth(n - 1, turn))
                    if n == 0:
                        pe.wait_ge(*v_even.nth(4, turn))
                        pe.wait_ge(*v_odd.nth(4, turn))
                    if n == 1:
                        pe.wait_ge(*layer_done.nth(0, turn))
                    lo = 0 if t else LOOK
                    k0 = t * TILE - LOOK + lo
                    for r in range(2):
                        b = 2 * (n % 2) + r
                        out = S[:, b, 0:2 * BAND].rearrange("p (c k) -> p c k", c=2)[:, :, lo:]
                        mask = const.mask[:, :].rearrange("p (c k) -> p c k", c=2)[:, :, lo:]
                        nc.tensor.matmul(out, const.identb, mask, start=True, stop=False, skip_group_check=True)
                    for c in range(2):
                        for r in range(2):
                            rows = slice(64 * r, 64 * r + 64)
                            mm = nc.tensor.matmul(S[:, 2 * (n % 2) + r, c * BAND + lo:(c + 1) * BAND],
                                                  QK[rows, 0, 2 * g + c, t * TILE:(t + 1) * TILE],
                                                  QK[rows, 1, 2 * g + c, k0:(t + 1) * TILE], start=False, stop=c == 1, skip_group_check=True)
                    mm.then_inc(*s_done.up())

                def turn_probs(n, turn):
                    pe.wait_ge(*p_ready.nth(n + 1, turn))
                    if n >= 1:
                        pe.wait_ge(*pt_copied.nth(n, turn))
                        pe.wait_ge(*po_copied.nth(n, turn))
                    for j in range(4):
                        mm = nc.tensor.transpose(PT[:, j * TILE:(j + 1) * TILE], Pb[:, n % 3, j, 128:], ident)
                    if n % 4:
                        for j in range(4):
                            mm = nc.tensor.transpose(PX[:, 256 + j * LOOK:256 + (j + 1) * LOOK], Pb[0:LOOK, n % 3, j, 0:128],
                                                     ident[0:LOOK, 0:LOOK])
                    mm.then_inc(*pt_done.up())

                def values(n, turn):
                    g, t = n // 4, n % 4
                    pe.wait_ge(*pt_copied.nth(n + 1, turn))
                    if t:
                        pe.wait_ge(*px_copied.nth(prevs(n), turn))
                    for r in range(2):
                        for c in range(2):
                            h = 4 * g + 2 * c + r
                            i = 2 * r + c
                            rows = slice(64 * r, 64 * r + 64)
                            mm = nc.tensor.matmul(PX[rows, c * TILE:(c + 1) * TILE], V[:, t, h * DH:(h + 1) * DH], PTs[:, n % 2, i, :],
                                                  start=True, stop=t == 0)
                            if t:
                                mm = nc.tensor.matmul(PX[rows, c * TILE:c * TILE + LOOK], V[:, t - 1, h * DH:(h + 1) * DH],
                                                      PT2s[:, n % 2, i, :], start=False, stop=True)
                    mm.then_inc(*pv_done.up())

                def out_proj(turn, l):
                    pe.wait_ge(wt_in.sem, l * 16 + 16)
                    pe.wait_ge(*po_copied.nth(NS, turn))
                    for p in range(PAIRS):
                        mm = nc.tensor.matmul(WO, WT[:, T_O + p * P:T_O + (p + 1) * P], OT[:, p, :], start=p == 0, stop=p == PAIRS - 1)
                    mm.then_inc(*wo_done.up())

                def mean(turn):
                    pe.wait_ge(*xs2_ready.nth(2, turn))
                    nc.tensor.matmul(MEAN, ones_mean, xs2[:, :], start=True, stop=True).then_inc(*mean_done.up())

                def variance(turn):
                    pe.wait_ge(*csq_ready.nth(1, turn))
                    nc.tensor.matmul(VAR, ones_mean, csq[:, :], start=True, stop=True).then_inc(*var_done.up())

                def inner(turn):
                    pe.wait_ge(*xn_ready.nth(1, turn))
                    for c, (f, m) in enumerate(FCH):
                        if c == 2:
                            pe.wait_ge(*gelus.nth(1, turn))
                        nc.tensor.matmul(GATE[c][0:m, :], WT[:, T_1 + FF + f:T_1 + FF + f + m], xn[:, :], start=True, stop=True)
                        if c == 2:
                            pe.wait_ge(*h_ready.nth(1, turn))
                        nc.tensor.matmul(VAL[c][0:m, :], WT[:, T_1 + f:T_1 + f + m], xn[:, :], start=True, stop=True).then_inc(*hg_done.up())

                def outer(turn):
                    pe.wait_ge(*gelus.nth(2, turn))
                    for c, (f, m) in enumerate(FCH):
                        pe.wait_ge(*h_ready.nth(c + 1, turn))
                        mm = nc.tensor.matmul(OUT, WT[0:m, T_2 + c * P:T_2 + (c + 1) * P], hh[0:m, c], start=c == 0, stop=c == 2)
                    mm.then_inc(*w2_done.up())

                def head():
                    pe.wait_ge(wh_in.sem, 16)
                    for u in range(CARRY):
                        proj(u, 0)
                        sumsq(u, 0)
                    for i in range(8):
                        v_proj(i, 0)
                    scores(0, 0)
                    pe.wait_ge(wh_in.sem, 32)
                    proj(CARRY, 0)
                    sumsq(CARRY, 0)

                def main(turn, s_next, new, last):
                    for n in range(1, NS):
                        units = beside(n, turn, last)
                        if new is not None and n == NU - CARRY:
                            pe.wait_ge(wh_in.sem, new * 32 + 16)
                        for u in units:
                            proj(*u)
                        scores(n, turn)
                        if n >= 2:
                            turn_probs(n - 2, turn)
                        for u in units:
                            sumsq(*u)
                        if n >= 2:
                            values(n - 2, turn)

                def tail(turn, s, l):
                    for n in (NS - 2, NS - 1):
                        turn_probs(n, turn)
                        values(n, turn)
                    out_proj(turn, l)
                    mean(turn)
                    variance(turn)
                    inner(turn)
                    outer(turn)

                def both(turn, s, l, s_next, l_next):
                    nxt = turn + 1
                    for i, n in enumerate((NS - 2, NS - 1)):
                        turn_probs(n, turn)
                        v_proj(2 * i, nxt)
                        v_proj(2 * i + 1, nxt)
                        values(n, turn)
                    v_proj(4, nxt)
                    v_proj(5, nxt)
                    out_proj(turn, l)
                    v_proj(6, nxt)
                    v_proj(7, nxt)
                    mean(turn)
                    scores(0, nxt)
                    variance(turn)
                    pe.wait_ge(wh_in.sem, l_next * 32 + 32)
                    proj(CARRY, nxt)
                    sumsq(CARRY, nxt)
                    inner(turn)
                    outer(turn)

                turns(pe, head, main, both, tail)

            @block.vector
            def _(dve):
                def shift(turn, s):
                    if not first(turn):
                        dve.wait_ge(*projected.nth(0, turn))
                    src = xf[:, bass.ds(s * (SEQ + 1), SEQ + 1)]
                    nc.vector.tensor_copy(xs[0:64, :], src[0:64, 1:SEQ + 1]).then_inc(*shifted.up())
                    nc.vector.tensor_copy(xs[64:P, :], src[64:P, 0:SEQ]).then_inc(*shifted.up())

                def products(u, turn):
                    kind = UNIT[u][0]
                    dve.wait_ge(*squared.nth(u + 1, turn))
                    if u >= 2 or not first(turn):
                        dve.wait_ge(*rotated.nth(u - 1, turn))
                    nc.vector.tensor_tensor(tcs[:, u % 2, 0], PAB[:, 0, :], TC[:, kind], ALU.mult).then_inc(*prods.up())
                    nc.vector.tensor_tensor(tcs[:, u % 2, 1], PAB[:, 1, :], TS[:, kind], ALU.mult).then_inc(*prods.up())

                def finish(u, turn):
                    kind, pair = UNIT[u]
                    dve.wait_ge(*rotated.nth(u + 1, turn))
                    dve.wait_ge(*rinvs.nth(u + 1, turn))
                    nc.vector.scalar_tensor_tensor(out=QK[:, kind, pair], in0=rinv[:, u % 2], scalar=1.0 / NORM_MIN,
                                                   in1=rot[:, u % 2], op0=ALU.min, op1=ALU.mult).then_inc(*qk_ready.up())

                def v_copy(t, turn):
                    dve.wait_ge(*v_done.nth(2 * t + 2, turn))
                    if not first(turn):
                        dve.wait_ge(*pv_done.nth(min(t - 2, 0), turn))
                    nc.vector.tensor_copy(V[:, t, 512:1024], S[:, (2 * t + 1) % 4, :]).then_inc(*v_odd.up())

                def row_max(n, turn):
                    dve.wait_ge(*s_done.nth(n + 1, turn))
                    lo = 0 if n % 4 else LOOK
                    b = 2 * (n % 2)
                    nc.vector.tensor_reduce(mx[:, n % 2].rearrange("p (b c) -> p b c", b=2),
                                            S[:, b:b + 2, 0:2 * BAND].rearrange("p b (c k) -> p b c k", c=2)[:, :, :, lo:],
                                            AX.X, ALU.max).then_inc(*maxed.up())
                    dve.wait_ge(*maxed.nth(n + 1, turn))
                    if n >= 2:
                        dve.wait_ge(*exps.nth(n - 1, turn))
                    nc.vector.tensor_scalar(nb[:, n % 2], mx[:, n % 2], -QK_SCALE, None, ALU.mult).then_inc(*nb_ready.up())

                def inv_sum(n, turn):
                    dve.wait_ge(*exps.nth(n + 1, turn))
                    if n >= 2:
                        dve.wait_ge(*p_ready.nth(n - 1, turn))
                    nc.vector.reciprocal(rs[:, n % 2], sums[:, n % 2]).then_inc(*rs_ready.up())

                def pt_copy(n, turn):
                    dve.wait_ge(*pt_done.nth(n + 1, turn))
                    if n >= 2:
                        dve.wait_ge(*pv_done.nth(n - 1, turn))
                    nc.vector.tensor_copy(PTs[:, n % 2], PT[:, :].rearrange("p (j q) -> p j q", j=4)).then_inc(*pt_copied.up())

                def residual(turn, s):
                    dve.wait_ge(*wo_done.nth(1, turn))
                    src = xf[:, bass.ds(s * (SEQ + 1), SEQ + 1)]
                    nc.vector.tensor_tensor(x1[:, 1:SEQ + 1], WO, src[:, 1:SEQ + 1], ALU.add).then_inc(*x1_ready.up())
                    dve.wait_ge(*x1_ready.nth(1, turn))
                    nc.vector.tensor_copy(xs2[0:64, :], x1[0:64, 1:SEQ + 1]).then_inc(*xs2_ready.up())
                    nc.vector.tensor_copy(xs2[64:P, :], x1[64:P, 0:SEQ]).then_inc(*xs2_ready.up())

                def centre(turn):
                    dve.wait_ge(*mean_done.nth(1, turn))
                    nc.vector.tensor_tensor(cen[:, :], xs2[:, :], MEAN, ALU.subtract).then_inc(*centred.up())

                def scale(turn):
                    dve.wait_ge(*rstd_ready.nth(1, turn))
                    nc.vector.tensor_tensor(xn[:, :], cen[:, :], rstd[:, :], ALU.mult).then_inc(*xnorm.up())
                    dve.wait_ge(*xnorm.nth(1, turn))
                    nc.vector.tensor_scalar(xn[:, :], xn[:, :], par("g"), par("b"), ALU.mult, ALU.add).then_inc(*xn_ready.up())

                def hidden(c, turn):
                    m = FCH[c][1]
                    dve.wait_ge(*gelus.nth(c + 1, turn))
                    nc.vector.scalar_tensor_tensor(out=hh[0:m, c], in0=VAL[c][0:m, :], scalar=par("b1", c)[0:m, :],
                                                   in1=gl[0:m, c], op0=ALU.add, op1=ALU.mult).then_inc(*h_ready.up())

                def finish_turn(turn, s):
                    dve.wait_ge(*w2_done.nth(1, turn))
                    dst = xf[:, bass.ds(s * (SEQ + 1) + 1, SEQ)]
                    nc.vector.scalar_tensor_tensor(out=dst, in0=OUT, scalar=par("b2"), in1=x1[:, 1:SEQ + 1],
                                                   op0=ALU.add, op1=ALU.add).then_inc(*layer_done.up())

                def tables_of(l):
                    dve.wait_ge(wh_in.sem, l * 32 + 16)
                    for kind in range(2):
                        own, partner = (WH[:, H_P + 2 * kind + i:H_P + 2 * kind + i + 1] for i in range(2))
                        nc.vector.tensor_scalar(TC[:, kind], base[:, 2 * kind], own, None, ALU.mult).then_inc(*tables.up())
                        nc.vector.tensor_scalar(TS[:, kind], base[:, 2 * kind + 1], partner, None, ALU.mult).then_inc(*tables.up())
                    dve.wait_ge(*tables.nth(4, l))

                def head():
                    shift(0, 0)
                    tables_of(0)
                    for u in range(CARRY):
                        products(u, 0)
                        finish(u, 0)
                    for t in range(TILES):
                        v_copy(t, 0)
                    row_max(0, 0)
                    products(CARRY, 0)
                    finish(CARRY, 0)

                def main(turn, s_next, new, last):
                    for n in range(1, NS):
                        if n == NU - CARRY and not last:
                            shift(turn + 1, s_next)
                            if new is not None:
                                tables_of(new)
                        units = beside(n, turn, last)
                        inv_sum(n - 1, turn)
                        for u in units:
                            products(*u)
                        if n >= 2:
                            pt_copy(n - 2, turn)
                        row_max(n, turn)
                        for u in units:
                            finish(*u)

                def tail(turn, s, l):
                    inv_sum(NS - 1, turn)
                    pt_copy(NS - 2, turn)
                    pt_copy(NS - 1, turn)
                    residual(turn, s)
                    centre(turn)
                    scale(turn)
                    for c in range(3):
                        hidden(c, turn)
                    finish_turn(turn, s)

                def both(turn, s, l, s_next, l_next):
                    nxt = turn + 1
                    inv_sum(NS - 1, turn)
                    pt_copy(NS - 2, turn)
                    v_copy(0, nxt)
                    pt_copy(NS - 1, turn)
                    for t in (1, 2):
                        v_copy(t, nxt)
                    residual(turn, s)
                    v_copy(3, nxt)
                    centre(turn)
                    row_max(0, nxt)
                    products(CARRY, nxt)
                    scale(turn)
                    finish(CARRY, nxt)
                    for c in range(3):
                        hidden(c, turn)
                    finish_turn(turn, s)

                nc.vector.memset(mx[:, :, :], 0.0).then_inc(*layer_done.prime())
                dve.wait_ge(base_in.sem, 16)
                dve.wait_ge(*zeroed.nth(2))
                turns(dve, head, main, both, tail)


A_Q = 0
A_K = A_Q + HEADS * 32
A_V = A_K + HEADS * 32
A_O = A_V + P
A_G = A_O + P
A_U = A_G + 512
A_D = A_U + 512
A_DOWN = A_D + 512
A_UP = A_DOWN + 512
A_WQT = A_UP + 512
A_KEYS = A_WQT + 512
A_BG = A_KEYS + 256
A_BU = A_BG + 4
A_BD = A_BU + 4
A_END = A_BD + 1
BIG = 1e30
TOP = 8
SPAN = {0: 0, 1: 512, 3: 896, 2: 1024}
SPANS = 1280


def level0(nc, x, w_dram, const, seqs):
    with ExitStack() as ctx:
        def sb(name, shape, dt=F32):
            return ctx.enter_context(nc.sbuf_tensor("a_" + name, shape, dt))

        def sig(name, per=0, primed=0):
            return Signal(ctx.enter_context(nc.semaphore("a_" + name)), per, primed)

        ident, ones_mean, ones_head, col = const.ident, const.mean, const.head, const.col
        W = sb("W", [P, A_END])
        Wsim = sb("Wsim", [P, 512])
        cen = sb("cen", [P, SEQ])
        csq = sb("csq", [P, SEQ])
        lnv_ = sb("lnv", [P, SEQ])
        rstd = sb("rstd", [P, SEQ])
        xn = sb("xn", [P, SEQ])
        QT = sb("QT", [P, 4, SEQ])
        KT = sb("KT", [P, 4, SEQ])
        V = sb("V", [P, TILES, HEADS, 9])
        AT = sb("AT", [P, 2, SPANS])
        sim = sb("sim", [P, TILES, 8, 64])
        sg = sb("sg", [P, TILES, 512])
        m8 = sb("m8", [P, 8, TOP])
        cand = sb("cand", [P, 4, TOP, TOP])
        c8 = sb("c8", [P, 4, TOP])
        nmax = sb("nmax", [P, 4])
        dlt = sb("dlt", [P, 4, TOP])
        ex8 = sb("ex8", [P, 4, TOP])
        Z = sb("Z", [P, 4])
        rZ = sb("rZ", [P, 4])
        penx = sb("penx", [P, 4, TOP])
        peny = sb("peny", [P, 4, 64])
        xm = sb("xm", [P, 4, TOP])
        ym = sb("ym", [P, 4, 64])
        D = sb("D", [P, 4, TOP, 64])
        E = sb("E", [P, 4, 512])
        pacc = sb("pacc", [P, 512])
        tot = sb("tot", [P, 1])
        rest = sb("rest", [P, 1])
        M = sb("M", [P, TILES, 512])
        MT = sb("MT", [P, 4, SEQ])
        den = sb("den", [P, TILES * HEADS])
        rden = sb("rden", [P, TILES * HEADS])
        o = sb("o", [P, TILES * HEADS, 8])
        oT = sb("oT", [P, SEQ])
        gs = sb("gs", [P, 4, SEQ])
        hT = sb("hT", [P, 4, SEQ])
        gate = sb("gate", [P, SEQ])
        sgate = sb("sgate", [P, SEQ])
        B = ctx.enter_context(nc.psum_tensor("a_B", [P, 8, 512], F32))

        PD = 31 * TILES
        w_in = sig("w_in")
        ones_set = sig("ones_set")
        folded = sig("folded")
        wsim_ready = sig("wsim_ready")
        out_done = sig("out_done", 1, 1)
        mean_done = sig("mean_done", 1)
        centred = sig("centred", 1)
        squared = sig("squared", 1)
        var_done = sig("var_done", 1)
        lnv = sig("lnv", 1)
        rstd_ready = sig("rstd_ready", 1)
        xn_ready = sig("xn_ready", 1)
        act_job = sig("act_job", 9)
        act_out = sig("act_out", 9)
        dve_job = sig("dve_job", 8)
        dve_out = sig("dve_out", 8)
        scored = sig("scored", HEADS)
        weighed = sig("weighed", HEADS)
        masked = sig("masked", 2 * HEADS)
        av_done = sig("av_done", HEADS)
        peer = sig("peer", PD)
        ex8_ready = sig("ex8_ready", TILES)
        e_ready = sig("e_ready", TILES)
        d_ready = sig("d_ready", TILES)
        dlt_ready = sig("dlt_ready", TILES)
        m_ready = sig("m_ready", TILES)
        den_ready = sig("den_ready", 2)
        rden_ready = sig("rden_ready", 1)
        o_ready = sig("o_ready", 2)
        gate_done = sig("gate_done", 4)
        gs_ready = sig("gs_ready", 4)
        up_done = sig("up_done", 4)
        h_ready = sig("h_ready", 4)
        oT_done = sig("oT_done", 1)
        oT_ready = sig("oT_ready", 1)
        s_done = sig("s_done", 1)
        mt_done = sig("mt_done", TILES)
        mt_ready = sig("mt_ready", TILES)
        ffn_done = sig("ffn_done", 1)
        gate_ready = sig("gate_ready", 1)
        gated = sig("gated", 1)

        jobs = []
        for b in range(4):
            jobs += [("act", "q", b), ("dve", "k", b)]
        jobs.append(("act", "v", 0))
        for t in range(TILES):
            jobs += [("dve", "sim", t), ("act", "down", t)]
        for_act = [j for j in jobs if j[0] == "act"]
        for_dve = [j for j in jobs if j[0] == "dve"]

        def bank(who, i):
            return B[:, (0 if who == "act" else 3) + i % 3, :]

        with nc.Block() as block:
            @block.sync
            def _(sp):
                sp.dma_start(W[:, :], w_dram).then_inc(w_in.sem, 16)

            @block.gpsimd
            def _(pool):
                nc.gpsimd.memset(V[:, :, :, :], 1.0).then_inc(*ones_set.up())
                both = const.tri.unsqueeze(1).broadcast_to([P, 2, P])
                with pool.Fori(0, seqs) as turn:
                    masked.n = 0
                    for h in range(HEADS):
                        pool.wait_ge(*weighed.nth(h + 1, turn))
                        a = AT[:, h % 2, 0:1024].rearrange("p (i t) -> p i t", i=2)[:, :, 0:P]
                        b = AT[:, h % 2, 896:1152].rearrange("p (i t) -> p i t", i=2)
                        nc.gpsimd.tensor_tensor(a, a, both, ALU.mult).then_inc(*masked.up())
                        nc.gpsimd.tensor_tensor(b, b, both, ALU.mult).then_inc(*masked.up())
                    masked.full()

            @block.scalar
            def _(act):
                nc.scalar.preload_act_table_set("natural_log_exp_and_others")
                act.wait_ge(*folded.nth(2))
                nc.scalar.activation(Wsim[:, 0:256], B[:, 0, 0:256], ACT.Copy).then_inc(*wsim_ready.up())
                nc.scalar.activation(Wsim[:, 256:512], B[:, 1, 0:256], ACT.Copy).then_inc(*wsim_ready.up())
                act.wait_ge(*ones_set.nth(1))

                def routing(t, turn):
                    act.wait_ge(*dlt_ready.nth(t + 1, turn))
                    nc.scalar.activation(ex8[:, :, :], dlt[:, :, :], ACT.Exp).then_inc(*ex8_ready.up())
                    act.wait_ge(*d_ready.nth(t + 1, turn))
                    for h in range(4):
                        mm = nc.scalar.activation(E[:, h, :], D[:, h].rearrange("p a b -> p (a b)"), ACT.Exp, bias=nmax[:, h:h + 1])
                    mm.then_inc(*e_ready.up())

                with act.Fori(0, seqs) as turn:
                    mine = (squared, lnv, rstd_ready, act_out, weighed, ex8_ready, e_ready, gs_ready, oT_ready, mt_ready, gate_ready)
                    for q in mine:
                        q.n = 0
                    act.wait_ge(*centred.nth(1, turn))
                    nc.scalar.activation(csq[:, :], cen[:, :], ACT.Square).then_inc(*squared.up())
                    act.wait_ge(*var_done.nth(1, turn))
                    nc.scalar.activation(lnv_[:, :], B[:, 7, :], ACT.Ln, bias=col["eps5"]).then_inc(*lnv.up())
                    act.wait_ge(*lnv.nth(1, turn))
                    nc.scalar.activation(rstd[:, :], lnv_[:, :], ACT.Exp, scale=-0.5).then_inc(*rstd_ready.up())
                    for i, (_, what, b) in enumerate(for_act):
                        act.wait_ge(*act_job.nth(i + 1, turn))
                        src = bank("act", i)
                        if what == "q":
                            nc.scalar.activation(QT[:, b, :], src, ACT.Copy).then_inc(*act_out.up())
                        elif what == "v":
                            nc.scalar.activation(V[:, :, :, 0:8].rearrange("p t h d -> p (t h) d"),
                                                            src.rearrange("p (a d) -> p a d", d=8), ACT.Copy).then_inc(*act_out.up())
                        else:
                            nc.scalar.activation(sg[:, b, :], src, ACT.Silu).then_inc(*act_out.up())
                    for h in range(HEADS):
                        act.wait_ge(*scored.nth(h + 1, turn))
                        if h >= 2:
                            act.wait_ge(*av_done.nth(h - 1, turn))
                        s = 3 * (h % 2)
                        nc.scalar.activation(AT[:, h % 2, :], B[:, s:s + 3, :].rearrange("p a b -> p (a b)")[:, 0:SPANS],
                                                        ACT.Square, scale=0.25).then_inc(*weighed.up())
                        if h % 4 == 3:
                            routing(h // 4, turn)
                    for c in range(4):
                        act.wait_ge(*gate_done.nth(c + 1, turn))
                        nc.scalar.activation(gs[:, c, :], B[:, c, :], ACT.Silu, bias=W[:, A_BG + c:A_BG + c + 1]).then_inc(*gs_ready.up())
                    act.wait_ge(*oT_done.nth(1, turn))
                    nc.scalar.activation(oT[:, :], B[:, 0, :], ACT.Copy).then_inc(*oT_ready.up())
                    for t in range(TILES):
                        act.wait_ge(*mt_done.nth(t + 1, turn))
                        nc.scalar.activation(MT[:, :, t * TILE:(t + 1) * TILE],
                                                         B[:, 6 + t % 2, :].rearrange("p (b t) -> p b t", b=4), ACT.Copy).then_inc(*mt_ready.up())
                    act.wait_ge(*ffn_done.nth(1, turn))
                    nc.scalar.activation(sgate[:, :], B[:, 2, :], ACT.Silu, bias=W[:, A_BD:A_BD + 1]).then_inc(*gate_ready.up())
                    for q in mine:
                        q.full()

            @block.tensor
            def _(pe):
                pe.wait_ge(w_in.sem, 16)
                for p in range(2):
                    r = slice(64 * p, 64 * p + 64)
                    for h in range(4):
                        mm = nc.tensor.matmul(B[:, p, h * 64:(h + 1) * 64], W[r, A_WQT + h * P:A_WQT + (h + 1) * P],
                                              W[r, A_KEYS + h * 64:A_KEYS + (h + 1) * 64], start=True, stop=True)
                    mm.then_inc(*folded.up())
                pe.wait_ge(*wsim_ready.nth(2))
                with pe.Fori(0, seqs) as turn:
                    mine = (mean_done, var_done, act_job, dve_job, scored, av_done, gate_done, up_done, oT_done, s_done, mt_done, ffn_done)
                    for q in mine:
                        q.n = 0
                    xin = x[:, bass.ds(turn * SEQ, SEQ)]
                    pe.wait_ge(*out_done.nth(0, turn))
                    nc.tensor.matmul(B[:, 6, :], ones_mean, xin, start=True, stop=True).then_inc(*mean_done.up())
                    pe.wait_ge(*squared.nth(1, turn))
                    nc.tensor.matmul(B[:, 7, :], ones_mean, csq[:, :], start=True, stop=True).then_inc(*var_done.up())
                    pe.wait_ge(*xn_ready.nth(1, turn))
                    n_act = n_dve = 0
                    for who, what, b in jobs:
                        if who == "act":
                            if n_act >= 3:
                                pe.wait_ge(*act_out.nth(n_act - 2, turn))
                            dst = bank(who, n_act)
                            n_act += 1
                        else:
                            if n_dve >= 3:
                                pe.wait_ge(*dve_out.nth(n_dve - 2, turn))
                            dst = bank(who, n_dve)
                            n_dve += 1
                        tok = slice(b * TILE, (b + 1) * TILE)
                        if what in "qk":
                            c = (A_Q if what == "q" else A_K) + b * P
                            mm = nc.tensor.matmul(dst, W[:, c:c + P], xn[:, :], start=True, stop=True)
                        elif what == "v":
                            for t in range(TILES):
                                mm = nc.tensor.matmul(dst[:, t * P:(t + 1) * P], xn[:, t * TILE:(t + 1) * TILE], W[:, A_V:A_V + P],
                                                      start=True, stop=True)
                        elif what == "sim":
                            mm = nc.tensor.matmul(dst, xn[:, tok], Wsim[:, :], start=True, stop=True)
                        else:
                            mm = nc.tensor.matmul(dst, xn[:, tok], W[:, A_DOWN:A_DOWN + 512], start=True, stop=True)
                        mm.then_inc(*(act_job if who == "act" else dve_job).up())

                    def head_scores(h):
                        if h < 2:
                            pe.wait_ge(*act_out.nth(9, turn))
                            pe.wait_ge(*dve_out.nth(8, turn))
                        else:
                            pe.wait_ge(*weighed.nth(h - 1, turn))
                        r = slice(32 * (h % 4), 32 * (h % 4) + 32)
                        flat = B[:, 3 * (h % 2):3 * (h % 2) + 3, :].rearrange("p a b -> p (a b)")
                        for i in range(TILES):
                            n = SEQ - i * TILE
                            mm = nc.tensor.matmul(flat[:, SPAN[i]:SPAN[i] + n], KT[r, h // 4, i * TILE:(i + 1) * TILE],
                                                  QT[r, h // 4, i * TILE:SEQ], start=True, stop=True)
                        mm.then_inc(*scored.up())

                    def head_values(h):
                        pe.wait_ge(*masked.nth(2 * h + 2, turn))
                        for t in range(TILES):
                            dst = B[:, 6 + t // 2, (t % 2) * 144 + h * 9:(t % 2) * 144 + h * 9 + 9]
                            for i in range(t + 1):
                                a = SPAN[i] + (t - i) * TILE
                                mm = nc.tensor.matmul(dst, AT[:, h % 2, a:a + TILE], V[:, i, h, :], start=i == 0, stop=i == t)
                        mm.then_inc(*av_done.up())

                    for h in range(HEADS):
                        head_scores(h)
                        if h:
                            head_values(h - 1)
                    head_values(HEADS - 1)
                    pe.wait_ge(*weighed.nth(HEADS, turn))
                    for c in range(4):
                        nc.tensor.matmul(B[:, c, :], W[:, A_G + c * P:A_G + (c + 1) * P], xn[:, :], start=True, stop=True).then_inc(*gate_done.up())
                    for c in range(4):
                        if c >= 2:
                            pe.wait_ge(*h_ready.nth(c - 1, turn))
                        nc.tensor.matmul(B[:, 4 + c % 2, :], W[:, A_U + c * P:A_U + (c + 1) * P], xn[:, :], start=True, stop=True).then_inc(*up_done.up())
                    pe.wait_ge(*o_ready.nth(2, turn))
                    pe.wait_ge(*gs_ready.nth(4, turn))
                    for t in range(TILES):
                        mm = nc.tensor.transpose(B[:, 0, t * TILE:(t + 1) * TILE],
                                                 o[:, t * HEADS:(t + 1) * HEADS, :].rearrange("p h d -> p (h d)"), ident)
                    mm.then_inc(*oT_done.up())
                    pe.wait_ge(*oT_ready.nth(1, turn))
                    nc.tensor.matmul(B[:, 1, :], W[:, A_O:A_O + P], oT[:, :], start=True, stop=True).then_inc(*s_done.up())
                    for t in range(TILES):
                        pe.wait_ge(*m_ready.nth(t + 1, turn))
                        if t >= 2:
                            pe.wait_ge(*mt_ready.nth(t - 1, turn))
                        for b in range(4):
                            mm = nc.tensor.transpose(B[:, 6 + t % 2, b * P:(b + 1) * P], M[:, t, b * P:(b + 1) * P], ident)
                        mm.then_inc(*mt_done.up())
                    pe.wait_ge(*h_ready.nth(4, turn))
                    for c in range(4):
                        nc.tensor.matmul(B[:, 2, :], W[:, A_D + c * P:A_D + (c + 1) * P], hT[:, c, :], start=c == 0, stop=False)
                    pe.wait_ge(*mt_ready.nth(4, turn))
                    for b in range(4):
                        mm = nc.tensor.matmul(B[:, 2, :], W[:, A_UP + b * P:A_UP + (b + 1) * P], MT[:, b, :], start=False, stop=b == 3)
                    mm.then_inc(*ffn_done.up())
                    for q in mine:
                        q.full()

            @block.vector
            def _(dve):
                def route(t, turn):
                    for g in range(8):
                        nc.vector.max(m8[:, g, :], sim[:, t, g, :]).then_inc(*peer.up())
                    dve.wait_ge(*peer.last(turn))
                    mx_, my_ = m8[:, 0:4, :], m8[:, 4:8, :]
                    nc.vector.tensor_tensor(cand[:, :, :, :], mx_.unsqueeze(3).broadcast_to([P, 4, TOP, TOP]),
                                                    my_.unsqueeze(2).broadcast_to([P, 4, TOP, TOP]), ALU.add).then_inc(*peer.up())
                    thx = m8[:, 0:4, 7:8].broadcast_to([P, 4, TOP])
                    thy = m8[:, 4:8, 7:8].broadcast_to([P, 4, 64])
                    nc.vector.tensor_tensor(penx[:, :, :], sim[:, t, 0:4, 0:TOP], thx, ALU.is_lt).then_inc(*peer.up())
                    nc.vector.tensor_tensor(peny[:, :, :], sim[:, t, 4:8, :], thy, ALU.is_lt).then_inc(*peer.up())
                    dve.wait_ge(*peer.last(turn))
                    nc.vector.scalar_tensor_tensor(out=xm[:, :, :], in0=penx[:, :, :], scalar=-BIG, in1=sim[:, t, 0:4, 0:TOP],
                                                           op0=ALU.mult, op1=ALU.add).then_inc(*peer.up())
                    nc.vector.scalar_tensor_tensor(out=ym[:, :, :], in0=peny[:, :, :], scalar=-BIG, in1=sim[:, t, 4:8, :],
                                                           op0=ALU.mult, op1=ALU.add).then_inc(*peer.up())
                    for h in range(4):
                        nc.vector.max(c8[:, h, :], cand[:, h].rearrange("p a b -> p (a b)")).then_inc(*peer.up())
                    dve.wait_ge(*peer.last(turn))
                    if t:
                        dve.wait_ge(*e_ready.nth(t, turn))
                    nc.vector.tensor_scalar(nmax[:, :], c8[:, :, 0], -1.0, None, ALU.mult).then_inc(*peer.up())
                    dve.wait_ge(*peer.last(turn))
                    nc.vector.tensor_tensor(dlt[:, :, :], c8[:, :, :], nmax[:, :].unsqueeze(2).broadcast_to([P, 4, TOP]), ALU.add).then_inc(*dlt_ready.up())
                    nc.vector.tensor_tensor(D[:, :, :, :], xm[:, :, :].unsqueeze(3).broadcast_to([P, 4, TOP, 64]),
                                                       ym[:, :, :].unsqueeze(2).broadcast_to([P, 4, TOP, 64]), ALU.add).then_inc(*d_ready.up())
                    dve.wait_ge(*ex8_ready.nth(t + 1, turn))
                    nc.vector.tensor_reduce(Z[:, :], ex8[:, :, :], AX.X, ALU.add).then_inc(*peer.up())
                    dve.wait_ge(*peer.last(turn))
                    nc.vector.reciprocal(rZ[:, :], Z[:, :]).then_inc(*peer.up())
                    dve.wait_ge(*e_ready.nth(t + 1, turn))
                    for h in range(4):
                        mm = nc.vector.scalar_tensor_tensor(out=E[:, h, :], in0=D[:, h].rearrange("p a b -> p (a b)"), scalar=c8[:, h, 7:8],
                                                            in1=E[:, h, :], op0=ALU.is_ge, op1=ALU.mult)
                        mm.then_inc(*peer.up())
                    dve.wait_ge(*peer.last(turn))
                    nc.vector.tensor_scalar(pacc[:, :], E[:, 0, :], rZ[:, 0:1], None, ALU.mult).then_inc(*peer.up())
                    for h in range(1, 4):
                        dve.wait_ge(*peer.last(turn))
                        nc.vector.scalar_tensor_tensor(out=pacc[:, :], in0=E[:, h, :], scalar=rZ[:, h:h + 1], in1=pacc[:, :],
                                                               op0=ALU.mult, op1=ALU.add).then_inc(*peer.up())
                    dve.wait_ge(*peer.last(turn))
                    nc.vector.tensor_reduce(tot[:, :], pacc[:, :], AX.X, ALU.add).then_inc(*peer.up())
                    dve.wait_ge(*peer.last(turn))
                    nc.vector.tensor_scalar(rest[:, :], tot[:, :], -1.0, 4.0, ALU.mult, ALU.add).then_inc(*peer.up())
                    dve.wait_ge(*peer.last(turn))
                    nc.vector.tensor_tensor(pacc[:, 511:512], pacc[:, 511:512], rest[:, :], ALU.add).then_inc(*peer.up())
                    dve.wait_ge(*peer.last(turn))
                    nc.vector.tensor_tensor(M[:, t, :], pacc[:, :], sg[:, t, :], ALU.mult).then_inc(*m_ready.up())

                nc.vector.memset(tot[:, :], 0.0).then_inc(*out_done.prime())
                with dve.Fori(0, seqs) as turn:
                    mine = (centred, xn_ready, dve_out, d_ready, dlt_ready, m_ready, den_ready, rden_ready, o_ready, h_ready, gated, out_done)
                    for q in mine + (peer,):
                        q.n = 0
                    xin = x[:, bass.ds(turn * SEQ, SEQ)]
                    dve.wait_ge(*mean_done.nth(1, turn))
                    nc.vector.tensor_tensor(cen[:, :], xin, B[:, 6, :], ALU.subtract).then_inc(*centred.up())
                    dve.wait_ge(*rstd_ready.nth(1, turn))
                    nc.vector.tensor_tensor(xn[:, :], cen[:, :], rstd[:, :], ALU.mult).then_inc(*xn_ready.up())
                    for i, (_, what, b) in enumerate(for_dve):
                        dve.wait_ge(*dve_job.nth(i + 1, turn))
                        dst = KT[:, b, :] if what == "k" else sim[:, b].rearrange("p g k -> p (g k)")
                        nc.vector.tensor_copy(dst, bank("dve", i)).then_inc(*dve_out.up())
                    dve.wait_ge(*dve_out.nth(8, turn))
                    dve.wait_ge(*act_out.nth(9, turn))
                    nc.vector.memset(tot[:, :], 0.0)
                    for t in range(TILES):
                        route(t, turn)
                    dve.wait_ge(*av_done.nth(HEADS, turn))
                    O = [B[:, 6 + b, 0:288].rearrange("p (a d) -> p a d", d=9) for b in range(2)]
                    for b in range(2):
                        nc.vector.tensor_scalar(den[:, 32 * b:32 * b + 32], O[b][:, :, 8], 1e-5, None, ALU.add).then_inc(*den_ready.up())
                    dve.wait_ge(*den_ready.nth(2, turn))
                    nc.vector.reciprocal(rden[:, :], den[:, :]).then_inc(*rden_ready.up())
                    dve.wait_ge(*rden_ready.nth(1, turn))
                    for b in range(2):
                        nc.vector.tensor_tensor(o[:, 32 * b:32 * b + 32, :], O[b][:, :, 0:8],
                                                           rden[:, 32 * b:32 * b + 32].unsqueeze(2).broadcast_to([P, 32, 8]), ALU.mult).then_inc(*o_ready.up())
                    for c in range(4):
                        dve.wait_ge(*up_done.nth(c + 1, turn))
                        dve.wait_ge(*gs_ready.nth(c + 1, turn))
                        nc.vector.scalar_tensor_tensor(out=hT[:, c, :], in0=B[:, 4 + c % 2, :], scalar=W[:, A_BU + c:A_BU + c + 1],
                                                                  in1=gs[:, c, :], op0=ALU.add, op1=ALU.mult).then_inc(*h_ready.up())
                    dve.wait_ge(*gate_ready.nth(1, turn))
                    nc.vector.tensor_tensor(gate[:, :], B[:, 1, :], sgate[:, :], ALU.mult).then_inc(*gated.up())
                    dve.wait_ge(*gated.nth(1, turn))
                    nc.vector.tensor_tensor(xin, xin, gate[:, :], ALU.add).then_inc(*out_done.up())
                    for q in mine:
                        q.full()
                    peer.full()


STATES, EXPERTS, HID = 64, 4, 512
B_IN = 0
B_DT = B_IN + 512
B_BP = B_DT + 2 * STATES
B_CP = B_BP + 2 * STATES
B_OUT = B_CP + 2 * STATES
B_GW = B_OUT + 2 * P
B_W1 = B_GW + EXPERTS
B_W2 = B_W1 + EXPERTS * HID
B_S2I = B_W2 + EXPERTS * 4 * P
B_B2 = B_S2I + 2 * P
B_GB = B_B2 + P
B_LT = B_GB + TILES * EXPERTS
B_SEL = B_LT + TILES * EXPERTS * EXPERTS
B_P = B_SEL + EXPERTS * P
BP = {"inb": 0, "conv": 4, "convb": 10, "dtb": 12, "bpb": 13, "cpb": 14, "s2ib": 15, "D": 17, "outb": 19, "n1": 20, "n2": 21, "b1": 22}
B_END = B_P + 22 + EXPERTS * 4


def level1(nc, x, xf, s1, w_dram, const, seqs):
    with ExitStack() as ctx:
        def sb(name, shape, dt=F32):
            return ctx.enter_context(nc.sbuf_tensor("b_" + name, shape, dt))

        def sig(name, per=0, primed=0):
            return Signal(ctx.enter_context(nc.semaphore("b_" + name)), per, primed)

        ident, ones_mean, ones_head, col = const.ident, const.mean, const.head, const.col
        T = [P, SEQ]
        W = sb("W", [P, B_END])
        cen, csq, lns, rstd, xn, nr, h1 = (sb(n, T) for n in ("cen", "csq", "lns", "rstd", "xn", "nr", "h1"))
        xc = sb("xc", [P, 2, 2 + SEQ])
        ca = sb("ca", [P, 2, SEQ])
        cb = sb("cb", [P, 2, SEQ])
        sgt = sb("sgt", [P, 2, SEQ])
        xm = sb("xm", [P, 2, SEQ])
        S = [STATES, SEQ]
        dt_, omd, db, st, y, yc, ysq, yln, yrs, yn = (sb(n, S) for n in ("dt", "omd", "db", "st", "y", "yc", "ysq", "yln", "yrs", "yn"))
        u1 = sb("u1", [P, 2, SEQ])
        u2 = sb("u2", [P, 2, SEQ])
        x2, x2sq, nr2, h2 = (sb(n, T) for n in ("x2", "x2sq", "nr2", "h2"))
        TE = TILES * EXPERTS
        lg, ls, ex, exs, rank, sel, wt = (sb(n, [P, TE]) for n in ("lg", "ls", "ex", "exs", "rank", "sel", "wt"))
        mxl, zz, rz = (sb(n, [P, TILES]) for n in ("mxl", "zz", "rz"))
        gt, eq = (sb(n, [P, TE, EXPERTS]) for n in ("gt", "eq"))
        wT = sb("wT", [EXPERTS, SEQ])
        spare = sb("spare", [P, 1])
        gl = sb("gl", [P, 3, SEQ])
        wb = sb("wb", [P, EXPERTS, SEQ])
        hw = sb("hw", [P, 3, SEQ])
        B = ctx.enter_context(nc.psum_tensor("b_B", [P, 8, 512], F32))

        def par(name, k=0, rows=P):
            c = B_P + BP[name] + k
            return W[0:rows, c:c + 1]

        NK = EXPERTS * 4
        w_in = sig("w_in")
        zeroed = sig("zeroed")
        out_done = sig("out_done", 1, 1)
        sums = sig("sums", 6)
        sq_ready = sig("sq_ready", 4)
        lnd = sig("lnd", 4)
        inv = sig("inv", 4)
        cen_ready = sig("cen_ready", 2)
        xn_ready = sig("xn_ready", 1)
        xf_ready = sig("xf_ready", 1, 1)
        n_ready = sig("n_ready", 4)
        in_done = sig("in_done", 4)
        xc_ready = sig("xc_ready", 2)
        gates = sig("gates", 2)
        conv = sig("conv", 6)
        xm_ready = sig("xm_ready", 2)
        dbc = sig("dbc", 3)
        dt_ready = sig("dt_ready", 1)
        ssm = sig("ssm", 5)
        s2i = sig("s2i", 2)
        u_ready = sig("u_ready", 4)
        out_p = sig("out_p", 1)
        x2_ready = sig("x2_ready", 1)
        logits = sig("logits", 1)
        ls_ready = sig("ls_ready", 1)
        route = sig("route", 10)
        ex_ready = sig("ex_ready", 1)
        wt_done = sig("wt_done", 1)
        wT_ready = sig("wT_ready", 1)
        wb_done = sig("wb_done", EXPERTS)
        wb_ready = sig("wb_ready", EXPERTS)
        hid = sig("hid", NK)
        gelus = sig("gelus", NK)
        hw_ready = sig("hw_ready", NK)
        eo_used = sig("eo_used", NK)
        step = sig("step", 1)

        with nc.Block() as block:
            @block.sync
            def _(sp):
                sp.dma_start(W[:, :], w_dram).then_inc(w_in.sem, 16)

            @block.gpsimd
            def _(pool):
                nc.gpsimd.memset(xc[:, :, 0:2], 0.0).then_inc(*zeroed.up())
                nc.gpsimd.memset(spare[:, :], 0.0).then_inc(*xf_ready.prime())
                nc.gpsimd.memset(xf[:, :].rearrange("p (s t) -> p s t", s=seqs)[:, :, 0:1], 0.0).then_inc(*zeroed.up())
                with pool.Fori(0, seqs) as turn:
                    xf_ready.n = 0
                    pool.wait_ge(*xn_ready.nth(1, turn))
                    nc.gpsimd.tensor_copy(xf[:, bass.ds(turn * (SEQ + 1) + 1, SEQ)], xn[:, :]).then_inc(*xf_ready.up())
                    xf_ready.full()

            @block.scalar
            def _(act):
                nc.scalar.preload_act_table_set("natural_log_exp_and_others")
                act.wait_ge(w_in.sem, 16)
                with act.Fori(0, seqs) as turn:
                    mine = (sq_ready, lnd, inv, gates, xm_ready, dt_ready, ex_ready, gelus)
                    for q in mine:
                        q.n = 0

                    def inverse_root(out, ln_out, src, eps, n):
                        act.wait_ge(*sums.nth(n, turn))
                        nc.scalar.activation(ln_out, src, ACT.Ln, bias=eps).then_inc(*lnd.up())
                        act.wait_ge(*lnd.last(turn))
                        nc.scalar.activation(out, ln_out, ACT.Exp, scale=-0.5).then_inc(*inv.up())

                    act.wait_ge(*cen_ready.nth(1, turn))
                    nc.scalar.activation(csq[:, :], cen[:, :], ACT.Square).then_inc(*sq_ready.up())
                    inverse_root(rstd[:, :], lns[:, :], B[:, 1, :], col["eps5"], 2)
                    act.wait_ge(*xn_ready.nth(1, turn))
                    nc.scalar.activation(csq[:, :], xn[:, :], ACT.Square).then_inc(*sq_ready.up())
                    act.wait_ge(*inv.nth(1, turn))
                    inverse_root(nr[:, :], lns[:, :], B[:, 2, :], col["eps6"], 3)
                    for b in range(2):
                        act.wait_ge(*in_done.nth(3 + b, turn))
                        nc.scalar.activation(sgt[:, b, :], B[:, 5 + b, :], ACT.Sigmoid, bias=par("inb", 2 + b)).then_inc(*gates.up())
                    for b in range(2):
                        act.wait_ge(*conv.nth(3 * b + 3, turn))
                        nc.scalar.activation(xm[:, b, :], ca[:, b, :], ACT.Silu, bias=par("convb", b)).then_inc(*xm_ready.up())
                    act.wait_ge(*dbc.nth(1, turn))
                    nc.scalar.activation(dt_[:, :], B[0:STATES, 0, :], ACT.Sigmoid, bias=par("dtb", 0, STATES)).then_inc(*dt_ready.up())
                    act.wait_ge(*cen_ready.nth(2, turn))
                    nc.scalar.activation(ysq[:, :], yc[:, :], ACT.Square).then_inc(*sq_ready.up())
                    inverse_root(yrs[:, :], yln[:, :], B[0:STATES, 4, :], col["eps5"][0:STATES, :], 5)
                    act.wait_ge(*x2_ready.nth(1, turn))
                    nc.scalar.activation(x2sq[:, :], x2[:, :], ACT.Square).then_inc(*sq_ready.up())
                    inverse_root(nr2[:, :], lns[:, :], B[:, 0, :], col["eps6"], 6)
                    act.wait_ge(*ls_ready.nth(1, turn))
                    nc.scalar.activation(ex[:, :], ls[:, :], ACT.Exp).then_inc(*ex_ready.up())
                    for k in range(NK):
                        act.wait_ge(*hid.nth(k + 1, turn))
                        if k >= 3:
                            act.wait_ge(*hw_ready.nth(k - 2, turn))
                        nc.scalar.activation(gl[:, k % 3, :], B[:, k % 3, :], ACT.Gelu, bias=par("b1", k)).then_inc(*gelus.up())
                    for q in mine:
                        q.full()

            @block.tensor
            def _(pe):
                pe.wait_ge(w_in.sem, 16)
                with pe.Fori(0, seqs) as turn:
                    mine = (sums, in_done, dbc, s2i, out_p, logits, wt_done, wb_done, hid, eo_used)
                    for q in mine:
                        q.n = 0
                    mean_s = const.mean64
                    pe.wait_ge(*out_done.nth(0, turn))
                    nc.tensor.matmul(B[:, 0, :], ones_mean, x[:, bass.ds(turn * SEQ, SEQ)], start=True, stop=True).then_inc(*sums.up())
                    pe.wait_ge(*sq_ready.nth(1, turn))
                    nc.tensor.matmul(B[:, 1, :], ones_mean, csq[:, :], start=True, stop=True).then_inc(*sums.up())
                    pe.wait_ge(*sq_ready.nth(2, turn))
                    nc.tensor.matmul(B[:, 2, :], ones_mean, csq[:, :], start=True, stop=True).then_inc(*sums.up())
                    pe.wait_ge(*n_ready.nth(2, turn))
                    for b in range(4):
                        nc.tensor.matmul(B[:, 3 + b, :], W[:, B_IN + b * P:B_IN + (b + 1) * P], h1[:, :], start=True, stop=True).then_inc(*in_done.up())
                    pe.wait_ge(*xm_ready.nth(2, turn))
                    for i, c in enumerate((B_DT, B_BP, B_CP)):
                        for b in range(2):
                            mm = nc.tensor.matmul(B[0:STATES, i, :], W[:, c + b * STATES:c + (b + 1) * STATES], xm[:, b, :], start=b == 0, stop=b == 1)
                        mm.then_inc(*dbc.up())
                    pe.wait_ge(*ssm.nth(4, turn))
                    nc.tensor.matmul(B[:, 3, :], mean_s, y[:, :], start=True, stop=True).then_inc(*sums.up())
                    pe.wait_ge(*sq_ready.nth(3, turn))
                    nc.tensor.matmul(B[:, 4, :], mean_s, ysq[:, :], start=True, stop=True).then_inc(*sums.up())
                    pe.wait_ge(*ssm.nth(5, turn))
                    for b in range(2):
                        nc.tensor.matmul(B[:, 5 + b, :], W[0:STATES, B_S2I + b * P:B_S2I + (b + 1) * P], yn[:, :], start=True, stop=True).then_inc(*s2i.up())
                    pe.wait_ge(*u_ready.nth(4, turn))
                    for b in range(2):
                        mm = nc.tensor.matmul(B[:, 7, :], W[:, B_OUT + b * P:B_OUT + (b + 1) * P], u2[:, b, :], start=b == 0, stop=b == 1)
                    mm.then_inc(*out_p.up())
                    pe.wait_ge(*sq_ready.nth(4, turn))
                    nc.tensor.matmul(B[:, 0, :], ones_mean, x2sq[:, :], start=True, stop=True).then_inc(*sums.up())
                    pe.wait_ge(*n_ready.nth(4, turn))
                    for t in range(TILES):
                        mm = nc.tensor.matmul(B[:, 1, t * EXPERTS:(t + 1) * EXPERTS], h2[:, t * TILE:(t + 1) * TILE], W[:, B_GW:B_GW + EXPERTS],
                                              start=True, stop=True)
                    mm.then_inc(*logits.up())
                    pe.wait_ge(*route.nth(10, turn))
                    for t in range(TILES):
                        mm = nc.tensor.transpose(B[0:EXPERTS, 2, t * TILE:(t + 1) * TILE], wt[:, t * EXPERTS:(t + 1) * EXPERTS], ident)
                    mm.then_inc(*wt_done.up())
                    pe.wait_ge(*wT_ready.nth(1, turn))
                    nc.tensor.matmul(B[:, 7, :], W[0:EXPERTS, B_B2:B_B2 + P], wT[:, :], start=True, stop=False, skip_group_check=True)
                    for e in range(EXPERTS):
                        nc.tensor.matmul(B[:, 3 + e, :], W[0:EXPERTS, B_SEL + e * P:B_SEL + (e + 1) * P], wT[:, :], start=True, stop=True).then_inc(*wb_done.up())

                    def result(k):
                        pe.wait_ge(*hw_ready.nth(k + 1, turn))
                        nc.tensor.matmul(B[:, 7, :], W[:, B_W2 + k * P:B_W2 + (k + 1) * P], hw[:, k % 3, :],
                                                    start=False, stop=k == NK - 1, skip_group_check=True).then_inc(*eo_used.up())

                    for k in range(NK):
                        if k >= 3:
                            pe.wait_ge(*gelus.nth(k - 2, turn))
                        nc.tensor.matmul(B[:, k % 3, :], W[:, B_W1 + k * P:B_W1 + (k + 1) * P], h2[:, :], start=True, stop=True).then_inc(*hid.up())
                        if k >= 2:
                            result(k - 2)
                    result(NK - 2)
                    result(NK - 1)
                    for q in mine:
                        q.full()

            @block.vector
            def _(dve):
                nc.vector.memset(rz[:, :], 0.0).then_inc(*out_done.prime())
                dve.wait_ge(w_in.sem, 16)
                dve.wait_ge(*zeroed.nth(2))
                TT, STT, TSC = nc.vector.tensor_tensor, nc.vector.scalar_tensor_tensor, nc.vector.tensor_scalar
                with dve.Fori(0, seqs) as turn:
                    mine = (cen_ready, xn_ready, n_ready, xc_ready, conv, ssm, u_ready, x2_ready, ls_ready, route, wT_ready, wb_ready,
                            hw_ready, out_done)
                    for q in mine:
                        q.n = 0
                    dve.wait_ge(*sums.nth(1, turn))
                    TT(cen[:, :], x[:, bass.ds(turn * SEQ, SEQ)], B[:, 0, :], ALU.subtract).then_inc(*cen_ready.up())
                    dve.wait_ge(*inv.nth(1, turn))
                    dve.wait_ge(*xf_ready.nth(0, turn))
                    TT(xn[:, :], cen[:, :], rstd[:, :], ALU.mult).then_inc(*xn_ready.up())
                    dve.wait_ge(*xn_ready.nth(1, turn))
                    TSC(h1[:, :], xn[:, :], par("n1"), None, ALU.mult).then_inc(*n_ready.up())
                    dve.wait_ge(*n_ready.nth(1, turn))
                    dve.wait_ge(*inv.nth(2, turn))
                    TT(h1[:, :], h1[:, :], nr[:, :], ALU.mult).then_inc(*n_ready.up())
                    for b in range(2):
                        dve.wait_ge(*in_done.nth(b + 1, turn))
                        TSC(xc[:, b, 2:], B[:, 3 + b, :], par("inb", b), None, ALU.add).then_inc(*xc_ready.up())
                    for b in range(2):
                        dve.wait_ge(*xc_ready.nth(b + 1, turn))
                        TSC(ca[:, b, :], xc[:, b, 2:], par("conv", 3 * b + 2), None, ALU.mult).then_inc(*conv.up())
                        dve.wait_ge(*conv.last(turn))
                        STT(out=cb[:, b, :], in0=xc[:, b, 1:1 + SEQ], scalar=par("conv", 3 * b + 1), in1=ca[:, b, :], op0=ALU.mult, op1=ALU.add).then_inc(*conv.up())
                        dve.wait_ge(*conv.last(turn))
                        STT(out=ca[:, b, :], in0=xc[:, b, 0:SEQ], scalar=par("conv", 3 * b), in1=cb[:, b, :], op0=ALU.mult, op1=ALU.add).then_inc(*conv.up())
                    dve.wait_ge(*dt_ready.nth(1, turn))
                    TSC(omd[:, :], dt_[:, :], -1.0, 1.0, ALU.mult, ALU.add).then_inc(*ssm.up())
                    dve.wait_ge(*dbc.nth(3, turn))
                    STT(out=db[:, :], in0=B[0:STATES, 1, :], scalar=par("bpb", 0, STATES), in1=dt_[:, :], op0=ALU.add, op1=ALU.mult).then_inc(*ssm.up())
                    dve.wait_ge(*ssm.last(turn))
                    nc.vector.tensor_tensor_scan(st[:, :], omd[:, :], db[:, :], 0.0, ALU.mult, ALU.add).then_inc(*ssm.up())
                    dve.wait_ge(*ssm.last(turn))
                    STT(out=y[:, :], in0=B[0:STATES, 2, :], scalar=par("cpb", 0, STATES), in1=st[:, :], op0=ALU.add, op1=ALU.mult).then_inc(*ssm.up())
                    dve.wait_ge(*ssm.last(turn))
                    dve.wait_ge(*sums.nth(4, turn))
                    TT(yc[:, :], y[:, :], B[0:STATES, 3, :], ALU.subtract).then_inc(*cen_ready.up())
                    dve.wait_ge(*cen_ready.nth(2, turn))
                    dve.wait_ge(*inv.nth(3, turn))
                    TT(yn[:, :], yc[:, :], yrs[:, :], ALU.mult).then_inc(*ssm.up())
                    for b in range(2):
                        dve.wait_ge(*s2i.nth(b + 1, turn))
                        dve.wait_ge(*gates.nth(b + 1, turn))
                        STT(out=u1[:, b, :], in0=xm[:, b, :], scalar=par("D", b), in1=B[:, 5 + b, :], op0=ALU.mult, op1=ALU.add).then_inc(*u_ready.up())
                        dve.wait_ge(*u_ready.last(turn))
                        STT(out=u2[:, b, :], in0=u1[:, b, :], scalar=par("s2ib", b), in1=sgt[:, b, :], op0=ALU.add, op1=ALU.mult).then_inc(*u_ready.up())
                    dve.wait_ge(*out_p.nth(1, turn))
                    STT(out=x2[:, :], in0=B[:, 7, :], scalar=par("outb"), in1=xn[:, :], op0=ALU.add, op1=ALU.add).then_inc(*x2_ready.up())
                    dve.wait_ge(*x2_ready.nth(1, turn))
                    TSC(h2[:, :], x2[:, :], par("n2"), None, ALU.mult).then_inc(*n_ready.up())
                    dve.wait_ge(*n_ready.nth(3, turn))
                    dve.wait_ge(*inv.nth(4, turn))
                    TT(h2[:, :], h2[:, :], nr2[:, :], ALU.mult).then_inc(*n_ready.up())
                    dve.wait_ge(*logits.nth(1, turn))
                    TT(lg[:, :], B[:, 1, 0:TE], W[:, B_GB:B_GB + TE], ALU.add).then_inc(*route.up())
                    dve.wait_ge(*route.last(turn))
                    lt = lg[:, :].rearrange("p (t e) -> p t e", t=TILES)
                    for t in range(TILES):
                        other = lg[:, t * EXPERTS:(t + 1) * EXPERTS].unsqueeze(1).broadcast_to([P, EXPERTS, EXPERTS])
                        own = lg[:, t * EXPERTS:(t + 1) * EXPERTS].unsqueeze(2).broadcast_to([P, EXPERTS, EXPERTS])
                        rows = slice(t * EXPERTS, (t + 1) * EXPERTS)
                        nc.vector.tensor_tensor(gt[:, rows, :], other, own, ALU.is_gt)
                        mm = nc.vector.tensor_tensor(eq[:, rows, :], other, own, ALU.is_equal)
                    mm.then_inc(*route.up())
                    nc.vector.tensor_reduce(mxl[:, :], lt, AX.X, ALU.max).then_inc(*route.up())
                    dve.wait_ge(*route.last(turn))
                    TT(ls[:, :].rearrange("p (t e) -> p t e", t=TILES), lt, mxl[:, :].unsqueeze(2).broadcast_to([P, TILES, EXPERTS]), ALU.subtract).then_inc(*ls_ready.up())
                    flat = lambda a: a.rearrange("p a b -> p (a b)")
                    TT(flat(eq[:, :, :]), flat(eq[:, :, :]), W[:, B_LT:B_LT + TE * EXPERTS], ALU.mult).then_inc(*route.up())
                    dve.wait_ge(*route.last(turn))
                    TT(flat(gt[:, :, :]), flat(gt[:, :, :]), flat(eq[:, :, :]), ALU.add).then_inc(*route.up())
                    dve.wait_ge(*route.last(turn))
                    nc.vector.tensor_reduce(rank[:, :], gt[:, :, :], AX.X, ALU.add).then_inc(*route.up())
                    dve.wait_ge(*route.last(turn))
                    dve.wait_ge(*ex_ready.nth(1, turn))
                    STT(out=exs[:, :], in0=rank[:, :], scalar=2.0, in1=ex[:, :], op0=ALU.is_lt, op1=ALU.mult).then_inc(*route.up())
                    dve.wait_ge(*route.last(turn))
                    nc.vector.tensor_reduce(zz[:, :], exs[:, :].rearrange("p (t e) -> p t e", t=TILES), AX.X, ALU.add).then_inc(*route.up())
                    dve.wait_ge(*route.last(turn))
                    nc.vector.reciprocal(rz[:, :], zz[:, :]).then_inc(*route.up())
                    dve.wait_ge(*route.last(turn))
                    TT(wt[:, :].rearrange("p (t e) -> p t e", t=TILES), exs[:, :].rearrange("p (t e) -> p t e", t=TILES),
                                rz[:, :].unsqueeze(2).broadcast_to([P, TILES, EXPERTS]), ALU.mult).then_inc(*route.up())
                    dve.wait_ge(*wt_done.nth(1, turn))
                    nc.vector.tensor_copy(wT[:, :], B[0:EXPERTS, 2, :]).then_inc(*wT_ready.up())
                    for e in range(EXPERTS):
                        dve.wait_ge(*wb_done.nth(e + 1, turn))
                        nc.vector.tensor_copy(wb[:, e, :], B[:, 3 + e, :]).then_inc(*wb_ready.up())
                    dve.wait_ge(*wb_ready.nth(EXPERTS, turn))
                    for k in range(NK):
                        dve.wait_ge(*gelus.nth(k + 1, turn))
                        if k >= 3:
                            dve.wait_ge(*eo_used.nth(k - 2, turn))
                        TT(hw[:, k % 3, :], gl[:, k % 3, :], wb[:, k // 4, :], ALU.mult).then_inc(*hw_ready.up())
                    dve.wait_ge(*eo_used.nth(NK, turn))
                    TT(s1[:, bass.ds(turn * SEQ, SEQ)], x2[:, :], B[:, 7, :], ALU.add).then_inc(*out_done.up())
                    for q in mine:
                        q.full()


C_ID, C_MEAN, C_HEAD, C_M64, C_TRI, C_MASK = (i * P for i in range(6))
C_COL = C_MASK + 2 * BAND
COLS = {"tiny": 2.0 ** -64, "shift": LN_SHIFT / 2 * float(np.log(2.0)), "eps5": 1e-5, "eps6": 1e-6}
C_END = C_COL + len(COLS)


class Constants:
    def __init__(self, c32, c16):
        self.ident = c32[:, C_ID:C_ID + P]
        self.mean = c32[:, C_MEAN:C_MEAN + P]
        self.head = c32[:, C_HEAD:C_HEAD + P]
        self.mean64 = c32[0:STATES, C_M64:C_M64 + P]
        self.tri = c32[:, C_TRI:C_TRI + P]
        self.col = {n: c32[:, C_COL + i:C_COL + i + 1] for i, n in enumerate(COLS)}
        self.identb = c16[:, 0:P]
        self.mask = c16[:, P:P + 2 * BAND]


def keep(nc, pairs):
    with ExitStack() as ctx:
        stored = ctx.enter_context(nc.semaphore("kept"))
        with nc.Block() as block:
            @block.sync
            def _(sp):
                for dram, sbuf in pairs:
                    sp.dma_start(dram, sbuf).then_inc(stored, 16)
                sp.wait_ge(stored, 16 * len(pairs))


def result(nc, x_kept, s1_kept, xf, out_dram, seqs):
    with ExitStack() as ctx:
        def sb(name):
            return ctx.enter_context(nc.sbuf_tensor("d_" + name, [P, seqs * SEQ], F32))

        def sig(name):
            return Signal(ctx.enter_context(nc.semaphore("d_" + name)))

        x, s1, g = sb("x"), sb("s1"), sb("g")
        loads = [ctx.enter_context(nc.semaphore(f"d_load{i}")) for i in range(seqs)]
        gates, prod, total, stored = sig("silu"), sig("product"), sig("total"), sig("stored")
        part = [slice(i * SEQ, (i + 1) * SEQ) for i in range(seqs)]
        with nc.Block() as block:
            @block.scalar
            def _(act):
                for i in range(seqs):
                    f = xf[:, i * (SEQ + 1) + 1:(i + 1) * (SEQ + 1)]
                    nc.scalar.activation(g[:, part[i]], f, ACT.Silu).then_inc(*gates.up())

            @block.vector
            def _(dve):
                for i in range(seqs):
                    dve.wait_ge(*gates.nth(i + 1))
                    dve.wait_ge(loads[i], 32)
                    nc.vector.tensor_tensor(g[:, part[i]], g[:, part[i]], s1[:, part[i]], ALU.mult).then_inc(*prod.up())
                    dve.wait_ge(*prod.nth(i + 1))
                    nc.vector.tensor_tensor(g[:, part[i]], g[:, part[i]], x[:, part[i]], ALU.add).then_inc(*total.up())

            @block.sync
            def _(sp):
                for i in range(seqs):
                    sp.dma_start(s1[:, part[i]], s1_kept[:, part[i]]).then_inc(loads[i], 16)
                    sp.dma_start(x[:, part[i]], x_kept[:, part[i]]).then_inc(loads[i], 16)
                for i in range(seqs):
                    sp.wait_ge(*total.nth(i + 1))
                    sp.dma_start(out_dram[:, part[i]], g[:, part[i]]).then_inc(stored.sem, 16)
                sp.wait_ge(stored.sem, 16 * seqs)


def program(nc, x_dram, wa, wb, wh, wt, tab, c32_dram, out_dram):
    with ExitStack() as ctx:
        def sb(name, shape, dt=F32, at=ctx):
            return at.enter_context(nc.sbuf_tensor(name, shape, dt))

        xf = sb("xf", [P, SEQS * (SEQ + 1)])
        c32 = sb("c32", [P, C_END])
        c16 = sb("c16", [P, P + 2 * BAND], BF16)
        x_kept = nc.dram_tensor("x_kept", (P, SEQS * SEQ), F32).ap()
        s1_kept = nc.dram_tensor("s1_kept", (P, SEQS * SEQ), F32).ap()
        loaded = ctx.enter_context(nc.semaphore("loaded"))
        const = Constants(c32, c16)
        with ExitStack() as early:
            x = sb("x", [P, SEQS * SEQ], at=early)
            s1 = sb("s1", [P, SEQS * SEQ], at=early)
            with nc.Block() as block:
                @block.sync
                def _(sp):
                    sp.dma_start(x[:, :], x_dram).then_inc(loaded, 16)
                    sp.dma_start(c32[:, :], c32_dram).then_inc(loaded, 16)
                    sp.wait_ge(loaded, 32)

                @block.vector
                def _(dve):
                    dve.wait_ge(loaded, 32)
                    nc.vector.tensor_copy(c16[:, 0:P], const.ident)
                    nc.vector.tensor_copy(c16[:, P:], c32[:, C_MASK:C_MASK + 2 * BAND])
            level0(nc, x, wa, const, SEQS)
            level1(nc, x, xf, s1, wb, const, SEQS)
            keep(nc, [(x_kept, x[:, :]), (s1_kept, s1[:, :])])
        network(nc, xf, wh, wt, tab, const, DEPTH, SEQS)
        result(nc, x_kept, s1_kept, xf, out_dram, SEQS)



def rows(a):
    return a.reshape(-1, P, a.shape[1]).transpose(1, 0, 2).reshape(P, -1)


def pack_level0(d):
    W = np.zeros((P, A_END), np.float32)
    for c, n in ((A_Q, "Wq"), (A_K, "Wk")):
        W[:, c:c + 512].reshape(P, HEADS, 32)[:, :, 0:16] = d["L0_attn_" + n].reshape(P, HEADS, 16)
    f = {n: d["L0_ffn_" + n] for n in ("Wg", "bg", "Wu", "bu", "Wd", "bd", "Wq", "keys", "down_embed", "up_embed")}
    W[:, A_V:A_V + P] = d["L0_attn_Wv"]
    W[:, A_O:A_O + P] = d["L0_attn_Wo"]
    W[:, A_G:A_G + 512] = f["Wg"]
    W[:, A_U:A_U + 512] = f["Wu"]
    W[:, A_D:A_D + 512] = rows(f["Wd"])
    W[:, A_DOWN:A_DOWN + 512] = f["down_embed"].T
    W[:, A_UP:A_UP + 512] = rows(f["up_embed"])
    W[:, A_WQT:A_WQT + 512] = f["Wq"].reshape(P, 2, 4, 64).transpose(1, 3, 2, 0).reshape(P, 512)
    W[:, A_KEYS:A_KEYS + 256] = f["keys"].transpose(2, 3, 0, 1).reshape(P, 256)
    W[:, A_BG:A_BG + 4] = f["bg"].reshape(4, P).T
    W[:, A_BU:A_BU + 4] = f["bu"].reshape(4, P).T
    W[:, A_BD] = f["bd"]
    return W


def pack_level1(d):
    W = np.zeros((P, B_END), np.float32)
    a = {n[8:]: v for n, v in d.items() if n.startswith("L1_attn_")}
    W[:, B_IN:B_IN + 512] = a["in_proj_w"]
    for c, n in ((B_DT, "dt_w"), (B_BP, "bp_w"), (B_CP, "cp_w")):
        W[:, c:c + 2 * STATES] = rows(a[n])
    W[:, B_OUT:B_OUT + 2 * P] = rows(a["out_w"])
    W[:, B_GW:B_GW + EXPERTS] = a["gate_w"]
    W[:, B_W1:B_W1 + EXPERTS * HID] = a["e_w1"].transpose(1, 0, 2).reshape(P, -1)
    W[:, B_W2:B_W2 + EXPERTS * HID] = a["e_w2"].reshape(EXPERTS, 4, P, P).transpose(2, 0, 1, 3).reshape(P, -1)
    W[0:STATES, B_S2I:B_S2I + 2 * P] = a["s2i_w"]
    W[0:EXPERTS, B_B2:B_B2 + P] = a["e_b2"]
    W[:, B_GB:B_GB + TILES * EXPERTS] = np.tile(a["gate_b"], (P, TILES))
    before = np.tril(np.ones((EXPERTS, EXPERTS)), -1).reshape(1, -1)
    W[:, B_LT:B_LT + TILES * EXPERTS * EXPERTS] = np.tile(before, (P, TILES))
    for e in range(EXPERTS):
        W[e, B_SEL + e * P:B_SEL + (e + 1) * P] = 1

    def put(name, block, height=P):
        c = B_P + BP[name]
        W[0:height, c:c + block.shape[1]] = block

    put("inb", a["in_proj_b"].reshape(4, P).T)
    put("conv", a["conv_w"].reshape(2, P, 3).transpose(1, 0, 2).reshape(P, 6))
    for name, n in (("convb", "conv_b"), ("s2ib", "s2i_b"), ("D", "D_param"), ("outb", "out_b"), ("n1", "norm1_w"), ("n2", "norm2_w")):
        put(name, a[n].reshape(-1, P).T)
    for name, n in (("dtb", "dt_b"), ("bpb", "bp_b"), ("cpb", "cp_b")):
        put(name, a[n].reshape(STATES, 1), STATES)
    put("b1", a["e_b1"].reshape(EXPERTS * 4, P).T)
    return W


def swapped(a):
    h = a.reshape(*a.shape[:-1], -1, 2, HALF)[..., ::-1, :]
    return h.reshape(a.shape)


def pack_network(d):
    a = {n[7:]: v for n, v in d.items() if n.startswith("L1_ffn_")}
    H = np.zeros((DEPTH, P, H_END), np.float32)
    T = np.zeros((DEPTH, P, T_END), np.float32)
    qkv, n = a["Wqkv"], HEADS * DH
    qk = qkv[:, :, 0:2 * n]
    both = np.stack([x.reshape(DEPTH, P, 2 * PAIRS, P) for x in (qk, swapped(qk))], 3)
    both = both[:, :, [kind * PAIRS + pair for kind, pair in UNIT]]
    H[:, :, H_QK:H_QK + 4 * n] = both.reshape(DEPTH, P, 4 * n)
    H[:, :, H_V:H_V + n] = qkv[:, :, 2 * n:]
    for i, s in enumerate((a["q_scale"], swapped(a["q_scale"]), a["k_scale"], swapped(a["k_scale"]))):
        H[:, :, H_P + i] = np.tile(s, (1, 2))
    T[:, :, T_O:T_O + n] = a["Wo"].reshape(DEPTH, n // P, P, P).transpose(0, 2, 1, 3).reshape(DEPTH, P, n)
    T[:, :, T_1:T_1 + 2 * FF] = a["W1"]
    for c, (f, m) in enumerate(FCH):
        T[:, 0:m, T_2 + c * P:T_2 + (c + 1) * P] = a["W2"][:, f:f + m]
        T[:, 0:m, T_P + PAR["b1"] + c] = a["b1"][:, f:f + m]
        T[:, 0:m, T_P + PAR["b1"] + 3 + c] = a["b1"][:, FF + f:FF + f + m]
    T[:, :, T_P + PAR["g"]] = a["ln_g"]
    T[:, :, T_P + PAR["b"]] = a["ln_b"]
    T[:, :, T_P + PAR["b2"]] = a["b2"]
    return H, T


def rotary_tables():
    f = np.float32
    half = np.arange(0, DH, 2, dtype=f)
    inv_freq = f(1.0) / f(10000.0) ** (half / f(DH))
    t = np.arange(SEQ, dtype=f)
    angle = t[:, None] * inv_freq[None, :]
    base = (half + f(0.4 * DH)) / f(1.4 * DH)
    scale = base[None, :] ** ((t - f(SEQ // 2)) / f(LOOK // 2))[:, None]
    c, s = (np.concatenate(x, 1) for x in ([np.cos(angle)] * 2, [-np.sin(angle), np.sin(angle)]))
    scale = np.concatenate([scale, scale], 1)
    tables = np.stack([c * scale, s * scale, c / scale, s / scale]).astype(f)
    return np.tile(tables.transpose(2, 0, 1), (2, 1, 1))


def constants():
    c = np.zeros((P, C_END), np.float32)
    c[:, C_ID:C_ID + P] = np.eye(P)
    c[:, C_MEAN:C_MEAN + P] = 1.0 / P
    c[:, C_HEAD:C_HEAD + P] = np.kron(np.eye(2), np.ones((DH, DH)))
    c[:, C_M64:C_M64 + P] = 1.0 / STATES
    c[:, C_TRI:C_TRI + P] = np.triu(np.ones((P, P)))
    i, k = np.arange(P)[:, None], np.arange(BAND)[None, :]
    c[:, C_MASK:C_MASK + 2 * BAND] = np.tile(np.where((k >= i) & (k <= i + LOOK), 0.0, -BIG), (1, 2))
    for i, v in enumerate(COLS.values()):
        c[:, C_COL + i] = v
    return c


def kernel(**inputs):
    import concourse.bacc as bacc
    from concourse.bass_utils import run_bass_kernel_spmd

    d = {n: np.asarray(v) for n, v in inputs.items()}
    x = d["L0_attn_hidden_states"]
    w_heads, w_tails = pack_network(d)
    arrays = {
        "x": x.transpose(2, 0, 1).reshape(P, SEQS * SEQ),
        "w_level0": pack_level0(d),
        "w_level1": pack_level1(d),
        "w_heads": w_heads,
        "w_tails": w_tails,
        "tables": rotary_tables(),
        "consts": constants(),
    }
    nc = bacc.Bacc("TRN2", target_bir_lowering=False, num_devices=1)
    given, args = {}, []
    for name, a in arrays.items():
        a = np.ascontiguousarray(a)
        given[f"in_{name}"] = a
        args.append(nc.dram_tensor(f"in_{name}", a.shape, mybir.dt.from_np(a.dtype), kind="ExternalInput").ap())
    out = nc.dram_tensor("out", (P, SEQS * SEQ), F32, kind="ExternalOutput").ap()
    program(nc, *args, out)
    r = run_bass_kernel_spmd(nc, [given], core_ids=[0])
    y = r.results[0]["out"]
    return np.ascontiguousarray(y.reshape(P, SEQS, SEQ).transpose(1, 2, 0)).reshape(x.shape)
```

```python
from contextlib import ExitStack

import numpy as np

import concourse.bass as bass
from concourse import mybir
from concourse.alu_op_type import AluOpType as ALU

ACT = mybir.ActivationFunctionType
F32 = mybir.dt.float32
F32R = mybir.dt.float32r
BF16 = mybir.dt.bfloat16
AX = mybir.AxisListType

P = 128
SEQS, SEQ = 8, 512
TILE = 128
TILES = SEQ // TILE
DEPTH = 6
HEADS, DH = 16, 64
HALF = DH // 2
LOOK = 32
BAND = LOOK + TILE
FF = 341
FCH = [(0, 128), (128, 128), (256, FF - 256)]
QK_SCALE = 8.0
NORM_MIN = 1e-12
LN_SHIFT = 20

PAIRS = HEADS // 2

NU = 2 * PAIRS
UNIT = [(u % 4 // 2, 2 * (u // 4) + u % 2) for u in range(NU)]
CARRY = 4

H_V = 0
H_QK = H_V + HEADS * DH
H_P = H_QK + NU * 2 * P
H_END = H_P + 4
CHUNKS = H_P // 512
CHUNKS_FIRST = 2 + CARRY // 2
T_O = 0
T_1 = T_O + HEADS * DH
T_2 = T_1 + 2 * FF
T_P = T_2 + 3 * P
PAR = {"g": 0, "b": 1, "b1": 2, "b2": 8}
T_END = T_P + 9


class Signal:

    def __init__(self, sem, per=0, primed=0):
        self.sem, self.per, self.primed, self.n = sem, per, primed, 0

    def prime(self):
        assert self.primed
        return self.sem, 1

    def up(self):
        self.n += 1
        return self.sem, 1

    def nth(self, n, turn=0):
        value = turn * self.per + (n + self.primed) if self.per else n
        assert not isinstance(value, int) or value > 0
        return self.sem, value

    def last(self, turn=0):
        return self.nth(self.n, turn)

    def full(self):
        assert self.n == self.per, (self.n, self.per)


def network(nc, xf, wh_dram, wt_dram, tab_dram, const, depth, seqs):
    with ExitStack() as ctx:
        def sb(name, shape, dt=F32):
            return ctx.enter_context(nc.sbuf_tensor("c_" + name, shape, dt))

        def sig(name, per=0, primed=0):
            return Signal(ctx.enter_context(nc.semaphore("c_" + name)), per, primed)

        ident, ones_mean, ones_head, col = const.ident, const.mean, const.head, const.col
        WH = sb("WH", [P, H_P], F32R)
        WL = sb("WL", [P, H_P], F32R)
        WP = sb("WP", [P, 4])
        WT = sb("WT", [P, T_END])
        base = sb("base", [P, 4, SEQ])
        TC = sb("TC", [P, 2, SEQ])
        TS = sb("TS", [P, 2, SEQ])
        xh = sb("xh", [P, SEQ], F32R)
        xl = sb("xl", [P, SEQ], F32R)
        sq = sb("sq", [P, 2, SEQ])
        lnr = sb("lnr", [P, SEQ])
        rinv = sb("rinv", [P, 2, SEQ])
        tcs = sb("tcs", [P, 2, 2, SEQ])
        rot = sb("rot", [P, 2, SEQ])
        QK = sb("QK", [P, 2, PAIRS, SEQ])
        V = sb("V", [P, TILES, HEADS * DH])
        OT = sb("OT", [P, PAIRS, SEQ])
        mx = sb("mx", [P, 2, 4])
        nb = sb("nb", [P, 2, 4])
        sums = sb("sums", [P, 2, 4])
        rs = sb("rs", [P, 2, 4])
        Pb = sb("Pb", [P, 3, 4, 96 + BAND])
        PTs = sb("PTs", [P, 2, 4, TILE])
        PT2s = sb("PT2s", [P, 2, 4, LOOK])
        x1 = sb("x1", [P, 1 + SEQ])
        stage = sb("stage", [P, 6, SEQ])
        hh = stage[:, 0:3]
        rstd, xn = stage[:, 3], stage[:, 4]
        xs2 = stage[:, 5]
        S = ctx.enter_context(nc.psum_tensor("c_S", [P, 4, 512], F32))
        PAB = ctx.enter_context(nc.psum_tensor("c_PAB", [P, 2, 512], F32))
        PT = ctx.enter_context(nc.psum_tensor("c_PT", [P, 512], F32))
        PX = ctx.enter_context(nc.psum_tensor("c_PX", [P, 512], F32))

        def par(name, k=0):
            return WT[:, T_P + PAR[name] + k:T_P + PAR[name] + k + 1]

        NS = 16
        wh_in = sig("wh_in")
        wp_in = sig("wp_in")
        wt_in = sig("wt_in")
        base_in = sig("base_in")
        layer_done = sig("layer_done", 1, 1)
        tables = sig("tables", 4)
        zeroed = sig("zeroed")
        split = sig("split", 2 * CHUNKS)
        shifted = sig("shifted", 4)
        projected = sig("projected", NU)
        squared = sig("squared", NU)
        prods = sig("prods", 2 * NU)
        summed = sig("summed", NU)
        logs = sig("logs", NU)
        rinvs = sig("rinvs", NU)
        rotated = sig("rotated", NU)
        qk_ready = sig("qk_ready", NU)
        v_done = sig("v_done", 8)
        v_even = sig("v_even", 4)
        v_odd = sig("v_odd", 4)
        s_done = sig("s_done", NS)
        maxed = sig("maxed", NS)
        nb_ready = sig("nb_ready", NS)
        exps = sig("exps", NS)
        rs_ready = sig("rs_ready", NS)
        p_ready = sig("p_ready", NS)
        pt_done = sig("pt_done", NS)
        pt_copied = sig("pt_copied", NS)
        px_copied = sig("px_copied", 12)
        pv_done = sig("pv_done", NS)
        po_copied = sig("po_copied", NS)
        wo_done = sig("wo_done", 1)
        x1_ready = sig("x1_ready", 1)
        xs2_ready = sig("xs2_ready", 2)
        mean_done = sig("mean_done", 1)
        centred = sig("centred", 1)
        csq_ready = sig("csq_ready", 1)
        var_done = sig("var_done", 1)
        lnv = sig("lnv", 1)
        rstd_ready = sig("rstd_ready", 1)
        xnorm = sig("xnorm", 1)
        xn_ready = sig("xn_ready", 1)
        hg_done = sig("hg_done", 3)
        gelus = sig("gelus", 3)
        h_ready = sig("h_ready", 3)
        w2_done = sig("w2_done", 1)

        def prevs(n):
            return (n // 4) * 3 + n % 4

        def first(turn):
            return isinstance(turn, int) and turn == 0

        def beside(n, turn, last):
            if n == 1:
                return []
            if n < NU - CARRY:
                return [(n + CARRY, turn)]
            return [] if last else [(n + CARRY - NU, turn + 1)]

        WO, MEAN, VAR, OUT = PT[:, :], PX[:, :], PT[:, :], S[:, 2, :]
        GATE = [PX, S[:, 2, :], PX]
        VAL = [PT, S[:, 3, :], PT]

        with nc.Block() as block:
            @block.sync
            def _(sp):
                cut = CHUNKS_FIRST * SEQ
                st = stage[:, :, :].rearrange("p a c -> p (a c)")
                sp.dma_start(st[:, 0:cut], wh_dram[0][:, 0:cut]).then_inc(wh_in.sem, 16)
                sp.dma_start(WP[:, :], wh_dram[0][:, H_P:]).then_inc(wp_in.sem, 16)
                sp.dma_start(base[:, :, :], tab_dram).then_inc(base_in.sem, 16)
                sp.dma_start(WT[:, :], wt_dram[0]).then_inc(wt_in.sem, 16)
                sp.wait_ge(*split.nth(2 * CHUNKS_FIRST))
                sp.dma_start(st[:, 0:H_P - cut], wh_dram[0][:, cut:H_P]).then_inc(wh_in.sem, 16)
                with sp.Fori(1, depth) as l:
                    wh = wh_dram[bass.ds(l, 1)].rearrange("a p c -> (a p) c")
                    sp.wait_ge(*layer_done.nth(-1, l * seqs))
                    sp.dma_start(st[:, 0:cut], wh[:, 0:cut]).then_inc(wh_in.sem, 16)
                    sp.dma_start(WP[:, :], wh[:, H_P:]).then_inc(wp_in.sem, 16)
                    sp.wait_ge(*split.nth(2 * CHUNKS_FIRST, l))
                    sp.dma_start(st[:, 0:H_P - cut], wh[:, cut:H_P]).then_inc(wh_in.sem, 16)
                    sp.wait_ge(*layer_done.nth(0, l * seqs))
                    sp.dma_start(WT[:, :], wt_dram[bass.ds(l, 1)].rearrange("a p c -> (a p) c")).then_inc(wt_in.sem, 16)

            def turns(eng, head, main, both, tail):
                head()
                with eng.Fori(0, depth - 1) as l:
                    with eng.Fori(0, seqs - 1) as s:
                        main(l * seqs + s, s + 1, None, False)
                        both(l * seqs + s, s, l, s + 1, l)
                    main(l * seqs + (seqs - 1), 0, l + 1, False)
                    both(l * seqs + (seqs - 1), seqs - 1, l, 0, l + 1)
                l = depth - 1
                with eng.Fori(0, seqs - 1) as s:
                    main(s + l * seqs, s + 1, None, False)
                    both(s + l * seqs, s, l, s + 1, l)
                main(l * seqs + seqs - 1, None, None, True)
                tail(l * seqs + seqs - 1, seqs - 1, l)

            @block.gpsimd
            def _(pool):
                nc.gpsimd.memset(Pb[:, :, :, 0:128], 0.0).then_inc(*zeroed.up())
                nc.gpsimd.memset(x1[:, 0:1], 0.0).then_inc(*zeroed.up())

                def rotate(u, turn):
                    pool.wait_ge(*prods.nth(2 * u + 2, turn))
                    if u >= 2 or not first(turn):
                        pool.wait_ge(*qk_ready.nth(u - 1, turn))
                    nc.gpsimd.tensor_tensor(rot[:, u % 2], tcs[:, u % 2, 0], tcs[:, u % 2, 1], ALU.add).then_inc(*rotated.up())

                def normalise(n, turn):
                    pool.wait_ge(*rs_ready.nth(n + 1, turn))
                    lo = 96 if n % 4 else 128
                    p = Pb[:, n % 3, :, lo:]
                    r = rs[:, n % 2, :].unsqueeze(2).broadcast_to([P, 4, 96 + BAND - lo])
                    nc.gpsimd.tensor_tensor(p, p, r, ALU.mult).then_inc(*p_ready.up())

                def head():
                    for u in range(CARRY + 2):
                        rotate(u, 0)

                def main(turn, s_next, new, last):
                    for n in range(1, NS):
                        for u in beside(n, turn, last):
                            rotate(*u)
                        normalise(n - 1, turn)

                def tail(turn, s, l):
                    normalise(NS - 1, turn)

                def both(turn, s, l, s_next, l_next):
                    normalise(NS - 1, turn)
                    rotate(CARRY, turn + 1)
                    rotate(CARRY + 1, turn + 1)

                turns(pool, head, main, both, tail)

            @block.scalar
            def _(act):
                def square(u, turn):
                    act.wait_ge(*projected.nth(u + 1, turn))
                    if u >= 2 or not first(turn):
                        act.wait_ge(*summed.nth(u - 1, turn))
                    nc.scalar.activation(sq[:, u % 2], PAB[:, 0, :], ACT.Square).then_inc(*squared.up())

                def inverse_norm(u, turn):
                    act.wait_ge(*summed.nth(u + 1, turn))
                    if u >= 2 or not first(turn):
                        act.wait_ge(*qk_ready.nth(u - 1, turn))
                    nc.scalar.activation(lnr[:, :], PAB[:, 0, :], ACT.Ln, bias=col["tiny"], scale=float(2 ** LN_SHIFT)).then_inc(*logs.up())
                    act.wait_ge(*logs.nth(u + 1, turn))
                    nc.scalar.activation(rinv[:, u % 2], lnr[:, :], ACT.Exp, bias=col["shift"], scale=-0.5).then_inc(*rinvs.up())

                def v_copy(t, turn):
                    act.wait_ge(*v_done.nth(2 * t + 1, turn))
                    if not first(turn):
                        act.wait_ge(*pv_done.nth(min(t - 2, 0), turn))
                    nc.scalar.activation(V[:, t, 0:512], S[:, 2 * t % 4, :], ACT.Copy).then_inc(*v_even.up())

                def exp(n, turn):
                    act.wait_ge(*nb_ready.nth(n + 1, turn))
                    if n == 0 and not first(turn):
                        act.wait_ge(*pt_done.nth(0, turn))
                    if n >= 3:
                        act.wait_ge(*pt_done.nth(n - 2, turn))
                    if n >= 2:
                        act.wait_ge(*rs_ready.nth(n - 1, turn))
                    lo = 0 if n % 4 else LOOK
                    for j in range(4):
                        b, c = 2 * (n % 2) + j % 2, (j // 2) * BAND
                        i = 2 * (j % 2) + j // 2
                        e = nc.scalar.activation(Pb[:, n % 3, i, 96 + lo:], S[:, b, c + lo:c + BAND], ACT.Exp,
                                                 bias=nb[:, n % 2, i:i + 1], scale=QK_SCALE, accum_out=sums[:, n % 2, i:i + 1])
                    e.then_inc(*exps.up())

                def prev_copy(n, turn):
                    if n % 4:
                        act.wait_ge(*pt_done.nth(n + 1, turn))
                        if n >= 2:
                            act.wait_ge(*pv_done.nth(n - 1, turn))
                        nc.scalar.activation(PT2s[:, n % 2], PX[:, 256:384].rearrange("p (j q) -> p j q", j=4), ACT.Copy)\
                            .then_inc(*px_copied.up())

                def out_copy(n, turn):
                    g, t = n // 4, n % 4
                    act.wait_ge(*pv_done.nth(n + 1, turn))
                    nc.scalar.activation(OT[:, 2 * g:2 * g + 2, t * TILE:(t + 1) * TILE],
                                         PX[:, 0:256].rearrange("p (j q) -> p j q", j=2), ACT.Copy).then_inc(*po_copied.up())

                def norm_squares(turn):
                    act.wait_ge(*centred.nth(1, turn))
                    nc.scalar.activation(xn[:, :], xs2[:, :], ACT.Square).then_inc(*csq_ready.up())

                def norm_root(turn):
                    act.wait_ge(*var_done.nth(1, turn))
                    nc.scalar.activation(xn[:, :], VAR, ACT.Ln, bias=col["eps5"]).then_inc(*lnv.up())
                    act.wait_ge(*lnv.nth(1, turn))
                    nc.scalar.activation(rstd[:, :], xn[:, :], ACT.Exp, scale=-0.5).then_inc(*rstd_ready.up())

                def gates(turn):
                    for c, (_, m) in enumerate(FCH):
                        act.wait_ge(*hg_done.nth(c + 1, turn))
                        nc.scalar.activation(hh[0:m, c], GATE[c][0:m, :], ACT.Gelu, bias=par("b1", 3 + c)[0:m, :]).then_inc(*gelus.up())
                    nc.scalar.preload_act_table_set("natural_log_exp_and_others")

                def head():
                    for u in range(CARRY):
                        square(u, 0)
                        inverse_norm(u, 0)
                    for t in range(TILES):
                        v_copy(t, 0)
                    for u in (CARRY, CARRY + 1):
                        square(u, 0)
                        inverse_norm(u, 0)

                def main(turn, s_next, new, last):
                    for n in range(1, NS):
                        units = beside(n, turn, last)
                        for u in units:
                            square(*u)
                        exp(n - 1, turn)
                        if n >= 2:
                            prev_copy(n - 2, turn)
                        for u in units:
                            inverse_norm(*u)
                        if n >= 2:
                            out_copy(n - 2, turn)

                def tail(turn, s, l):
                    exp(NS - 1, turn)
                    for n in (NS - 2, NS - 1):
                        prev_copy(n, turn)
                        out_copy(n, turn)
                    norm_squares(turn)
                    norm_root(turn)
                    gates(turn)

                def both(turn, s, l, s_next, l_next):
                    nxt = turn + 1
                    exp(NS - 1, turn)
                    prev_copy(NS - 2, turn)
                    v_copy(0, nxt)
                    out_copy(NS - 2, turn)
                    v_copy(1, nxt)
                    prev_copy(NS - 1, turn)
                    out_copy(NS - 1, turn)
                    v_copy(2, nxt)
                    v_copy(3, nxt)
                    square(CARRY, nxt)
                    norm_squares(turn)
                    norm_root(turn)
                    inverse_norm(CARRY, nxt)
                    square(CARRY + 1, nxt)
                    gates(turn)
                    inverse_norm(CARRY + 1, nxt)

                nc.scalar.preload_act_table_set("natural_log_exp_and_others")
                act.wait_ge(*zeroed.nth(2))
                turns(act, head, main, both, tail)

            @block.tensor
            def _(pe):
                def proj(u, turn):
                    if u == 0:
                        pe.wait_ge(*shifted.nth(4, turn))
                    if u or not first(turn):
                        pe.wait_ge(*prods.nth(2 * u, turn))
                        pe.wait_ge(*logs.nth(u, turn))
                    c = H_QK + u * 2 * P
                    for i in range(2):
                        w = slice(c + i * P, c + (i + 1) * P)
                        nc.tensor.matmul(PAB[:, i, :], WH[:, w], xh[:, :], start=True, stop=False)
                        nc.tensor.matmul(PAB[:, i, :], WL[:, w], xh[:, :], start=False, stop=False)
                        mm = nc.tensor.matmul(PAB[:, i, :], WH[:, w], xl[:, :], start=False, stop=True)
                    mm.then_inc(*projected.up())

                def sumsq(u, turn):
                    pe.wait_ge(*squared.nth(u + 1, turn))
                    pe.wait_ge(*prods.nth(2 * u + 1, turn))
                    nc.tensor.matmul(PAB[:, 0, :], ones_head, sq[:, u % 2], start=True, stop=True).then_inc(*summed.up())

                def v_proj(i, turn):
                    if i >= 4:
                        pe.wait_ge(*(v_even, v_odd)[i % 2].nth((i - 4) // 2 + 1, turn))
                    elif not first(turn):
                        pe.wait_ge(*exps.nth(i // 2 - 1, turn))
                    t, h = i // 2, i % 2
                    tok, w = slice(t * TILE, (t + 1) * TILE), slice(H_V + h * 512, H_V + h * 512 + 512)
                    nc.tensor.matmul(S[:, i % 4, :], xh[:, tok], WH[:, w], start=True, stop=False)
                    nc.tensor.matmul(S[:, i % 4, :], xh[:, tok], WL[:, w], start=False, stop=False)
                    nc.tensor.matmul(S[:, i % 4, :], xl[:, tok], WH[:, w], start=False, stop=True).then_inc(*v_done.up())

                def scores(n, turn):
                    g, t = n // 4, n % 4
                    if t == 0:
                        pe.wait_ge(*qk_ready.nth(4 * g + 4, turn))
                    if n >= 2:
                        pe.wait_ge(*exps.nth(n - 1, turn))
                    if n == 0:
                        pe.wait_ge(*v_even.nth(4, turn))
                        pe.wait_ge(*v_odd.nth(4, turn))
                    if n == 1:
                        pe.wait_ge(*layer_done.nth(0, turn))
                    lo = 0 if t else LOOK
                    k0 = t * TILE - LOOK + lo
                    for r in range(2):
                        b = 2 * (n % 2) + r
                        out = S[:, b, 0:2 * BAND].rearrange("p (c k) -> p c k", c=2)[:, :, lo:]
                        mask = const.mask[:, :].rearrange("p (c k) -> p c k", c=2)[:, :, lo:]
                        nc.tensor.matmul(out, const.identb, mask, start=True, stop=False, skip_group_check=True)
                    for c in range(2):
                        for r in range(2):
                            rows = slice(64 * r, 64 * r + 64)
                            mm = nc.tensor.matmul(S[:, 2 * (n % 2) + r, c * BAND + lo:(c + 1) * BAND],
                                                  QK[rows, 0, 2 * g + c, t * TILE:(t + 1) * TILE],
                                                  QK[rows, 1, 2 * g + c, k0:(t + 1) * TILE], start=False, stop=c == 1, skip_group_check=True)
                    mm.then_inc(*s_done.up())

                def turn_probs(n, turn):
                    pe.wait_ge(*p_ready.nth(n + 1, turn))
                    if n >= 1:
                        pe.wait_ge(*pt_copied.nth(n, turn))
                        pe.wait_ge(*po_copied.nth(n, turn))
                    for j in range(4):
                        mm = nc.tensor.transpose(PT[:, j * TILE:(j + 1) * TILE], Pb[:, n % 3, j, 128:], ident)
                    if n % 4:
                        for j in range(4):
                            mm = nc.tensor.transpose(PX[:, 256 + j * LOOK:256 + (j + 1) * LOOK], Pb[0:LOOK, n % 3, j, 0:128],
                                                     ident[0:LOOK, 0:LOOK])
                    mm.then_inc(*pt_done.up())

                def values(n, turn):
                    g, t = n // 4, n % 4
                    pe.wait_ge(*pt_copied.nth(n + 1, turn))
                    if t:
                        pe.wait_ge(*px_copied.nth(prevs(n), turn))
                    for r in range(2):
                        for c in range(2):
                            h = 4 * g + 2 * c + r
                            i = 2 * r + c
                            rows = slice(64 * r, 64 * r + 64)
                            mm = nc.tensor.matmul(PX[rows, c * TILE:(c + 1) * TILE], V[:, t, h * DH:(h + 1) * DH], PTs[:, n % 2, i, :],
                                                  start=True, stop=t == 0)
                            if t:
                                mm = nc.tensor.matmul(PX[rows, c * TILE:c * TILE + LOOK], V[:, t - 1, h * DH:(h + 1) * DH],
                                                      PT2s[:, n % 2, i, :], start=False, stop=True)
                    mm.then_inc(*pv_done.up())

                def out_proj(turn, l):
                    pe.wait_ge(wt_in.sem, l * 16 + 16)
                    pe.wait_ge(*po_copied.nth(NS, turn))
                    for p in range(PAIRS):
                        mm = nc.tensor.matmul(WO, WT[:, T_O + p * P:T_O + (p + 1) * P], OT[:, p, :], start=p == 0, stop=p == PAIRS - 1)
                    mm.then_inc(*wo_done.up())

                def mean(turn):
                    pe.wait_ge(*xs2_ready.nth(2, turn))
                    nc.tensor.matmul(MEAN, ones_mean, xs2[:, :], start=True, stop=True).then_inc(*mean_done.up())

                def variance(turn):
                    pe.wait_ge(*csq_ready.nth(1, turn))
                    nc.tensor.matmul(VAR, ones_mean, xn[:, :], start=True, stop=True).then_inc(*var_done.up())

                def inner(c, turn):
                    f, m = FCH[c]
                    if c == 0:
                        pe.wait_ge(*xn_ready.nth(1, turn))
                    if c == 2:
                        pe.wait_ge(*gelus.nth(1, turn))
                    nc.tensor.matmul(GATE[c][0:m, :], WT[:, T_1 + FF + f:T_1 + FF + f + m], xn[:, :], start=True, stop=True)
                    if c == 2:
                        pe.wait_ge(*h_ready.nth(1, turn))
                    nc.tensor.matmul(VAL[c][0:m, :], WT[:, T_1 + f:T_1 + f + m], xn[:, :], start=True, stop=True).then_inc(*hg_done.up())

                def outer(turn):
                    pe.wait_ge(*gelus.nth(2, turn))
                    for c, (f, m) in enumerate(FCH):
                        pe.wait_ge(*h_ready.nth(c + 1, turn))
                        mm = nc.tensor.matmul(OUT, WT[0:m, T_2 + c * P:T_2 + (c + 1) * P], hh[0:m, c], start=c == 0, stop=c == 2)
                    mm.then_inc(*w2_done.up())

                def head():
                    pe.wait_ge(*split.nth(2 * CHUNKS_FIRST, 0))
                    for u in range(CARRY):
                        proj(u, 0)
                        sumsq(u, 0)
                    for i in range(8):
                        v_proj(i, 0)
                    scores(0, 0)
                    pe.wait_ge(*split.nth(2 * CHUNKS, 0))
                    for u in (CARRY, CARRY + 1):
                        proj(u, 0)
                        sumsq(u, 0)

                def main(turn, s_next, new, last):
                    for n in range(1, NS):
                        units = beside(n, turn, last)
                        if new is not None and n == NU - CARRY:
                            pe.wait_ge(*split.nth(2 * CHUNKS_FIRST, new))
                        for u in units:
                            proj(*u)
                        scores(n, turn)
                        if n >= 2:
                            turn_probs(n - 2, turn)
                        for u in units:
                            sumsq(*u)
                        if n >= 2:
                            values(n - 2, turn)

                def tail(turn, s, l):
                    for n in (NS - 2, NS - 1):
                        turn_probs(n, turn)
                        values(n, turn)
                    out_proj(turn, l)
                    mean(turn)
                    variance(turn)
                    for c in range(3):
                        inner(c, turn)
                    outer(turn)

                def both(turn, s, l, s_next, l_next):
                    nxt = turn + 1
                    turn_probs(NS - 2, turn)
                    v_proj(0, nxt)
                    v_proj(1, nxt)
                    values(NS - 2, turn)
                    v_proj(2, nxt)
                    v_proj(3, nxt)
                    turn_probs(NS - 1, turn)
                    v_proj(4, nxt)
                    values(NS - 1, turn)
                    v_proj(5, nxt)
                    v_proj(6, nxt)
                    out_proj(turn, l)
                    v_proj(7, nxt)
                    pe.wait_ge(*split.nth(2 * CHUNKS, l_next))
                    proj(CARRY, nxt)
                    mean(turn)
                    scores(0, nxt)
                    variance(turn)
                    sumsq(CARRY, nxt)
                    proj(CARRY + 1, nxt)
                    inner(0, turn)
                    inner(1, turn)
                    sumsq(CARRY + 1, nxt)
                    inner(2, turn)
                    outer(turn)

                turns(pe, head, main, both, tail)

            @block.vector
            def _(dve):
                def shift(turn, s):
                    if not first(turn):
                        dve.wait_ge(*projected.nth(0, turn))
                    src = xf[:, bass.ds(s * (SEQ + 1), SEQ + 1)]
                    parts = ((slice(0, 64), slice(1, SEQ + 1)), (slice(64, P), slice(0, SEQ)))
                    for rows, tok in parts:
                        nc.vector.tensor_copy(xh[rows, :], src[rows, tok]).then_inc(*shifted.up())
                    dve.wait_ge(*shifted.nth(2, turn))
                    for rows, tok in parts:
                        nc.vector.tensor_tensor(xl[rows, :], src[rows, tok], xh[rows, :].bitcast(F32), ALU.subtract).then_inc(*shifted.up())

                def products(u, turn):
                    kind = UNIT[u][0]
                    dve.wait_ge(*squared.nth(u + 1, turn))
                    if u >= 2 or not first(turn):
                        dve.wait_ge(*rotated.nth(u - 1, turn))
                    nc.vector.tensor_tensor(tcs[:, u % 2, 0], PAB[:, 0, :], TC[:, kind], ALU.mult).then_inc(*prods.up())
                    nc.vector.tensor_tensor(tcs[:, u % 2, 1], PAB[:, 1, :], TS[:, kind], ALU.mult).then_inc(*prods.up())

                def finish(u, turn):
                    kind, pair = UNIT[u]
                    dve.wait_ge(*rotated.nth(u + 1, turn))
                    dve.wait_ge(*rinvs.nth(u + 1, turn))
                    nc.vector.scalar_tensor_tensor(out=QK[:, kind, pair], in0=rinv[:, u % 2], scalar=1.0 / NORM_MIN,
                                                   in1=rot[:, u % 2], op0=ALU.min, op1=ALU.mult).then_inc(*qk_ready.up())

                def v_copy(t, turn):
                    dve.wait_ge(*v_done.nth(2 * t + 2, turn))
                    if not first(turn):
                        dve.wait_ge(*pv_done.nth(min(t - 2, 0), turn))
                    nc.vector.tensor_copy(V[:, t, 512:1024], S[:, (2 * t + 1) % 4, :]).then_inc(*v_odd.up())

                def row_max(n, turn):
                    dve.wait_ge(*s_done.nth(n + 1, turn))
                    lo = 0 if n % 4 else LOOK
                    b = 2 * (n % 2)
                    nc.vector.tensor_reduce(mx[:, n % 2].rearrange("p (b c) -> p b c", b=2),
                                            S[:, b:b + 2, 0:2 * BAND].rearrange("p b (c k) -> p b c k", c=2)[:, :, :, lo:],
                                            AX.X, ALU.max).then_inc(*maxed.up())
                    dve.wait_ge(*maxed.nth(n + 1, turn))
                    if n >= 2:
                        dve.wait_ge(*exps.nth(n - 1, turn))
                    nc.vector.tensor_scalar(nb[:, n % 2], mx[:, n % 2], -QK_SCALE, None, ALU.mult).then_inc(*nb_ready.up())

                def inv_sum(n, turn):
                    dve.wait_ge(*exps.nth(n + 1, turn))
                    if n >= 2:
                        dve.wait_ge(*p_ready.nth(n - 1, turn))
                    nc.vector.reciprocal(rs[:, n % 2], sums[:, n % 2]).then_inc(*rs_ready.up())

                def pt_copy(n, turn):
                    dve.wait_ge(*pt_done.nth(n + 1, turn))
                    if n >= 2:
                        dve.wait_ge(*pv_done.nth(n - 1, turn))
                    nc.vector.tensor_copy(PTs[:, n % 2], PT[:, :].rearrange("p (j q) -> p j q", j=4)).then_inc(*pt_copied.up())

                def residual(turn, s):
                    dve.wait_ge(*wo_done.nth(1, turn))
                    src = xf[:, bass.ds(s * (SEQ + 1), SEQ + 1)]
                    nc.vector.tensor_tensor(x1[:, 1:SEQ + 1], WO, src[:, 1:SEQ + 1], ALU.add).then_inc(*x1_ready.up())
                    dve.wait_ge(*x1_ready.nth(1, turn))
                    nc.vector.tensor_copy(xs2[0:64, :], x1[0:64, 1:SEQ + 1]).then_inc(*xs2_ready.up())
                    nc.vector.tensor_copy(xs2[64:P, :], x1[64:P, 0:SEQ]).then_inc(*xs2_ready.up())

                def centre(turn):
                    dve.wait_ge(*mean_done.nth(1, turn))
                    nc.vector.tensor_tensor(xs2[:, :], xs2[:, :], MEAN, ALU.subtract).then_inc(*centred.up())

                def scale(turn):
                    dve.wait_ge(*rstd_ready.nth(1, turn))
                    nc.vector.tensor_tensor(xn[:, :], xs2[:, :], rstd[:, :], ALU.mult).then_inc(*xnorm.up())
                    dve.wait_ge(*xnorm.nth(1, turn))
                    nc.vector.tensor_scalar(xn[:, :], xn[:, :], par("g"), par("b"), ALU.mult, ALU.add).then_inc(*xn_ready.up())

                def hidden(c, turn):
                    m = FCH[c][1]
                    dve.wait_ge(*gelus.nth(c + 1, turn))
                    nc.vector.scalar_tensor_tensor(out=hh[0:m, c], in0=VAL[c][0:m, :], scalar=par("b1", c)[0:m, :],
                                                   in1=hh[0:m, c], op0=ALU.add, op1=ALU.mult).then_inc(*h_ready.up())

                def finish_turn(turn, s):
                    dve.wait_ge(*w2_done.nth(1, turn))
                    dst = xf[:, bass.ds(s * (SEQ + 1) + 1, SEQ)]
                    nc.vector.scalar_tensor_tensor(out=dst, in0=OUT, scalar=par("b2"), in1=x1[:, 1:SEQ + 1],
                                                   op0=ALU.add, op1=ALU.add).then_inc(*layer_done.up())

                def tables_of(l):
                    dve.wait_ge(wp_in.sem, l * 16 + 16)
                    for kind in range(2):
                        own, partner = (WP[:, 2 * kind + i:2 * kind + i + 1] for i in range(2))
                        nc.vector.tensor_scalar(TC[:, kind], base[:, 2 * kind], own, None, ALU.mult).then_inc(*tables.up())
                        nc.vector.tensor_scalar(TS[:, kind], base[:, 2 * kind + 1], partner, None, ALU.mult).then_inc(*tables.up())
                    dve.wait_ge(*tables.nth(4, l))

                def divide(c, l):
                    first_ones = c < CHUNKS_FIRST
                    dve.wait_ge(wh_in.sem, l * 32 + (16 if first_ones else 32))
                    w = stage[:, c if first_ones else c - CHUNKS_FIRST]
                    hi, lo = WH[:, c * SEQ:(c + 1) * SEQ], WL[:, c * SEQ:(c + 1) * SEQ]
                    nc.vector.tensor_copy(hi, w).then_inc(*split.up())
                    dve.wait_ge(*split.nth(2 * c + 1, l))
                    nc.vector.tensor_tensor(lo, w, hi.bitcast(F32), ALU.subtract).then_inc(*split.up())

                def head():
                    shift(0, 0)
                    tables_of(0)
                    for c in range(CHUNKS):
                        divide(c, 0)
                    for u in range(CARRY):
                        products(u, 0)
                        finish(u, 0)
                    for t in range(TILES):
                        v_copy(t, 0)
                    row_max(0, 0)
                    for u in (CARRY, CARRY + 1):
                        products(u, 0)
                        finish(u, 0)

                def main(turn, s_next, new, last):
                    for n in range(1, NS):
                        if n == NU - CARRY and new is not None:
                            tables_of(new)
                        units = beside(n, turn, last)
                        for u in units:
                            products(*u)
                        inv_sum(n - 1, turn)
                        if n >= 2:
                            pt_copy(n - 2, turn)
                        if n == NU - CARRY - 1 and not last:
                            shift(turn + 1, s_next)
                        row_max(n, turn)
                        for u in units:
                            finish(*u)
                        if new is not None:
                            for c in {4: (0,), 5: (1,), 6: (2,), 7: (3,), 12: (4,), 13: (5,), 14: (6, 7), 15: (8, 9)}.get(n, ()):
                                divide(c, new)

                def tail(turn, s, l):
                    inv_sum(NS - 1, turn)
                    pt_copy(NS - 2, turn)
                    pt_copy(NS - 1, turn)
                    residual(turn, s)
                    centre(turn)
                    scale(turn)
                    for c in range(3):
                        hidden(c, turn)
                    finish_turn(turn, s)

                def both(turn, s, l, s_next, l_next):
                    nxt = turn + 1
                    inv_sum(NS - 1, turn)
                    pt_copy(NS - 2, turn)
                    v_copy(0, nxt)
                    v_copy(1, nxt)
                    pt_copy(NS - 1, turn)
                    v_copy(2, nxt)
                    residual(turn, s)
                    v_copy(3, nxt)
                    centre(turn)
                    products(CARRY, nxt)
                    row_max(0, nxt)
                    scale(turn)
                    finish(CARRY, nxt)
                    products(CARRY + 1, nxt)
                    for c in range(3):
                        hidden(c, turn)
                    finish_turn(turn, s)
                    finish(CARRY + 1, nxt)

                nc.vector.memset(mx[:, :, :], 0.0).then_inc(*layer_done.prime())
                dve.wait_ge(base_in.sem, 16)
                dve.wait_ge(*zeroed.nth(2))
                turns(dve, head, main, both, tail)


A_Q = 0
A_K = A_Q + HEADS * 64
A_V = A_K + HEADS * 64
A_O = A_V + P
A_G = A_O + 4 * P
A_U = A_G + 512
A_D = A_U + 512
A_DOWN = A_D + 512
A_UP = A_DOWN + 512
A_WQT = A_UP + 512
A_KEYS = A_WQT + 512
A_BG = A_KEYS + 256
A_BU = A_BG + 4
A_BD = A_BU + 4
A_SEL = A_BD + 1
A_EPS = A_SEL + P
A_LOWQ = A_EPS + 1
A_LOWK = A_LOWQ + 1
A_END = A_LOWK + 1
BIG = 1e30
TOP = 8
ROUTED = (1, 6, 11, 15)
SPAN = {0: 0, 1: 512, 3: 896, 2: 1024}
SPANS = 1280


def level0(nc, x, w_dram, const, seqs):
    with ExitStack() as ctx:
        def sb(name, shape, dt=F32):
            return ctx.enter_context(nc.sbuf_tensor("a_" + name, shape, dt))

        def sig(name, per=0, primed=0):
            return Signal(ctx.enter_context(nc.semaphore("a_" + name)), per, primed)

        ident, ones_mean, ones_head, col = const.ident, const.mean, const.head, const.col
        W = sb("W", [P, A_END])
        Wsim = sb("Wsim", [P, 512])
        cen = sb("cen", [P, SEQ])
        csq = sb("csq", [P, SEQ])
        rstd = sb("rstd", [P, SEQ])
        xn = sb("xn", [P, SEQ])
        QS = sb("QS", [P, HEADS // 2, SEQ], F32R)
        KS = sb("KS", [P, HEADS // 2, SEQ], F32R)
        high = sb("high", [P, 2, SEQ], F32R)
        V = sb("V", [P, TILES, HEADS, 32])
        AT = sb("AT", [P, 2, SPANS])
        sim = sb("sim", [P, TILES, 8, 64])
        sg = sb("sg", [P, TILES, 512])
        m8 = sb("m8", [P, 8, TOP])
        cand = sb("cand", [P, 4, TOP, TOP])
        c8 = sb("c8", [P, 4, TOP])
        nmax = sb("nmax", [P, 4])
        dlt = sb("dlt", [P, 4, TOP])
        ex8 = sb("ex8", [P, 4, TOP])
        Z = sb("Z", [P, 4])
        rZ = sb("rZ", [P, 4])
        penx = sb("penx", [P, 4, TOP])
        peny = sb("peny", [P, 4, 64])
        xm = sb("xm", [P, 4, TOP])
        ym = sb("ym", [P, 4, 64])
        D = sb("D", [P, 4, TOP, 64])
        E = sb("E", [P, 4, 512])
        pacc = sb("pacc", [P, 512])
        tot = sb("tot", [P, 1])
        rest = sb("rest", [P, 1])
        M = sb("M", [P, TILES, 512])
        MT = sb("MT", [P, 4, SEQ])
        rden = sb("rden", [P, SEQ])
        U = sb("U", [P, 4, SEQ])
        gs = sb("gs", [P, 4, SEQ])
        hT = sb("hT", [P, 4, SEQ])
        sgate = sb("sgate", [P, SEQ])
        B = ctx.enter_context(nc.psum_tensor("a_B", [P, 8, 512], F32))

        PD = 31 * TILES
        w_in = sig("w_in")
        ones_set = sig("ones_set")
        folded = sig("folded")
        wsim_ready = sig("wsim_ready")
        out_done = sig("out_done", 1, 1)
        mean_done = sig("mean_done", 1)
        centred = sig("centred", 1)
        squared = sig("squared", 1)
        var_done = sig("var_done", 1)
        lnv = sig("lnv", 1)
        rstd_ready = sig("rstd_ready", 1)
        xn_ready = sig("xn_ready", 1)
        job = sig("job", 25)
        act_out = sig("act_out", 21)
        dve_out = sig("dve_out", 20)
        scored = sig("scored", HEADS)
        weighed = sig("weighed", HEADS)
        masked = sig("masked", 2 * HEADS)
        av_done = sig("av_done", HEADS)
        peer = sig("peer", PD)
        ex8_ready = sig("ex8_ready", TILES)
        e_ready = sig("e_ready", TILES)
        d_ready = sig("d_ready", TILES)
        dlt_ready = sig("dlt_ready", TILES)
        m_ready = sig("m_ready", TILES)
        u_ready = sig("u_ready", 4)
        den_done = sig("den_done", 4)
        rden_ready = sig("rden_ready", 4)
        o_ready = sig("o_ready", 4)
        gate_done = sig("gate_done", 4)
        gs_ready = sig("gs_ready", 4)
        up_done = sig("up_done", 4)
        h_ready = sig("h_ready", 4)
        s_done = sig("s_done", 1)
        mt_done = sig("mt_done", TILES)
        mt_ready = sig("mt_ready", TILES)
        ffn_done = sig("ffn_done", 1)
        gate_ready = sig("gate_ready", 1)
        gated = sig("gated", 1)

        jobs = [j for t in range(TILES) for j in (("sim", t), ("down", t))] + [("v", 0)]
        jobs += [(what, b) for b in range(HEADS // 2) for what in "qk"]
        for_act = [i for i, j in enumerate(jobs) if j[0] != "sim"]
        for_dve = [i for i, j in enumerate(jobs) if j[0] in ("sim", "q", "k")]

        def bank(i):
            return B[:, i % 6, :]

        with nc.Block() as block:
            @block.sync
            def _(sp):
                sp.dma_start(W[:, :], w_dram).then_inc(w_in.sem, 16)

            @block.gpsimd
            def _(pool):
                nc.gpsimd.memset(V[:, :, :, :], 0.0).then_inc(*ones_set.up())
                pool.wait_ge(*ones_set.nth(1))
                nc.gpsimd.memset(V[:, :, :, 8:9], 1.0).then_inc(*ones_set.up())
                both = const.tri.unsqueeze(1).broadcast_to([P, 2, P])
                with pool.Fori(0, seqs) as turn:
                    masked.n = 0
                    for h in range(HEADS):
                        pool.wait_ge(*weighed.nth(h + 1, turn))
                        a = AT[:, h % 2, 0:1024].rearrange("p (i t) -> p i t", i=2)[:, :, 0:P]
                        b = AT[:, h % 2, 896:1152].rearrange("p (i t) -> p i t", i=2)
                        nc.gpsimd.tensor_tensor(a, a, both, ALU.mult).then_inc(*masked.up())
                        nc.gpsimd.tensor_tensor(b, b, both, ALU.mult).then_inc(*masked.up())
                    masked.full()

            @block.scalar
            def _(act):
                nc.scalar.preload_act_table_set("natural_log_exp_and_others")
                act.wait_ge(*folded.nth(2))
                nc.scalar.activation(Wsim[:, 0:256], B[:, 0, 0:256], ACT.Copy).then_inc(*wsim_ready.up())
                nc.scalar.activation(Wsim[:, 256:512], B[:, 1, 0:256], ACT.Copy).then_inc(*wsim_ready.up())
                act.wait_ge(*ones_set.nth(2))

                def routing(t, turn):
                    act.wait_ge(*dlt_ready.nth(t + 1, turn))
                    nc.scalar.activation(ex8[:, :, :], dlt[:, :, :], ACT.Exp).then_inc(*ex8_ready.up())
                    act.wait_ge(*d_ready.nth(t + 1, turn))
                    for h in range(4):
                        mm = nc.scalar.activation(E[:, h, :], D[:, h].rearrange("p a b -> p (a b)"), ACT.Exp, bias=nmax[:, h:h + 1])
                    mm.then_inc(*e_ready.up())

                with act.Fori(0, seqs) as turn:
                    mine = (squared, lnv, rstd_ready, act_out, weighed, ex8_ready, e_ready, gs_ready, u_ready, mt_ready, gate_ready)
                    for q in mine:
                        q.n = 0
                    act.wait_ge(*centred.nth(1, turn))
                    nc.scalar.activation(csq[:, :], cen[:, :], ACT.Square).then_inc(*squared.up())
                    act.wait_ge(*var_done.nth(1, turn))
                    nc.scalar.activation(csq[:, :], B[:, 7, :], ACT.Ln, bias=col["eps5"]).then_inc(*lnv.up())
                    act.wait_ge(*lnv.nth(1, turn))
                    nc.scalar.activation(rstd[:, :], csq[:, :], ACT.Exp, scale=-0.5).then_inc(*rstd_ready.up())
                    for n, i in enumerate(for_act):
                        what, b = jobs[i]
                        act.wait_ge(*job.nth(i + 1, turn))
                        if what == "down":
                            nc.scalar.activation(sg[:, b, :], bank(i), ACT.Silu).then_inc(*act_out.up())
                            if b == TILES - 1:
                                nc.scalar.preload_act_table_set("natural_log_exp_and_others")
                        elif what == "v":
                            nc.scalar.activation(V[:, :, :, 0:8].rearrange("p t h d -> p (t h) d"),
                                                 bank(i).rearrange("p (a d) -> p a d", d=8), ACT.Copy).then_inc(*act_out.up())
                        else:
                            if jobs[i - 2][0] in "qk":
                                act.wait_ge(*dve_out.nth(for_dve.index(i - 2) + 1, turn))
                            nc.scalar.activation(high[:, n % 2], bank(i), ACT.Copy).then_inc(*act_out.up())

                    def group_out(g):
                        act.wait_ge(*av_done.nth(4 * g + 4, turn))
                        nc.scalar.activation(U[:, g, :], B[:, 6 + g % 2, :], ACT.Identity, bias=W[:, A_EPS:A_EPS + 1]).then_inc(*u_ready.up())

                    for h in range(HEADS):
                        act.wait_ge(*scored.nth(h + 1, turn))
                        if h >= 2:
                            act.wait_ge(*av_done.nth(h - 1, turn))
                        s = 3 * (h % 2)
                        nc.scalar.activation(AT[:, h % 2, :], B[:, s:s + 3, :].rearrange("p a b -> p (a b)")[:, 0:SPANS],
                                             ACT.Square, scale=0.25).then_inc(*weighed.up())
                        if h in ROUTED:
                            routing(ROUTED.index(h), turn)
                        if h >= 5 and h % 4 == 1:
                            group_out(h // 4 - 1)
                    group_out(3)
                    for c in range(4):
                        act.wait_ge(*gate_done.nth(c + 1, turn))
                        nc.scalar.activation(gs[:, c, :], B[:, c, :], ACT.Silu, bias=W[:, A_BG + c:A_BG + c + 1]).then_inc(*gs_ready.up())
                    for t in range(TILES):
                        act.wait_ge(*mt_done.nth(t + 1, turn))
                        nc.scalar.activation(MT[:, :, t * TILE:(t + 1) * TILE],
                                                         B[:, 6 + t % 2, :].rearrange("p (b t) -> p b t", b=4), ACT.Copy).then_inc(*mt_ready.up())
                    act.wait_ge(*ffn_done.nth(1, turn))
                    nc.scalar.activation(sgate[:, :], B[:, 2, :], ACT.Silu, bias=W[:, A_BD:A_BD + 1]).then_inc(*gate_ready.up())
                    nc.scalar.preload_act_table_set("natural_log_exp_and_others")
                    for q in mine:
                        q.full()

            @block.tensor
            def _(pe):
                pe.wait_ge(w_in.sem, 16)
                for p in range(2):
                    r = slice(64 * p, 64 * p + 64)
                    for h in range(4):
                        mm = nc.tensor.matmul(B[:, p, h * 64:(h + 1) * 64], W[r, A_WQT + h * P:A_WQT + (h + 1) * P],
                                              W[r, A_KEYS + h * 64:A_KEYS + (h + 1) * 64], start=True, stop=True)
                    mm.then_inc(*folded.up())
                pe.wait_ge(*wsim_ready.nth(2))
                with pe.Fori(0, seqs) as turn:
                    mine = (mean_done, var_done, job, scored, av_done, den_done, gate_done, up_done, s_done, mt_done, ffn_done)
                    for q in mine:
                        q.n = 0
                    xin = x[:, bass.ds(turn * SEQ, SEQ)]
                    pe.wait_ge(*out_done.nth(0, turn))
                    nc.tensor.matmul(B[:, 6, :], ones_mean, xin, start=True, stop=True).then_inc(*mean_done.up())
                    pe.wait_ge(*squared.nth(1, turn))
                    nc.tensor.matmul(B[:, 7, :], ones_mean, csq[:, :], start=True, stop=True).then_inc(*var_done.up())
                    pe.wait_ge(*xn_ready.nth(1, turn))
                    for i, (what, b) in enumerate(jobs):
                        if i >= 6:
                            if i - 6 in for_dve:
                                pe.wait_ge(*dve_out.nth(for_dve.index(i - 6) + 1, turn))
                            else:
                                pe.wait_ge(*act_out.nth(for_act.index(i - 6) + 1, turn))
                        tok = slice(b * TILE, (b + 1) * TILE)
                        if what in "qk":
                            c = (A_Q if what == "q" else A_K) + b * P
                            mm = nc.tensor.matmul(bank(i), W[:, c:c + P], xn[:, :], start=True, stop=True)
                        elif what == "v":
                            for t in range(TILES):
                                mm = nc.tensor.matmul(bank(i)[:, t * P:(t + 1) * P], xn[:, t * TILE:(t + 1) * TILE], W[:, A_V:A_V + P],
                                                      start=True, stop=True)
                        elif what == "sim":
                            mm = nc.tensor.matmul(bank(i), xn[:, tok], Wsim[:, :], start=True, stop=True)
                        else:
                            mm = nc.tensor.matmul(bank(i), xn[:, tok], W[:, A_DOWN:A_DOWN + 512], start=True, stop=True)
                        mm.then_inc(*job.up())

                    def head_scores(h):
                        if h < 2:
                            pe.wait_ge(*act_out.nth(len(for_act), turn))
                            pe.wait_ge(*dve_out.nth(len(for_dve), turn))
                        else:
                            pe.wait_ge(*weighed.nth(h - 1, turn))
                        r = slice(64 * (h % 2), 64 * (h % 2) + 64)
                        flat = B[:, 3 * (h % 2):3 * (h % 2) + 3, :].rearrange("p a b -> p (a b)")
                        for i in range(TILES):
                            n = SEQ - i * TILE
                            mm = nc.tensor.matmul(flat[:, SPAN[i]:SPAN[i] + n], KS[r, h // 2, i * TILE:(i + 1) * TILE],
                                                  QS[r, h // 2, i * TILE:SEQ], start=True, stop=True)
                        mm.then_inc(*scored.up())

                    def head_values(h):
                        g, j = h // 4, h % 4
                        if g >= 2 and j == 0:
                            pe.wait_ge(*u_ready.nth(g - 1, turn))
                        pe.wait_ge(*masked.nth(2 * h + 2, turn))
                        for i in range(TILES):
                            mm = nc.tensor.matmul(B[32 * j:32 * j + 32, 6 + g % 2, i * TILE:SEQ], V[:, i, h, :],
                                                  AT[:, h % 2, SPAN[i]:SPAN[i] + SEQ - i * TILE], start=i == 0, stop=i == TILES - 1)
                        mm.then_inc(*av_done.up())

                    for h in range(HEADS):
                        head_scores(h)
                        if h:
                            head_values(h - 1)
                    head_values(HEADS - 1)
                    pe.wait_ge(*weighed.nth(HEADS, turn))
                    for c in range(4):
                        nc.tensor.matmul(B[:, c, :], W[:, A_G + c * P:A_G + (c + 1) * P], xn[:, :], start=True, stop=True).then_inc(*gate_done.up())

                    def spread(g):
                        pe.wait_ge(*u_ready.nth(4, turn))
                        if g >= 2:
                            pe.wait_ge(*rden_ready.nth(g - 1, turn))
                        nc.tensor.matmul(B[:, 6 + g % 2, :], W[:, A_SEL:A_SEL + P], U[:, g, :], start=True, stop=True).then_inc(*den_done.up())

                    spread(0)
                    spread(1)
                    for c in range(4):
                        if c >= 2:
                            pe.wait_ge(*h_ready.nth(c - 1, turn))
                        nc.tensor.matmul(B[:, 4 + c % 2, :], W[:, A_U + c * P:A_U + (c + 1) * P], xn[:, :], start=True, stop=True).then_inc(*up_done.up())
                    spread(2)
                    spread(3)
                    pe.wait_ge(*o_ready.nth(4, turn))
                    pe.wait_ge(*gs_ready.nth(4, turn))
                    for g in range(4):
                        mm = nc.tensor.matmul(B[:, 1, :], W[:, A_O + g * P:A_O + (g + 1) * P], U[:, g, :], start=g == 0, stop=g == 3)
                    mm.then_inc(*s_done.up())
                    for t in range(TILES):
                        pe.wait_ge(*m_ready.nth(t + 1, turn))
                        if t >= 2:
                            pe.wait_ge(*mt_ready.nth(t - 1, turn))
                        for b in range(4):
                            mm = nc.tensor.transpose(B[:, 6 + t % 2, b * P:(b + 1) * P], M[:, t, b * P:(b + 1) * P], ident)
                        mm.then_inc(*mt_done.up())
                    pe.wait_ge(*h_ready.nth(4, turn))
                    for c in range(4):
                        nc.tensor.matmul(B[:, 2, :], W[:, A_D + c * P:A_D + (c + 1) * P], hT[:, c, :], start=c == 0, stop=False)
                    pe.wait_ge(*mt_ready.nth(4, turn))
                    for b in range(4):
                        mm = nc.tensor.matmul(B[:, 2, :], W[:, A_UP + b * P:A_UP + (b + 1) * P], MT[:, b, :], start=False, stop=b == 3)
                    mm.then_inc(*ffn_done.up())
                    for q in mine:
                        q.full()

            @block.vector
            def _(dve):
                def route(t, turn):
                    for g in range(8):
                        nc.vector.max(m8[:, g, :], sim[:, t, g, :]).then_inc(*peer.up())
                    dve.wait_ge(*peer.last(turn))
                    mx_, my_ = m8[:, 0:4, :], m8[:, 4:8, :]
                    nc.vector.tensor_tensor(cand[:, :, :, :], mx_.unsqueeze(3).broadcast_to([P, 4, TOP, TOP]),
                                                    my_.unsqueeze(2).broadcast_to([P, 4, TOP, TOP]), ALU.add).then_inc(*peer.up())
                    thx = m8[:, 0:4, 7:8].broadcast_to([P, 4, TOP])
                    thy = m8[:, 4:8, 7:8].broadcast_to([P, 4, 64])
                    nc.vector.tensor_tensor(penx[:, :, :], sim[:, t, 0:4, 0:TOP], thx, ALU.is_lt).then_inc(*peer.up())
                    nc.vector.tensor_tensor(peny[:, :, :], sim[:, t, 4:8, :], thy, ALU.is_lt).then_inc(*peer.up())
                    dve.wait_ge(*peer.last(turn))
                    nc.vector.scalar_tensor_tensor(out=xm[:, :, :], in0=penx[:, :, :], scalar=-BIG, in1=sim[:, t, 0:4, 0:TOP],
                                                           op0=ALU.mult, op1=ALU.add).then_inc(*peer.up())
                    nc.vector.scalar_tensor_tensor(out=ym[:, :, :], in0=peny[:, :, :], scalar=-BIG, in1=sim[:, t, 4:8, :],
                                                           op0=ALU.mult, op1=ALU.add).then_inc(*peer.up())
                    for h in range(4):
                        nc.vector.max(c8[:, h, :], cand[:, h].rearrange("p a b -> p (a b)")).then_inc(*peer.up())
                    dve.wait_ge(*peer.last(turn))
                    if t:
                        dve.wait_ge(*e_ready.nth(t, turn))
                    nc.vector.tensor_scalar(nmax[:, :], c8[:, :, 0], -1.0, None, ALU.mult).then_inc(*peer.up())
                    dve.wait_ge(*peer.last(turn))
                    nc.vector.tensor_tensor(dlt[:, :, :], c8[:, :, :], nmax[:, :].unsqueeze(2).broadcast_to([P, 4, TOP]), ALU.add).then_inc(*dlt_ready.up())
                    nc.vector.tensor_tensor(D[:, :, :, :], xm[:, :, :].unsqueeze(3).broadcast_to([P, 4, TOP, 64]),
                                                       ym[:, :, :].unsqueeze(2).broadcast_to([P, 4, TOP, 64]), ALU.add).then_inc(*d_ready.up())
                    dve.wait_ge(*ex8_ready.nth(t + 1, turn))
                    nc.vector.tensor_reduce(Z[:, :], ex8[:, :, :], AX.X, ALU.add).then_inc(*peer.up())
                    dve.wait_ge(*peer.last(turn))
                    nc.vector.reciprocal(rZ[:, :], Z[:, :]).then_inc(*peer.up())
                    dve.wait_ge(*e_ready.nth(t + 1, turn))
                    for h in range(4):
                        mm = nc.vector.scalar_tensor_tensor(out=E[:, h, :], in0=D[:, h].rearrange("p a b -> p (a b)"), scalar=c8[:, h, 7:8],
                                                            in1=E[:, h, :], op0=ALU.is_ge, op1=ALU.mult)
                        mm.then_inc(*peer.up())
                    dve.wait_ge(*peer.last(turn))
                    nc.vector.tensor_scalar(pacc[:, :], E[:, 0, :], rZ[:, 0:1], None, ALU.mult).then_inc(*peer.up())
                    for h in range(1, 4):
                        dve.wait_ge(*peer.last(turn))
                        nc.vector.scalar_tensor_tensor(out=pacc[:, :], in0=E[:, h, :], scalar=rZ[:, h:h + 1], in1=pacc[:, :],
                                                               op0=ALU.mult, op1=ALU.add).then_inc(*peer.up())
                    dve.wait_ge(*peer.last(turn))
                    nc.vector.tensor_reduce(tot[:, :], pacc[:, :], AX.X, ALU.add).then_inc(*peer.up())
                    dve.wait_ge(*peer.last(turn))
                    nc.vector.tensor_scalar(rest[:, :], tot[:, :], -1.0, 4.0, ALU.mult, ALU.add).then_inc(*peer.up())
                    dve.wait_ge(*peer.last(turn))
                    nc.vector.tensor_tensor(pacc[:, 511:512], pacc[:, 511:512], rest[:, :], ALU.add).then_inc(*peer.up())
                    dve.wait_ge(*peer.last(turn))
                    nc.vector.tensor_tensor(M[:, t, :], pacc[:, :], sg[:, t, :], ALU.mult).then_inc(*m_ready.up())

                nc.vector.memset(tot[:, :], 0.0).then_inc(*out_done.prime())
                with dve.Fori(0, seqs) as turn:
                    mine = (centred, xn_ready, dve_out, d_ready, dlt_ready, m_ready, rden_ready, o_ready, h_ready, gated, out_done)
                    for q in mine + (peer,):
                        q.n = 0
                    xin = x[:, bass.ds(turn * SEQ, SEQ)]
                    dve.wait_ge(*mean_done.nth(1, turn))
                    nc.vector.tensor_tensor(cen[:, :], xin, B[:, 6, :], ALU.subtract).then_inc(*centred.up())
                    dve.wait_ge(*rstd_ready.nth(1, turn))
                    nc.vector.tensor_tensor(xn[:, :], cen[:, :], rstd[:, :], ALU.mult).then_inc(*xn_ready.up())
                    for n, i in enumerate(for_dve):
                        what, b = jobs[i]
                        if what == "sim":
                            dve.wait_ge(*job.nth(i + 1, turn))
                            nc.vector.tensor_copy(sim[:, b].rearrange("p g k -> p (g k)"), bank(i)).then_inc(*dve_out.up())
                        else:
                            a = for_act.index(i)
                            dve.wait_ge(*act_out.nth(a + 1, turn))
                            dst, low = (QS, A_LOWQ) if what == "q" else (KS, A_LOWK)
                            nc.vector.scalar_tensor_tensor(out=dst[:, b, :], in0=high[:, a % 2].bitcast(F32), scalar=W[:, low:low + 1],
                                                           in1=bank(i), op0=ALU.mult, op1=ALU.add).then_inc(*dve_out.up())
                    dve.wait_ge(*dve_out.nth(len(for_dve), turn))
                    dve.wait_ge(*act_out.nth(len(for_act), turn))
                    nc.vector.memset(tot[:, :], 0.0)
                    for t in range(TILES):
                        route(t, turn)
                    def divide(g):
                        dve.wait_ge(*den_done.nth(g + 1, turn))
                        if g:
                            dve.wait_ge(*o_ready.nth(g, turn))
                        nc.vector.reciprocal(rden[:, :], B[:, 6 + g % 2, :]).then_inc(*rden_ready.up())
                        dve.wait_ge(*rden_ready.nth(g + 1, turn))
                        nc.vector.tensor_tensor(U[:, g, :], U[:, g, :], rden[:, :], ALU.mult).then_inc(*o_ready.up())

                    divide(0)
                    divide(1)
                    for c in range(4):
                        dve.wait_ge(*up_done.nth(c + 1, turn))
                        dve.wait_ge(*gs_ready.nth(c + 1, turn))
                        nc.vector.scalar_tensor_tensor(out=hT[:, c, :], in0=B[:, 4 + c % 2, :], scalar=W[:, A_BU + c:A_BU + c + 1],
                                                                  in1=gs[:, c, :], op0=ALU.add, op1=ALU.mult).then_inc(*h_ready.up())
                    divide(2)
                    divide(3)
                    dve.wait_ge(*gate_ready.nth(1, turn))
                    nc.vector.tensor_tensor(cen[:, :], B[:, 1, :], sgate[:, :], ALU.mult).then_inc(*gated.up())
                    dve.wait_ge(*gated.nth(1, turn))
                    nc.vector.tensor_tensor(xin, xin, cen[:, :], ALU.add).then_inc(*out_done.up())
                    for q in mine:
                        q.full()
                    peer.full()


STATES, EXPERTS, HID = 64, 4, 512
B_IN = 0
B_DT = B_IN + 512
B_BP = B_DT + 2 * STATES
B_CP = B_BP + 2 * STATES
B_OUT = B_CP + 2 * STATES
B_GW = B_OUT + 2 * P
B_W1 = B_GW + EXPERTS
B_W2 = B_W1 + EXPERTS * HID
B_S2I = B_W2 + EXPERTS * 4 * P
B_B2 = B_S2I + 2 * P
B_GB = B_B2 + P
B_LT = B_GB + TILES * EXPERTS
B_SEL = B_LT + TILES * EXPERTS * EXPERTS
B_P = B_SEL + EXPERTS * P
BP = {"inb": 0, "conv": 4, "convb": 10, "dtb": 12, "bpb": 13, "cpb": 14, "s2ib": 15, "D": 17, "outb": 19, "n1": 20, "n2": 21, "b1": 22}
B_END = B_P + 22 + EXPERTS * 4


def level1(nc, x, xf, s1, w_dram, const, seqs):
    with ExitStack() as ctx:
        def sb(name, shape, dt=F32):
            return ctx.enter_context(nc.sbuf_tensor("b_" + name, shape, dt))

        def sig(name, per=0, primed=0):
            return Signal(ctx.enter_context(nc.semaphore("b_" + name)), per, primed)

        ident, ones_mean, ones_head, col = const.ident, const.mean, const.head, const.col
        T = [P, SEQ]
        W = sb("W", [P, B_END])
        cen, csq, lns, rstd, xn, nr, h1 = (sb(n, T) for n in ("cen", "csq", "lns", "rstd", "xn", "nr", "h1"))
        xc = sb("xc", [P, 2, 2 + SEQ])
        ca = sb("ca", [P, 2, SEQ])
        cb = sb("cb", [P, 2, SEQ])
        sgt = sb("sgt", [P, 2, SEQ])
        xm = sb("xm", [P, 2, SEQ])
        S = [STATES, SEQ]
        dt_, omd, db, st, y, yc, ysq, yln, yrs, yn = (sb(n, S) for n in ("dt", "omd", "db", "st", "y", "yc", "ysq", "yln", "yrs", "yn"))
        u1 = sb("u1", [P, 2, SEQ])
        u2 = sb("u2", [P, 2, SEQ])
        x2, x2sq, nr2, h2 = (sb(n, T) for n in ("x2", "x2sq", "nr2", "h2"))
        TE = TILES * EXPERTS
        lg, ls, ex, exs, rank, wt = (sb(n, [P, TE]) for n in ("lg", "ls", "ex", "exs", "rank", "wt"))
        mxl, zz, rz = (sb(n, [P, TILES]) for n in ("mxl", "zz", "rz"))
        gt, eq = (sb(n, [P, TE, EXPERTS]) for n in ("gt", "eq"))
        wT = sb("wT", [EXPERTS, SEQ])
        spare = sb("spare", [P, 1])
        gl = sb("gl", [P, 3, SEQ])
        wb = sb("wb", [P, EXPERTS, SEQ])
        hw = sb("hw", [P, 3, SEQ])
        B = ctx.enter_context(nc.psum_tensor("b_B", [P, 8, 512], F32))

        def par(name, k=0, rows=P):
            c = B_P + BP[name] + k
            return W[0:rows, c:c + 1]

        NK = EXPERTS * 4
        w_in = sig("w_in")
        zeroed = sig("zeroed")
        out_done = sig("out_done", 1, 1)
        sums = sig("sums", 6)
        sq_ready = sig("sq_ready", 4)
        lnd = sig("lnd", 4)
        inv = sig("inv", 4)
        cen_ready = sig("cen_ready", 2)
        xn_ready = sig("xn_ready", 1)
        xf_ready = sig("xf_ready", 1, 1)
        n_ready = sig("n_ready", 4)
        in_done = sig("in_done", 4)
        xc_ready = sig("xc_ready", 2)
        gates = sig("gates", 2)
        conv = sig("conv", 6)
        xm_ready = sig("xm_ready", 2)
        dbc = sig("dbc", 3)
        dt_ready = sig("dt_ready", 1)
        ssm = sig("ssm", 5)
        s2i = sig("s2i", 2)
        u_ready = sig("u_ready", 4)
        out_p = sig("out_p", 1)
        x2_ready = sig("x2_ready", 1)
        logits = sig("logits", 1)
        ls_ready = sig("ls_ready", 1)
        route = sig("route", 10)
        ex_ready = sig("ex_ready", 1)
        wt_done = sig("wt_done", 1)
        wT_ready = sig("wT_ready", 1)
        wb_done = sig("wb_done", EXPERTS)
        wb_ready = sig("wb_ready", EXPERTS)
        hid = sig("hid", NK)
        gelus = sig("gelus", NK)
        hw_ready = sig("hw_ready", NK)
        eo_used = sig("eo_used", NK)

        with nc.Block() as block:
            @block.sync
            def _(sp):
                sp.dma_start(W[:, :], w_dram).then_inc(w_in.sem, 16)

            @block.gpsimd
            def _(pool):
                nc.gpsimd.memset(xc[:, :, 0:2], 0.0).then_inc(*zeroed.up())
                nc.gpsimd.memset(spare[:, :], 0.0).then_inc(*xf_ready.prime())
                nc.gpsimd.memset(xf[:, :].rearrange("p (s t) -> p s t", s=seqs)[:, :, 0:1], 0.0).then_inc(*zeroed.up())
                with pool.Fori(0, seqs) as turn:
                    xf_ready.n = 0
                    pool.wait_ge(*xn_ready.nth(1, turn))
                    nc.gpsimd.tensor_copy(xf[:, bass.ds(turn * (SEQ + 1) + 1, SEQ)], xn[:, :]).then_inc(*xf_ready.up())
                    xf_ready.full()

            @block.scalar
            def _(act):
                nc.scalar.preload_act_table_set("natural_log_exp_and_others")
                act.wait_ge(w_in.sem, 16)
                with act.Fori(0, seqs) as turn:
                    mine = (sq_ready, lnd, inv, gates, xm_ready, dt_ready, ex_ready, gelus)
                    for q in mine:
                        q.n = 0

                    def inverse_root(out, ln_out, src, eps, n):
                        act.wait_ge(*sums.nth(n, turn))
                        nc.scalar.activation(ln_out, src, ACT.Ln, bias=eps).then_inc(*lnd.up())
                        act.wait_ge(*lnd.last(turn))
                        nc.scalar.activation(out, ln_out, ACT.Exp, scale=-0.5).then_inc(*inv.up())

                    act.wait_ge(*cen_ready.nth(1, turn))
                    nc.scalar.activation(csq[:, :], cen[:, :], ACT.Square).then_inc(*sq_ready.up())
                    inverse_root(rstd[:, :], lns[:, :], B[:, 1, :], col["eps5"], 2)
                    act.wait_ge(*xn_ready.nth(1, turn))
                    nc.scalar.activation(csq[:, :], xn[:, :], ACT.Square).then_inc(*sq_ready.up())
                    act.wait_ge(*inv.nth(1, turn))
                    inverse_root(nr[:, :], lns[:, :], B[:, 2, :], col["eps6"], 3)
                    for b in range(2):
                        act.wait_ge(*conv.nth(3 * b + 3, turn))
                        nc.scalar.activation(xm[:, b, :], ca[:, b, :], ACT.Silu, bias=par("convb", b)).then_inc(*xm_ready.up())
                    act.wait_ge(*dbc.nth(1, turn))
                    nc.scalar.activation(dt_[:, :], B[0:STATES, 0, :], ACT.Sigmoid, bias=par("dtb", 0, STATES)).then_inc(*dt_ready.up())
                    for b in range(2):
                        act.wait_ge(*in_done.nth(3 + b, turn))
                        nc.scalar.activation(sgt[:, b, :], B[:, 5 + b, :], ACT.Sigmoid, bias=par("inb", 2 + b)).then_inc(*gates.up())
                    nc.scalar.preload_act_table_set("natural_log_exp_and_others")
                    act.wait_ge(*cen_ready.nth(2, turn))
                    nc.scalar.activation(ysq[:, :], yc[:, :], ACT.Square).then_inc(*sq_ready.up())
                    inverse_root(yrs[:, :], yln[:, :], B[0:STATES, 4, :], col["eps5"][0:STATES, :], 5)
                    act.wait_ge(*x2_ready.nth(1, turn))
                    nc.scalar.activation(x2sq[:, :], x2[:, :], ACT.Square).then_inc(*sq_ready.up())
                    inverse_root(nr2[:, :], lns[:, :], B[:, 0, :], col["eps6"], 6)
                    act.wait_ge(*ls_ready.nth(1, turn))
                    nc.scalar.activation(ex[:, :], ls[:, :], ACT.Exp).then_inc(*ex_ready.up())
                    for k in range(NK):
                        act.wait_ge(*hid.nth(k + 1, turn))
                        if k >= 3:
                            act.wait_ge(*hw_ready.nth(k - 2, turn))
                        nc.scalar.activation(gl[:, k % 3, :], B[:, k % 3, :], ACT.Gelu, bias=par("b1", k)).then_inc(*gelus.up())
                    nc.scalar.preload_act_table_set("natural_log_exp_and_others")
                    for q in mine:
                        q.full()

            @block.tensor
            def _(pe):
                pe.wait_ge(w_in.sem, 16)
                with pe.Fori(0, seqs) as turn:
                    mine = (sums, in_done, dbc, s2i, out_p, logits, wt_done, wb_done, hid, eo_used)
                    for q in mine:
                        q.n = 0
                    mean_s = const.mean64
                    pe.wait_ge(*out_done.nth(0, turn))
                    nc.tensor.matmul(B[:, 0, :], ones_mean, x[:, bass.ds(turn * SEQ, SEQ)], start=True, stop=True).then_inc(*sums.up())
                    pe.wait_ge(*sq_ready.nth(1, turn))
                    nc.tensor.matmul(B[:, 1, :], ones_mean, csq[:, :], start=True, stop=True).then_inc(*sums.up())
                    pe.wait_ge(*sq_ready.nth(2, turn))
                    nc.tensor.matmul(B[:, 2, :], ones_mean, csq[:, :], start=True, stop=True).then_inc(*sums.up())
                    pe.wait_ge(*n_ready.nth(2, turn))
                    for b in range(4):
                        nc.tensor.matmul(B[:, 3 + b, :], W[:, B_IN + b * P:B_IN + (b + 1) * P], h1[:, :], start=True, stop=True).then_inc(*in_done.up())
                    pe.wait_ge(*xm_ready.nth(2, turn))
                    for i, c in enumerate((B_DT, B_BP, B_CP)):
                        for b in range(2):
                            mm = nc.tensor.matmul(B[0:STATES, i, :], W[:, c + b * STATES:c + (b + 1) * STATES], xm[:, b, :], start=b == 0, stop=b == 1)
                        mm.then_inc(*dbc.up())
                    pe.wait_ge(*ssm.nth(4, turn))
                    nc.tensor.matmul(B[:, 3, :], mean_s, y[:, :], start=True, stop=True).then_inc(*sums.up())
                    pe.wait_ge(*sq_ready.nth(3, turn))
                    nc.tensor.matmul(B[:, 4, :], mean_s, ysq[:, :], start=True, stop=True).then_inc(*sums.up())
                    pe.wait_ge(*ssm.nth(5, turn))
                    for b in range(2):
                        nc.tensor.matmul(B[:, 5 + b, :], W[0:STATES, B_S2I + b * P:B_S2I + (b + 1) * P], yn[:, :], start=True, stop=True).then_inc(*s2i.up())
                    pe.wait_ge(*u_ready.nth(4, turn))
                    for b in range(2):
                        mm = nc.tensor.matmul(B[:, 7, :], W[:, B_OUT + b * P:B_OUT + (b + 1) * P], u2[:, b, :], start=b == 0, stop=b == 1)
                    mm.then_inc(*out_p.up())
                    pe.wait_ge(*sq_ready.nth(4, turn))
                    nc.tensor.matmul(B[:, 0, :], ones_mean, x2sq[:, :], start=True, stop=True).then_inc(*sums.up())
                    pe.wait_ge(*n_ready.nth(4, turn))
                    for t in range(TILES):
                        mm = nc.tensor.matmul(B[:, 1, t * EXPERTS:(t + 1) * EXPERTS], h2[:, t * TILE:(t + 1) * TILE], W[:, B_GW:B_GW + EXPERTS],
                                              start=True, stop=True)
                    mm.then_inc(*logits.up())

                    def hidden(k):
                        nc.tensor.matmul(B[:, k % 3, :], W[:, B_W1 + k * P:B_W1 + (k + 1) * P], h2[:, :], start=True, stop=True).then_inc(*hid.up())

                    hidden(0)
                    pe.wait_ge(*route.nth(1, turn))
                    hidden(1)
                    pe.wait_ge(*route.nth(10, turn))
                    for t in range(TILES):
                        mm = nc.tensor.transpose(B[0:EXPERTS, 2, t * TILE:(t + 1) * TILE], wt[:, t * EXPERTS:(t + 1) * EXPERTS], ident)
                    mm.then_inc(*wt_done.up())
                    pe.wait_ge(*wT_ready.nth(1, turn))
                    nc.tensor.matmul(B[:, 7, :], W[0:EXPERTS, B_B2:B_B2 + P], wT[:, :], start=True, stop=False, skip_group_check=True)
                    for e in range(EXPERTS):
                        nc.tensor.matmul(B[:, 3 + e, :], W[0:EXPERTS, B_SEL + e * P:B_SEL + (e + 1) * P], wT[:, :], start=True, stop=True).then_inc(*wb_done.up())

                    def result(k):
                        pe.wait_ge(*hw_ready.nth(k + 1, turn))
                        nc.tensor.matmul(B[:, 7, :], W[:, B_W2 + k * P:B_W2 + (k + 1) * P], hw[:, k % 3, :],
                                                    start=False, stop=k == NK - 1, skip_group_check=True).then_inc(*eo_used.up())

                    for k in range(2, NK):
                        if k >= 3:
                            pe.wait_ge(*gelus.nth(k - 2, turn))
                        hidden(k)
                        result(k - 2)
                    result(NK - 2)
                    result(NK - 1)
                    for q in mine:
                        q.full()

            @block.vector
            def _(dve):
                nc.vector.memset(rz[:, :], 0.0).then_inc(*out_done.prime())
                dve.wait_ge(w_in.sem, 16)
                dve.wait_ge(*zeroed.nth(2))
                TT, STT, TSC = nc.vector.tensor_tensor, nc.vector.scalar_tensor_tensor, nc.vector.tensor_scalar
                with dve.Fori(0, seqs) as turn:
                    mine = (cen_ready, xn_ready, n_ready, xc_ready, conv, ssm, u_ready, x2_ready, ls_ready, route, wT_ready, wb_ready,
                            hw_ready, out_done)
                    for q in mine:
                        q.n = 0
                    dve.wait_ge(*sums.nth(1, turn))
                    TT(cen[:, :], x[:, bass.ds(turn * SEQ, SEQ)], B[:, 0, :], ALU.subtract).then_inc(*cen_ready.up())
                    dve.wait_ge(*inv.nth(1, turn))
                    dve.wait_ge(*xf_ready.nth(0, turn))
                    TT(xn[:, :], cen[:, :], rstd[:, :], ALU.mult).then_inc(*xn_ready.up())
                    dve.wait_ge(*xn_ready.nth(1, turn))
                    TSC(h1[:, :], xn[:, :], par("n1"), None, ALU.mult).then_inc(*n_ready.up())
                    dve.wait_ge(*n_ready.nth(1, turn))
                    dve.wait_ge(*inv.nth(2, turn))
                    TT(h1[:, :], h1[:, :], nr[:, :], ALU.mult).then_inc(*n_ready.up())
                    for b in range(2):
                        dve.wait_ge(*in_done.nth(b + 1, turn))
                        TSC(xc[:, b, 2:], B[:, 3 + b, :], par("inb", b), None, ALU.add).then_inc(*xc_ready.up())
                    for b in range(2):
                        dve.wait_ge(*xc_ready.nth(b + 1, turn))
                        TSC(ca[:, b, :], xc[:, b, 2:], par("conv", 3 * b + 2), None, ALU.mult).then_inc(*conv.up())
                        dve.wait_ge(*conv.last(turn))
                        STT(out=cb[:, b, :], in0=xc[:, b, 1:1 + SEQ], scalar=par("conv", 3 * b + 1), in1=ca[:, b, :], op0=ALU.mult, op1=ALU.add).then_inc(*conv.up())
                        dve.wait_ge(*conv.last(turn))
                        STT(out=ca[:, b, :], in0=xc[:, b, 0:SEQ], scalar=par("conv", 3 * b), in1=cb[:, b, :], op0=ALU.mult, op1=ALU.add).then_inc(*conv.up())
                    dve.wait_ge(*dt_ready.nth(1, turn))
                    TSC(omd[:, :], dt_[:, :], -1.0, 1.0, ALU.mult, ALU.add).then_inc(*ssm.up())
                    dve.wait_ge(*dbc.nth(3, turn))
                    STT(out=db[:, :], in0=B[0:STATES, 1, :], scalar=par("bpb", 0, STATES), in1=dt_[:, :], op0=ALU.add, op1=ALU.mult).then_inc(*ssm.up())
                    dve.wait_ge(*ssm.last(turn))
                    nc.vector.tensor_tensor_scan(st[:, :], omd[:, :], db[:, :], 0.0, ALU.mult, ALU.add).then_inc(*ssm.up())
                    dve.wait_ge(*ssm.last(turn))
                    STT(out=y[:, :], in0=B[0:STATES, 2, :], scalar=par("cpb", 0, STATES), in1=st[:, :], op0=ALU.add, op1=ALU.mult).then_inc(*ssm.up())
                    dve.wait_ge(*ssm.last(turn))
                    dve.wait_ge(*sums.nth(4, turn))
                    TT(yc[:, :], y[:, :], B[0:STATES, 3, :], ALU.subtract).then_inc(*cen_ready.up())
                    dve.wait_ge(*cen_ready.nth(2, turn))
                    dve.wait_ge(*inv.nth(3, turn))
                    TT(yn[:, :], yc[:, :], yrs[:, :], ALU.mult).then_inc(*ssm.up())
                    for b in range(2):
                        dve.wait_ge(*s2i.nth(b + 1, turn))
                        dve.wait_ge(*gates.nth(b + 1, turn))
                        STT(out=u1[:, b, :], in0=xm[:, b, :], scalar=par("D", b), in1=B[:, 5 + b, :], op0=ALU.mult, op1=ALU.add).then_inc(*u_ready.up())
                        dve.wait_ge(*u_ready.last(turn))
                        STT(out=u2[:, b, :], in0=u1[:, b, :], scalar=par("s2ib", b), in1=sgt[:, b, :], op0=ALU.add, op1=ALU.mult).then_inc(*u_ready.up())
                    dve.wait_ge(*out_p.nth(1, turn))
                    STT(out=x2[:, :], in0=B[:, 7, :], scalar=par("outb"), in1=xn[:, :], op0=ALU.add, op1=ALU.add).then_inc(*x2_ready.up())
                    dve.wait_ge(*x2_ready.nth(1, turn))
                    TSC(h2[:, :], x2[:, :], par("n2"), None, ALU.mult).then_inc(*n_ready.up())
                    dve.wait_ge(*n_ready.nth(3, turn))
                    dve.wait_ge(*inv.nth(4, turn))
                    TT(h2[:, :], h2[:, :], nr2[:, :], ALU.mult).then_inc(*n_ready.up())
                    dve.wait_ge(*logits.nth(1, turn))
                    TT(lg[:, :], B[:, 1, 0:TE], W[:, B_GB:B_GB + TE], ALU.add).then_inc(*route.up())
                    dve.wait_ge(*route.last(turn))
                    lt = lg[:, :].rearrange("p (t e) -> p t e", t=TILES)
                    for t in range(TILES):
                        other = lg[:, t * EXPERTS:(t + 1) * EXPERTS].unsqueeze(1).broadcast_to([P, EXPERTS, EXPERTS])
                        own = lg[:, t * EXPERTS:(t + 1) * EXPERTS].unsqueeze(2).broadcast_to([P, EXPERTS, EXPERTS])
                        rows = slice(t * EXPERTS, (t + 1) * EXPERTS)
                        nc.vector.tensor_tensor(gt[:, rows, :], other, own, ALU.is_gt)
                        mm = nc.vector.tensor_tensor(eq[:, rows, :], other, own, ALU.is_equal)
                    mm.then_inc(*route.up())
                    nc.vector.tensor_reduce(mxl[:, :], lt, AX.X, ALU.max).then_inc(*route.up())
                    dve.wait_ge(*route.last(turn))
                    TT(ls[:, :].rearrange("p (t e) -> p t e", t=TILES), lt, mxl[:, :].unsqueeze(2).broadcast_to([P, TILES, EXPERTS]), ALU.subtract).then_inc(*ls_ready.up())
                    flat = lambda a: a.rearrange("p a b -> p (a b)")
                    TT(flat(eq[:, :, :]), flat(eq[:, :, :]), W[:, B_LT:B_LT + TE * EXPERTS], ALU.mult).then_inc(*route.up())
                    dve.wait_ge(*route.last(turn))
                    TT(flat(gt[:, :, :]), flat(gt[:, :, :]), flat(eq[:, :, :]), ALU.add).then_inc(*route.up())
                    dve.wait_ge(*route.last(turn))
                    nc.vector.tensor_reduce(rank[:, :], gt[:, :, :], AX.X, ALU.add).then_inc(*route.up())
                    dve.wait_ge(*route.last(turn))
                    dve.wait_ge(*ex_ready.nth(1, turn))
                    STT(out=exs[:, :], in0=rank[:, :], scalar=2.0, in1=ex[:, :], op0=ALU.is_lt, op1=ALU.mult).then_inc(*route.up())
                    dve.wait_ge(*route.last(turn))
                    nc.vector.tensor_reduce(zz[:, :], exs[:, :].rearrange("p (t e) -> p t e", t=TILES), AX.X, ALU.add).then_inc(*route.up())
                    dve.wait_ge(*route.last(turn))
                    nc.vector.reciprocal(rz[:, :], zz[:, :]).then_inc(*route.up())
                    dve.wait_ge(*route.last(turn))
                    TT(wt[:, :].rearrange("p (t e) -> p t e", t=TILES), exs[:, :].rearrange("p (t e) -> p t e", t=TILES),
                                rz[:, :].unsqueeze(2).broadcast_to([P, TILES, EXPERTS]), ALU.mult).then_inc(*route.up())
                    dve.wait_ge(*wt_done.nth(1, turn))
                    nc.vector.tensor_copy(wT[:, :], B[0:EXPERTS, 2, :]).then_inc(*wT_ready.up())
                    for e in range(EXPERTS):
                        dve.wait_ge(*wb_done.nth(e + 1, turn))
                        nc.vector.tensor_copy(wb[:, e, :], B[:, 3 + e, :]).then_inc(*wb_ready.up())
                    dve.wait_ge(*wb_ready.nth(EXPERTS, turn))
                    for k in range(NK):
                        dve.wait_ge(*gelus.nth(k + 1, turn))
                        if k >= 3:
                            dve.wait_ge(*eo_used.nth(k - 2, turn))
                        TT(hw[:, k % 3, :], gl[:, k % 3, :], wb[:, k // 4, :], ALU.mult).then_inc(*hw_ready.up())
                    dve.wait_ge(*eo_used.nth(NK, turn))
                    TT(s1[:, bass.ds(turn * SEQ, SEQ)], x2[:, :], B[:, 7, :], ALU.add).then_inc(*out_done.up())
                    for q in mine:
                        q.full()


C_ID, C_MEAN, C_HEAD, C_M64, C_TRI, C_MASK = (i * P for i in range(6))
C_COL = C_MASK + 2 * BAND
COLS = {"tiny": 2.0 ** -64, "shift": LN_SHIFT / 2 * float(np.log(2.0)), "eps5": 1e-5, "eps6": 1e-6}
C_END = C_COL + len(COLS)


class Constants:
    def __init__(self, c32, c16):
        self.ident = c32[:, C_ID:C_ID + P]
        self.mean = c32[:, C_MEAN:C_MEAN + P]
        self.head = c32[:, C_HEAD:C_HEAD + P]
        self.mean64 = c32[0:STATES, C_M64:C_M64 + P]
        self.tri = c32[:, C_TRI:C_TRI + P]
        self.col = {n: c32[:, C_COL + i:C_COL + i + 1] for i, n in enumerate(COLS)}
        self.identb = c16[:, 0:P]
        self.mask = c16[:, P:P + 2 * BAND]


def keep(nc, pairs):
    with ExitStack() as ctx:
        stored = ctx.enter_context(nc.semaphore("kept"))
        with nc.Block() as block:
            @block.sync
            def _(sp):
                for dram, sbuf in pairs:
                    sp.dma_start(dram, sbuf).then_inc(stored, 16)
                sp.wait_ge(stored, 16 * len(pairs))


def result(nc, x_kept, s1_kept, xf, out_dram, seqs):
    with ExitStack() as ctx:
        def sb(name):
            return ctx.enter_context(nc.sbuf_tensor("d_" + name, [P, seqs * SEQ], F32))

        def sig(name):
            return Signal(ctx.enter_context(nc.semaphore("d_" + name)))

        x, s1, g = sb("x"), sb("s1"), sb("g")
        loads = [ctx.enter_context(nc.semaphore(f"d_load{i}")) for i in range(seqs)]
        gates, prod, total, stored = sig("silu"), sig("product"), sig("total"), sig("stored")
        part = [slice(i * SEQ, (i + 1) * SEQ) for i in range(seqs)]
        with nc.Block() as block:
            @block.scalar
            def _(act):
                for i in range(seqs):
                    f = xf[:, i * (SEQ + 1) + 1:(i + 1) * (SEQ + 1)]
                    nc.scalar.activation(g[:, part[i]], f, ACT.Silu).then_inc(*gates.up())

            @block.vector
            def _(dve):
                for i in range(seqs):
                    dve.wait_ge(*gates.nth(i + 1))
                    dve.wait_ge(loads[i], 32)
                    nc.vector.tensor_tensor(g[:, part[i]], g[:, part[i]], s1[:, part[i]], ALU.mult).then_inc(*prod.up())
                    dve.wait_ge(*prod.nth(i + 1))
                    nc.vector.tensor_tensor(g[:, part[i]], g[:, part[i]], x[:, part[i]], ALU.add).then_inc(*total.up())

            @block.sync
            def _(sp):
                for i in range(seqs):
                    sp.dma_start(s1[:, part[i]], s1_kept[:, part[i]]).then_inc(loads[i], 16)
                    sp.dma_start(x[:, part[i]], x_kept[:, part[i]]).then_inc(loads[i], 16)
                for i in range(seqs):
                    sp.wait_ge(*total.nth(i + 1))
                    sp.dma_start(out_dram[:, part[i]], g[:, part[i]]).then_inc(stored.sem, 16)
                sp.wait_ge(stored.sem, 16 * seqs)


def program(nc, x_dram, wa, wb, wh, wt, tab, c32_dram, out_dram):
    with ExitStack() as ctx:
        def sb(name, shape, dt=F32, at=ctx):
            return at.enter_context(nc.sbuf_tensor(name, shape, dt))

        xf = sb("xf", [P, SEQS * (SEQ + 1)])
        c32 = sb("c32", [P, C_END])
        c16 = sb("c16", [P, P + 2 * BAND], BF16)
        x_kept = nc.dram_tensor("x_kept", (P, SEQS * SEQ), F32).ap()
        s1_kept = nc.dram_tensor("s1_kept", (P, SEQS * SEQ), F32).ap()
        loaded = ctx.enter_context(nc.semaphore("loaded"))
        const = Constants(c32, c16)
        with ExitStack() as early:
            x = sb("x", [P, SEQS * SEQ], at=early)
            with nc.Block() as block:
                @block.sync
                def _(sp):
                    sp.dma_start(x[:, :], x_dram).then_inc(loaded, 16)
                    sp.dma_start(c32[:, :], c32_dram).then_inc(loaded, 16)
                    sp.wait_ge(loaded, 32)

                @block.vector
                def _(dve):
                    dve.wait_ge(loaded, 32)
                    nc.vector.tensor_copy(c16[:, 0:P], const.ident)
                    nc.vector.tensor_copy(c16[:, P:], c32[:, C_MASK:C_MASK + 2 * BAND])
            level0(nc, x, wa, const, SEQS)
            s1 = sb("s1", [P, SEQS * SEQ], at=early)
            level1(nc, x, xf, s1, wb, const, SEQS)
            keep(nc, [(x_kept, x[:, :]), (s1_kept, s1[:, :])])
        network(nc, xf, wh, wt, tab, const, DEPTH, SEQS)
        result(nc, x_kept, s1_kept, xf, out_dram, SEQS)



def rows(a):
    return a.reshape(-1, P, a.shape[1]).transpose(1, 0, 2).reshape(P, -1)


def pack_level0(d):
    W = np.zeros((P, A_END), np.float32)
    for c, n in ((A_Q, "Wq"), (A_K, "Wk")):
        W[:, c:c + HEADS * 64] = np.tile(d["L0_attn_" + n].reshape(P, HEADS, 1, 16), (1, 1, 4, 1)).reshape(P, HEADS * 64)
    f = {n: d["L0_ffn_" + n] for n in ("Wg", "bg", "Wu", "bu", "Wd", "bd", "Wq", "keys", "down_embed", "up_embed")}
    W[:, A_V:A_V + P] = d["L0_attn_Wv"]
    wo = np.zeros((4, 4, 32, P), np.float32)
    wo[:, :, 0:8] = d["L0_attn_Wo"].reshape(4, 4, 8, P)
    W[:, A_O:A_O + 4 * P] = rows(wo.reshape(4 * P, P))
    W[:, A_G:A_G + 512] = f["Wg"]
    W[:, A_U:A_U + 512] = f["Wu"]
    W[:, A_D:A_D + 512] = rows(f["Wd"])
    W[:, A_DOWN:A_DOWN + 512] = f["down_embed"].T
    W[:, A_UP:A_UP + 512] = rows(f["up_embed"])
    W[:, A_WQT:A_WQT + 512] = f["Wq"].reshape(P, 2, 4, 64).transpose(1, 3, 2, 0).reshape(P, 512)
    W[:, A_KEYS:A_KEYS + 256] = f["keys"].transpose(2, 3, 0, 1).reshape(P, 256)
    W[:, A_BG:A_BG + 4] = f["bg"].reshape(4, P).T
    W[:, A_BU:A_BU + 4] = f["bu"].reshape(4, P).T
    W[:, A_BD] = f["bd"]
    r = np.arange(P)
    W[:, A_SEL:A_SEL + P] = r[:, None] == r[None, :] // 32 * 32 + 8
    W[:, A_EPS] = np.where(r % 32 == 8, np.float32(1e-5), 0)
    W[:, A_LOWQ] = -(r // 16 % 2)
    W[:, A_LOWK] = -(r // 32 % 2)
    return W


def pack_level1(d):
    W = np.zeros((P, B_END), np.float32)
    a = {n[8:]: v for n, v in d.items() if n.startswith("L1_attn_")}
    W[:, B_IN:B_IN + 512] = a["in_proj_w"]
    for c, n in ((B_DT, "dt_w"), (B_BP, "bp_w"), (B_CP, "cp_w")):
        W[:, c:c + 2 * STATES] = rows(a[n])
    W[:, B_OUT:B_OUT + 2 * P] = rows(a["out_w"])
    W[:, B_GW:B_GW + EXPERTS] = a["gate_w"]
    W[:, B_W1:B_W1 + EXPERTS * HID] = a["e_w1"].transpose(1, 0, 2).reshape(P, -1)
    W[:, B_W2:B_W2 + EXPERTS * HID] = a["e_w2"].reshape(EXPERTS, 4, P, P).transpose(2, 0, 1, 3).reshape(P, -1)
    W[0:STATES, B_S2I:B_S2I + 2 * P] = a["s2i_w"]
    W[0:EXPERTS, B_B2:B_B2 + P] = a["e_b2"]
    W[:, B_GB:B_GB + TILES * EXPERTS] = np.tile(a["gate_b"], (P, TILES))
    before = np.tril(np.ones((EXPERTS, EXPERTS)), -1).reshape(1, -1)
    W[:, B_LT:B_LT + TILES * EXPERTS * EXPERTS] = np.tile(before, (P, TILES))
    for e in range(EXPERTS):
        W[e, B_SEL + e * P:B_SEL + (e + 1) * P] = 1

    def put(name, block, height=P):
        c = B_P + BP[name]
        W[0:height, c:c + block.shape[1]] = block

    put("inb", a["in_proj_b"].reshape(4, P).T)
    put("conv", a["conv_w"].reshape(2, P, 3).transpose(1, 0, 2).reshape(P, 6))
    for name, n in (("convb", "conv_b"), ("s2ib", "s2i_b"), ("D", "D_param"), ("outb", "out_b"), ("n1", "norm1_w"), ("n2", "norm2_w")):
        put(name, a[n].reshape(-1, P).T)
    for name, n in (("dtb", "dt_b"), ("bpb", "bp_b"), ("cpb", "cp_b")):
        put(name, a[n].reshape(STATES, 1), STATES)
    put("b1", a["e_b1"].reshape(EXPERTS * 4, P).T)
    return W


def swapped(a):
    h = a.reshape(*a.shape[:-1], -1, 2, HALF)[..., ::-1, :]
    return h.reshape(a.shape)


def pack_network(d):
    a = {n[7:]: v for n, v in d.items() if n.startswith("L1_ffn_")}
    H = np.zeros((DEPTH, P, H_END), np.float32)
    T = np.zeros((DEPTH, P, T_END), np.float32)
    qkv, n = a["Wqkv"], HEADS * DH
    qk = qkv[:, :, 0:2 * n]
    both = np.stack([x.reshape(DEPTH, P, 2 * PAIRS, P) for x in (qk, swapped(qk))], 3)
    both = both[:, :, [kind * PAIRS + pair for kind, pair in UNIT]]
    H[:, :, H_QK:H_QK + 4 * n] = both.reshape(DEPTH, P, 4 * n)
    H[:, :, H_V:H_V + n] = qkv[:, :, 2 * n:]
    for i, s in enumerate((a["q_scale"], swapped(a["q_scale"]), a["k_scale"], swapped(a["k_scale"]))):
        H[:, :, H_P + i] = np.tile(s, (1, 2))
    T[:, :, T_O:T_O + n] = a["Wo"].reshape(DEPTH, n // P, P, P).transpose(0, 2, 1, 3).reshape(DEPTH, P, n)
    T[:, :, T_1:T_1 + 2 * FF] = a["W1"]
    for c, (f, m) in enumerate(FCH):
        T[:, 0:m, T_2 + c * P:T_2 + (c + 1) * P] = a["W2"][:, f:f + m]
        T[:, 0:m, T_P + PAR["b1"] + c] = a["b1"][:, f:f + m]
        T[:, 0:m, T_P + PAR["b1"] + 3 + c] = a["b1"][:, FF + f:FF + f + m]
    T[:, :, T_P + PAR["g"]] = a["ln_g"]
    T[:, :, T_P + PAR["b"]] = a["ln_b"]
    T[:, :, T_P + PAR["b2"]] = a["b2"]
    return H, T


def rotary_tables():
    f = np.float32
    half = np.arange(0, DH, 2, dtype=f)
    inv_freq = f(1.0) / f(10000.0) ** (half / f(DH))
    t = np.arange(SEQ, dtype=f)
    angle = t[:, None] * inv_freq[None, :]
    base = (half + f(0.4 * DH)) / f(1.4 * DH)
    scale = base[None, :] ** ((t - f(SEQ // 2)) / f(LOOK // 2))[:, None]
    c, s = (np.concatenate(x, 1) for x in ([np.cos(angle)] * 2, [-np.sin(angle), np.sin(angle)]))
    scale = np.concatenate([scale, scale], 1)
    tables = np.stack([c * scale, s * scale, c / scale, s / scale]).astype(f)
    return np.tile(tables.transpose(2, 0, 1), (2, 1, 1))


def constants():
    c = np.zeros((P, C_END), np.float32)
    c[:, C_ID:C_ID + P] = np.eye(P)
    c[:, C_MEAN:C_MEAN + P] = 1.0 / P
    c[:, C_HEAD:C_HEAD + P] = np.kron(np.eye(2), np.ones((DH, DH)))
    c[:, C_M64:C_M64 + P] = 1.0 / STATES
    c[:, C_TRI:C_TRI + P] = np.triu(np.ones((P, P)))
    i, k = np.arange(P)[:, None], np.arange(BAND)[None, :]
    c[:, C_MASK:C_MASK + 2 * BAND] = np.tile(np.where((k >= i) & (k <= i + LOOK), 0.0, -BIG), (1, 2))
    for i, v in enumerate(COLS.values()):
        c[:, C_COL + i] = v
    return c


def kernel(**inputs):
    import concourse.bacc as bacc
    from concourse.bass_utils import run_bass_kernel_spmd

    d = {n: np.asarray(v) for n, v in inputs.items()}
    x = d["L0_attn_hidden_states"]
    w_heads, w_tails = pack_network(d)
    arrays = {
        "x": x.transpose(2, 0, 1).reshape(P, SEQS * SEQ),
        "w_level0": pack_level0(d),
        "w_level1": pack_level1(d),
        "w_heads": w_heads,
        "w_tails": w_tails,
        "tables": rotary_tables(),
        "consts": constants(),
    }
    nc = bacc.Bacc("TRN2", target_bir_lowering=False, num_devices=1)
    given, args = {}, []
    for name, a in arrays.items():
        a = np.ascontiguousarray(a)
        given[f"in_{name}"] = a
        args.append(nc.dram_tensor(f"in_{name}", a.shape, mybir.dt.from_np(a.dtype), kind="ExternalInput").ap())
    out = nc.dram_tensor("out", (P, SEQS * SEQ), F32, kind="ExternalOutput").ap()
    program(nc, *args, out)
    r = run_bass_kernel_spmd(nc, [given], core_ids=[0])
    y = r.results[0]["out"]
    return np.ascontiguousarray(y.reshape(P, SEQS, SEQ).transpose(1, 2, 0)).reshape(x.shape)
```
